# Optimizing a Trainium2 kernel written in Bass

```python
import numpy as np
import jax
import jax.numpy as jnp

def _softmax(x, axis=-1):
    return jax.nn.softmax(x, axis=axis)

def _gelu(x):
    return jax.nn.gelu(x, approximate=True)

def _silu(x):
    return jax.nn.silu(x)

def _sigmoid(x):
    return jax.nn.sigmoid(x)

def _layernorm(x, axis=-1, eps=1e-05):
    m = jnp.mean(x, axis=axis, keepdims=True)
    v = jnp.var(x, axis=axis, keepdims=True)
    return (x - m) / jnp.sqrt(v + eps)

def _scatter_add(tgt, idx, src, axis=0):
    return tgt.at[idx].add(src)

def _segment_sum(src, seg, n):
    return jax.ops.segment_sum(src, seg, n)
kernel_name = 'mk_lm_tower_d1_tok_ids768_r4_a3f2ce'

def setup_inputs(seed: int=0):
    np.random.seed(seed)
    _w = jnp.asarray

    def _rec_inputs():
        import jax
        import jax.numpy as jnp
        _rk = jax.random.key(seed)
        x = jax.random.randint(jax.random.fold_in(_rk, 1), (8, 256), 0, 31993, jnp.int32)
        return x
    x = _rec_inputs()

    def _L0_tok_setup():
        import jax, jax.numpy as jnp
        import numpy as np
        EPS = 1e-05

        def pos_encoding(max_steps, d):
            p, i = np.meshgrid(np.arange(max_steps), np.arange(d // 2))
            pe = np.zeros((max_steps, d), dtype=np.float32)
            pe[:, ::2] = np.sin(p / 2500 ** (2 * i / d)).T
            pe[:, 1::2] = np.cos(p / 2500 ** (2 * i / d)).T
            return jnp.asarray(pe)

        def batchnorm(x, gamma, beta):
            mean = jnp.mean(x, axis=(0, 1))
            var = jnp.var(x, axis=(0, 1))
            return (x - mean) * jax.lax.rsqrt(var + EPS) * gamma + beta
        key = jax.random.key(seed)
        ks = jax.random.split(key, 12)
        B, S, D, V = (8, 256, 192, 8000)
        Dc = D // 3
        s = 0.02
        return {'x': jax.random.randint(ks[0], (B, S), 0, V, dtype=jnp.int32), 'emb': jax.random.normal(ks[1], (V, D), dtype=jnp.float32) * s, 'Wq': jax.random.normal(ks[2], (Dc, D), dtype=jnp.float32) * s, 'bq': jnp.zeros((D,), jnp.float32), 'Wk': jax.random.normal(ks[3], (Dc, D), dtype=jnp.float32) * s, 'bk': jnp.zeros((D,), jnp.float32), 'Wv': jax.random.normal(ks[4], (Dc, D), dtype=jnp.float32) * s, 'bv': jnp.zeros((D,), jnp.float32), 'Wf': jax.random.normal(ks[5], (D, D), dtype=jnp.float32) * s, 'bf': jnp.zeros((D,), jnp.float32), 'g1': jnp.ones((D,), jnp.float32), 'b1': jnp.zeros((D,), jnp.float32), 'g2': jnp.ones((D,), jnp.float32), 'b2': jnp.zeros((D,), jnp.float32)}
    _L0_tok_all = _L0_tok_setup()
    _L0_tok_in = {k: v for k, v in _L0_tok_all.items() if k in ('emb', 'Wq', 'bq', 'Wk', 'bk', 'Wv', 'bv', 'Wf', 'bf', 'g1', 'b1', 'g2', 'b2')}
    del _L0_tok_all

    def _L0_attn_setup():
        import jax, jax.numpy as jnp
        import numpy as np
        DIM = 192
        HEADS = 12
        DH = DIM // HEADS
        M = 64
        EPS = 0.0001

        def softmax_kernel(data, proj, is_query):
            data_normalizer = data.shape[-1] ** (-0.25)
            ratio = proj.shape[0] ** (-0.5)
            data_dash = jnp.einsum('bhsd,md->bhsm', data_normalizer * data, proj)
            diag = 0.5 * data_normalizer ** 2 * jnp.sum(data * data, axis=-1, keepdims=True)
            if is_query:
                stab = jnp.max(data_dash, axis=-1, keepdims=True)
            else:
                stab = jnp.max(data_dash, axis=(-2, -1), keepdims=True)
            stab = jax.lax.stop_gradient(stab)
            return ratio * (jnp.exp(data_dash - diag - stab) + EPS)
        key = jax.random.key(seed)
        kx, kq, kk, kv, ko, kp = jax.random.split(key, 6)
        B, S = (8, 1024)
        w_scale = DIM ** (-0.5)
        return {'x': jax.random.normal(kx, (B, S, DIM), jnp.float32), 'Wq': jax.random.normal(kq, (DIM, DIM), jnp.float32) * w_scale, 'Wk': jax.random.normal(kk, (DIM, DIM), jnp.float32) * w_scale, 'Wv': jax.random.normal(kv, (DIM, DIM), jnp.float32) * w_scale, 'Wo': jax.random.normal(ko, (DIM, DIM), jnp.float32) * w_scale, 'proj': jax.random.normal(kp, (M, DH), jnp.float32)}
    _L0_attn_all = _L0_attn_setup()
    _L0_attn_in = {k: v for k, v in _L0_attn_all.items() if k in ('Wq', 'Wk', 'Wv', 'Wo', 'proj')}
    del _L0_attn_all

    def _L0_ffn_setup():
        import jax, jax.numpy as jnp
        import numpy as np
        DIM = 192
        HEADS = 12
        EXPERTS = 8
        HID = 768
        TOP_K = 2
        LN_EPS = 1e-05

        def _layer_norm(x, g, b):
            mu = x.mean(-1, keepdims=True)
            var = ((x - mu) ** 2).mean(-1, keepdims=True)
            return (x - mu) * jax.lax.rsqrt(var + LN_EPS) * g + b

        def _attention(x, qkv_w, qkv_b, proj_w, proj_b):
            B, N, C = x.shape
            hd = C // HEADS
            qkv = (x @ qkv_w + qkv_b).reshape(B, N, 3, HEADS, hd).transpose(2, 0, 3, 1, 4)
            q, k, v = (qkv[0], qkv[1], qkv[2])
            attn = jax.nn.softmax(jnp.einsum('bhnd,bhmd->bhnm', q, k) * hd ** (-0.5), axis=-1)
            o = jnp.einsum('bhnm,bhmd->bhnd', attn, v).transpose(0, 2, 1, 3).reshape(B, N, C)
            return o @ proj_w + proj_b

        def _moe_mlp(xn, gate_w, w1, b1, w2, b2):
            T = xn.shape[0]
            logits = xn @ gate_w
            top_logits, top_idx = jax.lax.top_k(logits, TOP_K)
            top_gates = jax.nn.softmax(top_logits, axis=-1)
            gates = jnp.zeros((T, EXPERTS), xn.dtype).at[jnp.arange(T)[:, None], top_idx].set(top_gates)
            h = jax.nn.gelu(jnp.einsum('td,edh->teh', xn, w1) + b1, approximate=False)
            y = jnp.einsum('teh,ehd->ted', h, w2) + b2
            return jnp.einsum('ted,te->td', y, gates)
        key = jax.random.key(seed)
        ks = jax.random.split(key, 16)
        s = 0.02
        return {'x': jax.random.normal(ks[0], (8, 196, DIM), jnp.float32), 'ln1_g': jnp.ones((DIM,), jnp.float32), 'ln1_b': jnp.zeros((DIM,), jnp.float32), 'qkv_w': jax.random.normal(ks[1], (DIM, 3 * DIM), jnp.float32) * s, 'qkv_b': jnp.zeros((3 * DIM,), jnp.float32), 'proj_w': jax.random.normal(ks[2], (DIM, DIM), jnp.float32) * s, 'proj_b': jnp.zeros((DIM,), jnp.float32), 'ln2_g': jnp.ones((DIM,), jnp.float32), 'ln2_b': jnp.zeros((DIM,), jnp.float32), 'gate_w': jax.random.normal(ks[3], (DIM, EXPERTS), jnp.float32) * s, 'w1': jax.random.normal(ks[4], (EXPERTS, DIM, HID), jnp.float32) * s, 'b1': jnp.zeros((EXPERTS, HID), jnp.float32), 'w2': jax.random.normal(ks[5], (EXPERTS, HID, DIM), jnp.float32) * s, 'b2': jnp.zeros((EXPERTS, DIM), jnp.float32)}
    _L0_ffn_all = _L0_ffn_setup()
    _L0_ffn_in = {k: v for k, v in _L0_ffn_all.items() if k in ('ln1_g', 'ln1_b', 'qkv_w', 'qkv_b', 'proj_w', 'proj_b', 'ln2_g', 'ln2_b', 'gate_w', 'w1', 'b1', 'w2', 'b2')}
    del _L0_ffn_all
    return {'x': x, 'L0_tok_emb': _L0_tok_in['emb'], 'L0_tok_Wq': _L0_tok_in['Wq'], 'L0_tok_bq': _L0_tok_in['bq'], 'L0_tok_Wk': _L0_tok_in['Wk'], 'L0_tok_bk': _L0_tok_in['bk'], 'L0_tok_Wv': _L0_tok_in['Wv'], 'L0_tok_bv': _L0_tok_in['bv'], 'L0_tok_Wf': _L0_tok_in['Wf'], 'L0_tok_bf': _L0_tok_in['bf'], 'L0_tok_g1': _L0_tok_in['g1'], 'L0_tok_b1': _L0_tok_in['b1'], 'L0_tok_g2': _L0_tok_in['g2'], 'L0_tok_b2': _L0_tok_in['b2'], 'L0_attn_Wq': _L0_attn_in['Wq'], 'L0_attn_Wk': _L0_attn_in['Wk'], 'L0_attn_Wv': _L0_attn_in['Wv'], 'L0_attn_Wo': _L0_attn_in['Wo'], 'L0_attn_proj': _L0_attn_in['proj'], 'L0_ffn_ln1_g': _L0_ffn_in['ln1_g'], 'L0_ffn_ln1_b': _L0_ffn_in['ln1_b'], 'L0_ffn_qkv_w': _L0_ffn_in['qkv_w'], 'L0_ffn_qkv_b': _L0_ffn_in['qkv_b'], 'L0_ffn_proj_w': _L0_ffn_in['proj_w'], 'L0_ffn_proj_b': _L0_ffn_in['proj_b'], 'L0_ffn_ln2_g': _L0_ffn_in['ln2_g'], 'L0_ffn_ln2_b': _L0_ffn_in['ln2_b'], 'L0_ffn_gate_w': _L0_ffn_in['gate_w'], 'L0_ffn_w1': _L0_ffn_in['w1'], 'L0_ffn_b1': _L0_ffn_in['b1'], 'L0_ffn_w2': _L0_ffn_in['w2'], 'L0_ffn_b2': _L0_ffn_in['b2']}

def reference(x, L0_tok_emb, L0_tok_Wq, L0_tok_bq, L0_tok_Wk, L0_tok_bk, L0_tok_Wv, L0_tok_bv, L0_tok_Wf, L0_tok_bf, L0_tok_g1, L0_tok_b1, L0_tok_g2, L0_tok_b2, L0_attn_Wq, L0_attn_Wk, L0_attn_Wv, L0_attn_Wo, L0_attn_proj, L0_ffn_ln1_g, L0_ffn_ln1_b, L0_ffn_qkv_w, L0_ffn_qkv_b, L0_ffn_proj_w, L0_ffn_proj_b, L0_ffn_ln2_g, L0_ffn_ln2_b, L0_ffn_gate_w, L0_ffn_w1, L0_ffn_b1, L0_ffn_w2, L0_ffn_b2):
    import jax
    import jax.numpy as jnp

    def _L0_tok_ref(x, emb, Wq, bq, Wk, bk, Wv, bv, Wf, bf, g1, b1, g2, b2):
        import jax, jax.numpy as jnp
        import numpy as np
        EPS = 1e-05

        def pos_encoding(max_steps, d):
            p, i = np.meshgrid(np.arange(max_steps), np.arange(d // 2))
            pe = np.zeros((max_steps, d), dtype=np.float32)
            pe[:, ::2] = np.sin(p / 2500 ** (2 * i / d)).T
            pe[:, 1::2] = np.cos(p / 2500 ** (2 * i / d)).T
            return jnp.asarray(pe)

        def batchnorm(x, gamma, beta):
            mean = jnp.mean(x, axis=(0, 1))
            var = jnp.var(x, axis=(0, 1))
            return (x - mean) * jax.lax.rsqrt(var + EPS) * gamma + beta
        B, S = x.shape
        D = emb.shape[1]
        H = 12
        hd = D // H
        N = 2
        scale = 1.0 / jnp.sqrt(jnp.asarray(D, jnp.float32))
        e = emb[x]
        P = pos_encoding(S, D)
        h = e + (e + P)

        def split_heads(t):
            return t.reshape(B, S, H, hd)
        for _ in range(N):
            q, k, v = jnp.split(h, 3, axis=-1)
            Q = split_heads(jax.nn.relu(q @ Wq + bq))
            K = split_heads(jax.nn.relu(k @ Wk + bk))
            V = split_heads(jax.nn.relu(v @ Wv + bv))
            scores = jnp.einsum('bqhd,bkhd->bhqk', Q, K) * scale
            attn = jax.nn.softmax(scores, axis=-1)
            o = jnp.einsum('bhqk,bkhd->bqhd', attn, V).reshape(B, S, D)
            t = batchnorm(h + o, g1, b1)
            h = batchnorm(t + (t @ Wf + bf), g2, b2)
        return h

    def _L0_attn_ref(x, Wq, Wk, Wv, Wo, proj):
        import jax, jax.numpy as jnp
        import numpy as np
        DIM = 192
        HEADS = 12
        DH = DIM // HEADS
        M = 64
        EPS = 0.0001

        def softmax_kernel(data, proj, is_query):
            data_normalizer = data.shape[-1] ** (-0.25)
            ratio = proj.shape[0] ** (-0.5)
            data_dash = jnp.einsum('bhsd,md->bhsm', data_normalizer * data, proj)
            diag = 0.5 * data_normalizer ** 2 * jnp.sum(data * data, axis=-1, keepdims=True)
            if is_query:
                stab = jnp.max(data_dash, axis=-1, keepdims=True)
            else:
                stab = jnp.max(data_dash, axis=(-2, -1), keepdims=True)
            stab = jax.lax.stop_gradient(stab)
            return ratio * (jnp.exp(data_dash - diag - stab) + EPS)
        B, S, _ = x.shape

        def split_heads(t):
            return t.reshape(B, S, HEADS, DH).transpose(0, 2, 1, 3)
        q = split_heads(x @ Wq)
        k = split_heads(x @ Wk)
        v = split_heads(x @ Wv)
        qp = softmax_kernel(q, proj, is_query=True)
        kp = softmax_kernel(k, proj, is_query=False)
        k_sum = jnp.sum(kp, axis=2)
        d_inv = 1.0 / jnp.einsum('bhsm,bhm->bhs', qp, k_sum)
        ctx = jnp.einsum('bhsm,bhsd->bhmd', kp, v)
        out = jnp.einsum('bhsm,bhmd,bhs->bhsd', qp, ctx, d_inv)
        out = out.transpose(0, 2, 1, 3).reshape(B, S, DIM)
        return out @ Wo

    def _L0_ffn_ref(x, ln1_g, ln1_b, qkv_w, qkv_b, proj_w, proj_b, ln2_g, ln2_b, gate_w, w1, b1, w2, b2):
        import jax, jax.numpy as jnp
        import numpy as np
        DIM = 192
        HEADS = 12
        EXPERTS = 8
        HID = 768
        TOP_K = 2
        LN_EPS = 1e-05

        def _layer_norm(x, g, b):
            mu = x.mean(-1, keepdims=True)
            var = ((x - mu) ** 2).mean(-1, keepdims=True)
            return (x - mu) * jax.lax.rsqrt(var + LN_EPS) * g + b

        def _attention(x, qkv_w, qkv_b, proj_w, proj_b):
            B, N, C = x.shape
            hd = C // HEADS
            qkv = (x @ qkv_w + qkv_b).reshape(B, N, 3, HEADS, hd).transpose(2, 0, 3, 1, 4)
            q, k, v = (qkv[0], qkv[1], qkv[2])
            attn = jax.nn.softmax(jnp.einsum('bhnd,bhmd->bhnm', q, k) * hd ** (-0.5), axis=-1)
            o = jnp.einsum('bhnm,bhmd->bhnd', attn, v).transpose(0, 2, 1, 3).reshape(B, N, C)
            return o @ proj_w + proj_b

        def _moe_mlp(xn, gate_w, w1, b1, w2, b2):
            T = xn.shape[0]
            logits = xn @ gate_w
            top_logits, top_idx = jax.lax.top_k(logits, TOP_K)
            top_gates = jax.nn.softmax(top_logits, axis=-1)
            gates = jnp.zeros((T, EXPERTS), xn.dtype).at[jnp.arange(T)[:, None], top_idx].set(top_gates)
            h = jax.nn.gelu(jnp.einsum('td,edh->teh', xn, w1) + b1, approximate=False)
            y = jnp.einsum('teh,ehd->ted', h, w2) + b2
            return jnp.einsum('ted,te->td', y, gates)
        B, N, C = x.shape
        x = x + _attention(_layer_norm(x, ln1_g, ln1_b), qkv_w, qkv_b, proj_w, proj_b)
        xn = _layer_norm(x, ln2_g, ln2_b).reshape(B * N, C)
        moe_out = _moe_mlp(xn, gate_w, w1, b1, w2, b2).reshape(B, N, C)
        return x + moe_out
    h = _L0_tok_ref(x, L0_tok_emb, L0_tok_Wq, L0_tok_bq, L0_tok_Wk, L0_tok_bk, L0_tok_Wv, L0_tok_bv, L0_tok_Wf, L0_tok_bf, L0_tok_g1, L0_tok_b1, L0_tok_g2, L0_tok_b2)
    h = h + _L0_attn_ref(_layernorm(h, axis=-1), L0_attn_Wq, L0_attn_Wk, L0_attn_Wv, L0_attn_Wo, L0_attn_proj)
    h = h + _L0_ffn_ref(_layernorm(h, axis=-1), L0_ffn_ln1_g, L0_ffn_ln1_b, L0_ffn_qkv_w, L0_ffn_qkv_b, L0_ffn_proj_w, L0_ffn_proj_b, L0_ffn_ln2_g, L0_ffn_ln2_b, L0_ffn_gate_w, L0_ffn_w1, L0_ffn_b1, L0_ffn_w2, L0_ffn_b2)
    return h

_drawn_inputs = setup_inputs


def setup_inputs(seed=0):
    import zlib

    import numpy as np

    out = dict(_drawn_inputs(seed))
    spreads = {'L0_tok_bq': (0.0, 0.8),
     'L0_tok_bk': (0.0, 0.8),
     'L0_tok_bv': (0.0, 0.8),
     'L0_tok_bf': (0.0, 2.0),
     'L0_tok_g1': (1.0, 0.2),
     'L0_tok_b1': (0.0, 2.0),
     'L0_tok_g2': (1.0, 0.2),
     'L0_tok_b2': (0.0, 0.1),
     'L0_ffn_ln1_g': (1.0, 0.6),
     'L0_ffn_ln1_b': (0.0, 0.8),
     'L0_ffn_qkv_b': (0.0, 0.456),
     'L0_ffn_proj_b': (0.0, 0.1),
     'L0_ffn_ln2_g': (1.0, 0.6),
     'L0_ffn_ln2_b': (0.0, 0.581),
     'L0_ffn_b1': (0.0, 0.764),
     'L0_ffn_b2': (0.0, 0.388)}
    factors = {'L0_tok_Wq': 8.0,
     'L0_tok_Wk': 8.0,
     'L0_tok_Wv': 7.777,
     'L0_ffn_qkv_w': 7.347,
     'L0_ffn_proj_w': 3.031}
    for name, (base, spread) in spreads.items():
        noise = np.random.default_rng([zlib.crc32(name.encode()), seed]).standard_normal(out[name].shape)
        drawn = base * np.exp(spread * noise) if base else spread * noise
        out[name] = jnp.asarray(drawn.astype(out[name].dtype))
    for name, factor in factors.items():
        out[name] = (out[name] * factor).astype(out[name].dtype)
    return out
```

```python
from contextlib import ExitStack

import numpy as np

import concourse.bass as bass
from concourse import mybir

F32 = mybir.dt.float32
BF16 = mybir.dt.bfloat16
I32 = mybir.dt.int32
ALU = mybir.AluOpType
ACT = mybir.ActivationFunctionType
AX = mybir.AxisListType.X

B, S, D, V = 8, 256, 192, 8000
T = B * S
H, HD = 12, 16
G, J = 3, 4
DC = D // 3
C1 = D - 128
M = 64
E, HID = 8, 768
HT = HID // 128
NT = T // 128
QT_ = S // 128
CH = 512
NCH = T // CH
LAYERS = 2
LAYER_LINKS = 84
STEPS = B * G
BN_EPS, LN_EPS, RF_EPS = 1e-5, 1e-5, 1e-4


class Chain:

    def __init__(self, eng, sem):
        self.eng, self.sem, self.base, self.k = eng, sem, 0, 0

    def put(self, ins):
        ins.then_inc(self.sem, 1)
        self.k += 1

    def wait(self):
        self.eng.wait_ge(self.sem, self.base + self.k)

    def link(self, ins):
        self.put(ins)
        self.wait()

    def enter(self, i, per):
        saved = self.base, self.k
        self.base, self.k = i * per + self.base + self.k, 0
        return saved, per

    def leave(self, mark, turns):
        (base, k), per = mark
        assert self.k == per, (self.k, per)
        self.base, self.k = base, k + turns * per


def build(nc, a, out):
    with ExitStack() as ctx:
        def sb(name, shape, dt=F32):
            return ctx.enter_context(nc.sbuf_tensor(name, shape, dt))

        def sem(name):
            return ctx.enter_context(nc.semaphore(name))

        PS = ctx.enter_context(nc.psum_tensor("PS", [128, 8, CH], F32))

        ident = sb("ident", [128, 128])
        half_ones = sb("half_ones", [128, 2, 2, HD])
        head_mask = sb("head_mask", [128, J])
        head_ones = sb("head_ones", [128, J])
        pos = sb("pos", [128, QT_, D])
        expert_no = sb("expert_no", [128, E])
        mean_w = sb("mean_w", [128, 128])
        ones12 = sb("ones12", [H, 128])

        tok_wq = sb("tok_wq", [128, G, J, 32])
        tok_wk = sb("tok_wk", [128, G, J, 32])
        tok_wv = sb("tok_wv", [C1 + 1, D])
        tok_qb = sb("tok_qb", [128, G])
        tok_kb = sb("tok_kb", [128, G])
        tok_wf0 = sb("tok_wf0", [128, D])
        tok_wf1 = sb("tok_wf1", [C1 + 1, D])
        bn_g = sb("bn_g", [128, 2, 2])
        bn_b = sb("bn_b", [128, 2, 2])
        rf_wq0 = sb("rf_wq0", [128, G, J, 32])
        rf_wq1 = sb("rf_wq1", [C1, G, J, 32])
        rf_wk0 = sb("rf_wk0", [128, G, J, 32])
        rf_wk1 = sb("rf_wk1", [C1, G, J, 32])
        rf_wv0 = sb("rf_wv0", [128, D])
        rf_wv1 = sb("rf_wv1", [C1, D])
        rf_wo0 = sb("rf_wo0", [128, D])
        rf_wo1 = sb("rf_wo1", [C1, D])
        rf_proj = sb("rf_proj", [128, J, M])
        ff_wq0 = sb("ff_wq0", [128, G, J, 32])
        ff_wq1 = sb("ff_wq1", [C1, G, J, 32])
        ff_wk0 = sb("ff_wk0", [128, G, J, 32])
        ff_wk1 = sb("ff_wk1", [C1, G, J, 32])
        ff_wv0 = sb("ff_wv0", [128, D])
        ff_wv1 = sb("ff_wv1", [C1 + 1, D])
        ff_qb = sb("ff_qb", [128, G])
        ff_kb = sb("ff_kb", [128, G])
        ff_wp0 = sb("ff_wp0", [128, D])
        ff_wp1 = sb("ff_wp1", [C1 + 1, D])
        ln_g = sb("ln_g", [128, 2, 2])
        ln_b = sb("ln_b", [128, 2, 2])
        gate0 = sb("gate0", [128, E])
        gate1 = sb("gate1", [C1, E])
        w1_0 = sb("w1_0", [128, E, HID])
        w1_1_all = sb("w1_1_all", [128, E, HID])
        w1_1 = w1_1_all[0:C1]
        w2_s = sb("w2_s", [128, E, HT, D])
        b1_s = sb("b1_s", [128, E, HT])
        b2_s = sb("b2_s", [E, D])

        tok_idx = sb("tok_idx", [128, NT], I32)
        idx_a = sb("idx_a", [128, NT], I32)
        idx_b = sb("idx_b", [128, NT], I32)
        rows = sb("rows", [128, NT, D])
        hT0 = sb("hT0", [128, T])
        hT1 = sb("hT1", [C1 + 1, T])
        nT0 = sb("nT0", [128, T])
        nT1 = sb("nT1", [C1 + 1, T])
        xT0 = sb("xT0", [128, T])
        xT1 = sb("xT1", [C1, T])
        oT0, oT1 = nT0, nT1
        in0 = sb("in0", [128, 2, S])
        in1 = sb("in1", [C1 + 1, 2, S])
        carved = [0]

        def carve(n, dt=F32):
            flat = w2_s[:].rearrange("p e t d -> p (e t d)")[:, carved[0]:carved[0] + n]
            carved[0] += n
            assert carved[0] <= E * HT * D
            return flat if dt == F32 else flat.bitcast(dt)

        QT = carve(2 * S).rearrange("p (k q) -> p k q", k=2)
        KT = carve(2 * S).rearrange("p (k q) -> p k q", k=2)
        QTb = carve(S, BF16).rearrange("p (k q) -> p k q", k=2)
        QM = carve(2 * J * S).rearrange("p (k j q) -> p k j q", k=2, j=J)
        KMb = carve(J * S, BF16).rearrange("p (k j q) -> p k j q", k=2, j=J)
        VA = carve(G * QT_ * J * 32).rearrange("p (g t j d) -> p g t j d", g=G, t=QT_, j=J)
        rmax = carve(QT_ * J * 32).rearrange("p (t j d) -> p t j d", t=QT_, j=J)
        FW = QT_ * H * M
        early = w1_1_all[:].rearrange("p e n -> p (e n)")
        P = early[:, 0:8 * QT_ * S].rearrange("p (n j t q) -> p n j t q", n=4, j=2, t=QT_)
        KP, QP = (early[:, n * FW:(n + 1) * FW].rearrange("p (t h m) -> p t h m", t=QT_, h=H) for n in range(2))
        QPT = early[:, 2 * FW:3 * FW].rearrange("p (t q n) -> p t q n", t=QT_, n=128)
        QK = early[:, 3 * FW:4 * FW].rearrange("p (g k q) -> p g k q", g=G, k=2)
        rsum = carve(S)
        on = carve(S)
        stats = sb("stats", [128, 2, NCH, 6])
        mv = sb("mv", [128, 2, 2])
        eps_t = sb("eps_t", [128, 1])
        bn_s = sb("bn_s", [128, 3, 2])
        HB = sb("HB", [128, 2, HT, CH])
        sq = HB[:, 1, 0:4].rearrange("p (k c) q -> p k c q", k=2)
        rstd = HB[:, 1, 4:6]
        SQ = carve(G * 2 * S).rearrange("p (g k q) -> p g k q", g=G, k=2)
        VB = carve(QT_ * H * (HD + 1)).rearrange("p (t h d) -> p t h d", t=QT_, h=H)
        fmax = sb("fmax", [128, 2, QT_, H])
        fsub = sb("fsub", [128, 2, QT_, H])
        stab = sb("stab", [H, 1])
        stab_d = sb("stab_d", [H, H])
        CTX = carve(H * (HD + 1)).rearrange("p (q h d) -> p q h d", q=H // 2, h=2)
        oinv = sb("oinv", [128, QT_, H])
        ob = carve(QT_ * D).rearrange("p (t d) -> p t d", t=QT_)
        obT0 = carve(S)
        obT1 = carve(S)[0:C1]
        lgT, gatesT = (HB[0:E, 0].rearrange("p m q -> p (m q)")[:, 0:T], HB[0:E, 1].rearrange("p m q -> p (m q)")[:, 0:T])
        lg = sb("lg", [128, NT, E])
        gt = sb("gt", [128, 6, NT, E])
        gs = sb("gs", [128, 6, NT])
        gT_b = sb("gT_b", [E, S])

        names = """const_in weights_in moe_in pad_done out_done
            idx_ready pool_set pool_turn dve_step emb_sum emb_ps emb_ev h_ready
            in_ready proj_ps v_ps qkv_ev cast_done smax_ps smax_red mT_ps aug_done st_ps p_ready av_ps o_done
            bn_var bn_root bn1_done ffn_ps lnm_ps ln_cent ln_sq lnv_ps ln_root ln_norm ln_aff
            rf_v rf_vev rf_qk rf_qkev rf_diag rf_diagev rf_dd rf_fmax rf_stT rf_std rf_stb rf_sub rf_exp rf_eps rf_ctx rf_ctxev
            rf_qpT rf_qpTev rf_out rf_o rf_oT rf_oTev rf_y rf_done
            xp_ps x2_done res_done lg_ps lg_ev lgT_ps gate_arg gate_exp gates_done gT_ps gT_ev
            fin_in fin_ps fin_cp fin_ev up_ps hid_ready down_ps y_done""".split()
        s = {n: sem(n) for n in names}
        rows_in = [sem(f"rows_in{b}") for b in range(B)]

        ctx.enter_context(nc.allow_non_contiguous_dma(reason="small vectors laid onto partitions once"))
        block = ctx.enter_context(nc.Block())

        consts = [(ident, a["c_ident"]), (head_mask, a["c_head_mask"]), (head_ones, a["c_head_ones"]),
                  (pos, a["c_pos"].rearrange("(t p) d -> p t d", p=128)), (expert_no, a["c_expert_no"]),
                  (tok_idx, a["x"].rearrange("b (t p) -> p (b t)", p=128))]
        pads = []

        def by_head(w):
            return w.rearrange("c (g j d) -> c g j d", g=G, j=J)

        heads = []
        for w, src, lo, n, r0 in ((tok_wq, a["L0_tok_Wq"], 0, DC, 0), (tok_wk, a["L0_tok_Wk"], 0, DC, DC),
                                  (rf_wq0, a["L0_attn_Wq"], 0, 128, 0), (rf_wq1, a["L0_attn_Wq"], 128, C1, 0),
                                  (rf_wk0, a["L0_attn_Wk"], 0, 128, 0), (rf_wk1, a["L0_attn_Wk"], 128, C1, 0)):
            for g in range(G):
                heads.append((w[r0:r0 + n, g, :, 0:HD], by_head(src)[lo:lo + n, g]))
        qkv_w = a["L0_ffn_qkv_w"]
        for w, part, lo, n in ((ff_wq0, 0, 0, 128), (ff_wq1, 0, 128, C1), (ff_wk0, 1, 0, 128), (ff_wk1, 1, 128, C1)):
            for g in range(G):
                heads.append((w[0:n, g, :, 0:HD], by_head(qkv_w[:, part * D:(part + 1) * D])[lo:lo + n, g]))

        def bias_cols(t, v):
            return [(t[32 * j:32 * j + HD, :], v.rearrange("(g j d) -> j d g", g=G, j=J)[j]) for j in range(J)]

        qkv_b = a["L0_ffn_qkv_b"]
        heads += bias_cols(tok_qb, a["L0_tok_bq"]) + bias_cols(tok_kb, a["L0_tok_bk"])
        heads += bias_cols(ff_qb, qkv_b[0:D]) + bias_cols(ff_kb, qkv_b[D:2 * D])
        heads += [(rf_proj[32 * j:32 * j + HD, j, :], a["c_projT"]) for j in range(J)]

        def row(v):
            return v.rearrange("(a d) -> a d", a=1)

        def cols(t, k, v):
            return [(t[:, k, 0:1], v[0:128].rearrange("(p a) -> p a", a=1)),
                    (t[0:C1, k, 1:2], v[128:D].rearrange("(p a) -> p a", a=1))]

        plain = [(tok_wv[0:C1, :], a["L0_tok_Wv"]), (tok_wv[C1:, :], row(a["L0_tok_bv"])),
                 (tok_wf0[:], a["L0_tok_Wf"][0:128, :]), (tok_wf1[0:C1, :], a["L0_tok_Wf"][128:D, :]),
                 (tok_wf1[C1:, :], row(a["L0_tok_bf"])),
                 (rf_wv0[:], a["L0_attn_Wv"][0:128, :]), (rf_wv1[:], a["L0_attn_Wv"][128:D, :]),
                 (rf_wo0[:], a["L0_attn_Wo"][0:128, :]), (rf_wo1[:], a["L0_attn_Wo"][128:D, :]),
                 (ff_wv0[:], qkv_w[0:128, 2 * D:]), (ff_wv1[0:C1, :], qkv_w[128:D, 2 * D:]),
                 (ff_wv1[C1:, :], row(qkv_b[2 * D:])),
                 (ff_wp0[:], a["L0_ffn_proj_w"][0:128, :]), (ff_wp1[0:C1, :], a["L0_ffn_proj_w"][128:D, :]),
                 (ff_wp1[C1:, :], row(a["L0_ffn_proj_b"])),
                 (gate0[:], a["L0_ffn_gate_w"][0:128, :]), (gate1[:], a["L0_ffn_gate_w"][128:D, :])]
        plain += cols(bn_g, 0, a["L0_tok_g1"]) + cols(bn_b, 0, a["L0_tok_b1"])
        plain += cols(bn_g, 1, a["L0_tok_g2"]) + cols(bn_b, 1, a["L0_tok_b2"])
        plain += cols(ln_g, 0, a["L0_ffn_ln1_g"]) + cols(ln_b, 0, a["L0_ffn_ln1_b"])
        plain += cols(ln_g, 1, a["L0_ffn_ln2_g"]) + cols(ln_b, 1, a["L0_ffn_ln2_b"])
        moe = [(w1_0[:], a["L0_ffn_w1"][:, 0:128, :].rearrange("e c n -> c e n")),
               (b1_s[:], a["L0_ffn_b1"].rearrange("e (t p) -> p e t", p=128)),
               (b2_s[:], a["L0_ffn_b2"])]
        late = [(w1_1, a["L0_ffn_w1"][:, 128:D, :].rearrange("e c n -> c e n"))]
        late += [(w2_s[:, e], a["L0_ffn_w2"][e].rearrange("(t p) d -> p t d", p=128)) for e in range(E)]
        zeroed = [tok_wq, tok_wk, rf_wq0, rf_wq1, rf_wk0, rf_wk1, ff_wq0, ff_wq1, ff_wk0, ff_wk1, rf_proj, tok_qb, ff_qb]
        MEMSETS = len(zeroed) + 15
        WEIGHTS_IN = 16 * (len(plain) + len(heads))

        @block.sync
        def _(sp):
            for dst, src in consts:
                sp.dma_start(dst[:], src).then_inc(s["const_in"], 16)
            sp.dma_start(tok_kb[:], a["c_kones"]).then_inc(s["pad_done"], 16)
            sp.dma_start(ff_kb[:], a["c_kones"]).then_inc(s["pad_done"], 16)
            for dst, src in plain:
                sp.dma_start(dst, src).then_inc(s["weights_in"], 16)
            sp.wait_ge(s["pad_done"], 32)
            sp.wait_ge(s["pool_set"], MEMSETS)
            for dst, src in heads:
                sp.dma_start(dst, src).then_inc(s["weights_in"], 16)
            for dst, src in moe:
                sp.dma_start(dst, src).then_inc(s["moe_in"], 16)
            sp.wait_ge(s["o_done"], (LAYERS + 1) * STEPS)
            for dst, src in late:
                sp.dma_start(dst, src).then_inc(s["moe_in"], 16)
            sp.wait_ge(s["y_done"], 4 + NCH * 4 * E)
            sp.dma_start(out.rearrange("b (t p) d -> p (b t) d", p=128), rows[:]).then_inc(s["out_done"], 16)
            sp.wait_ge(s["out_done"], 16)

        @block.gpsimd
        def _(pool):
            k = 0
            for t in zeroed:
                nc.gpsimd.memset(t[:], 0.0).then_inc(s["pool_set"], 1)
                k += 1
            for t, v in ((mean_w[:], 1.0 / D), (ones12[:], 1.0), (eps_t[:], BN_EPS), (VA, 0.0), (QM, 0.0), (VB, 1.0), (rmax, 0.0), (half_ones[:], 0.0),
                         (half_ones[:, 0, 0], 1.0), (half_ones[:, 1, 1], 1.0),
                         (hT1[C1:, :], 1.0), (nT1[C1:, :], 1.0), (CTX, 0.0),
                         (bn_g[64:, :, 1:2], 0.0), (bn_b[64:, :, 1:2], 0.0)):
                pool.wait_ge(s["pool_set"], k)
                nc.gpsimd.memset(t, v).then_inc(s["pool_set"], 1)
                k += 1
            assert k == MEMSETS
            pool.wait_ge(s["idx_ready"], 1)
            for t in range(NT):
                pool.indirect_dma_start(rows[:, t, :], None, a["L0_tok_emb"],
                                        bass.IndirectOffsetOnAxis(ap=idx_a[:, t:t + 1], axis=0)).then_inc(rows_in[t // QT_], 16)

            def then(value, name):
                pool.wait_ge(s[name], value)
                pool.sem_inc(s["pool_turn"], 1)

            def copy_in(src0, src1, b, slot):
                cols = bass.ds(b * S, S)
                nc.gpsimd.tensor_copy(in0[:, slot, :], src0[:, cols]).then_inc(s["in_ready"], 1)
                nc.gpsimd.tensor_copy(in1[:, slot, :], src1[:, cols]).then_inc(s["in_ready"], 1)

            def attention(src0, src1, s0):
                def turn(c, i):
                    then(3 * s0 + 18 * i + (3 * c + 2), "qkv_ev")
                    nc.gpsimd.tensor_copy(QTb[:, c % 2, :], QT[:, c % 2, :]).then_inc(s["cast_done"], 1)
                    nc.gpsimd.tensor_tensor(KMb[:, c % 2], KT[:, c % 2, :][:, None, :].broadcast_to([128, J, S]),
                                            head_mask[:, :, None].broadcast_to([128, J, S]), ALU.mult)\
                      .then_inc(s["cast_done"], 1)
                    if c % G == 0 and c // G + 1 < B:
                        copy_in(src0, src1, 2 * i + c // G + 1, (c // G + 1) % 2)

                copy_in(src0, src1, 0, 0)
                for c in range(3):
                    turn(c, 0)
                with pool.Fori(0, 3) as i:
                    for c in range(3, 9):
                        turn(c, i)
                for c in range(21, STEPS):
                    turn(c, 0)

            with pool.Fori(0, LAYERS) as l:
                then(l + 1, "h_ready")
                attention(hT0, hT1, l * STEPS)
            pool.wait_ge(s["ln_norm"], 2 * NCH)
            with pool.Fori(0, B) as b:
                then(b * 2 + 1, "rf_done")
                copy_in(nT0, nT1, b, 0)
            pool.wait_ge(s["ln_aff"], 2 * NCH)
            attention(nT0, nT1, LAYERS * STEPS)
            pool.wait_ge(s["res_done"], 2)
            pool.wait_ge(s["gT_ev"], 1)
            with pool.Fori(0, B) as b:
                then(b + 1, "fin_ps")
                cols = bass.ds(b * S, S)
                nc.gpsimd.tensor_copy(in0[:, 0, :], hT0[:, cols]).then_inc(s["fin_in"], 1)
                nc.gpsimd.tensor_copy(in1[0:C1, 0, :], hT1[0:C1, cols]).then_inc(s["fin_in"], 1)
                nc.gpsimd.tensor_copy(gT_b[:], gatesT[:, cols]).then_inc(s["fin_in"], 1)

        @block.tensor
        def _(pe):
            pe.sem_inc(s["fin_ps"], 1)
            pe.sem_inc(s["down_ps"], 8)
            pe.wait_ge(s["const_in"], 16 * len(consts))
            for b in range(B):
                pe.wait_ge(s["emb_sum"], b + 1)
                if b >= 4:
                    pe.wait_ge(s["emb_ev"], 2 * (b - 3))
                for t in range(QT_):
                    pe.transpose(PS[:, 2 * (b % 4), 128 * t:128 * t + 128], rows[:, QT_ * b + t, 0:128], ident[:])
                    last = pe.transpose(PS[0:C1, 2 * (b % 4) + 1, 128 * t:128 * t + 128], rows[:, QT_ * b + t, 128:D],
                                        ident[:])
                last.then_inc(s["emb_ps"], 1)

            def proj(c, step, wq, wk, batch2):
                g, pb = c % G, (c // G) % 2
                if c % G == 0:
                    pe.wait_ge(s["in_ready"], batch2)
                if c > 0:
                    pe.wait_ge(s["qkv_ev"], 3 * step)
                ins = (in0[:, pb, :], in1[:, pb, :])
                for w, lo in ((wq, 0), (wk, S)):
                    for n, (wt, ch) in enumerate(w):
                        last = pe.matmul(PS[:, 6, lo:lo + S], wt[:, g].rearrange("c j d -> c (j d)"),
                                  ins[ch][0:wt.shape[0]], start=n == 0, stop=n == len(w) - 1)
                last.then_inc(s["proj_ps"], 1)

            def proj_v(c, step, wv):
                g, pb = c % G, (c // G) % 2
                ins = (in0[:, pb, :], in1[:, pb, :])
                if c == 1:
                    pe.wait_ge(s["qkv_ev"], 3 * step)
                if c > 1:
                    pe.wait_ge(s["smax_red"], 4 * step)
                for t in range(QT_):
                    for n, (wt, ch) in enumerate(wv):
                        last = pe.matmul(PS[:, 5, 64 * t:64 * t + 64],
                                         ins[ch][0:wt.shape[0], 128 * t:128 * t + 128],
                                         wt[:, 64 * g:64 * g + 64], start=n == 0, stop=n == len(wv) - 1)
                last.then_inc(s["v_ps"], 1)

            def smax(c, step):
                p = c % 2
                pe.wait_ge(s["cast_done"], 2 * (step + 1))
                for j in range(J):
                    if j == 0 and c > 0:
                        pe.wait_ge(s["aug_done"], 4 * step)
                    if j == 1:
                        pe.wait_ge(s["qkv_ev"], 3 * step + (3 if c > 0 else 6))
                    if j >= 2:
                        pe.wait_ge(s["smax_red"], 4 * step + j - 1)
                    for t in range(QT_):
                        last = pe.matmul(PS[:, 4 + j % 2, S * t:S * t + S],
                                         QTb[:, p, 128 * t:128 * t + 128], KMb[:, p, j, :], start=True, stop=True)
                    last.then_inc(s["smax_ps"], 1)

            def turn_max(c, step):
                pe.wait_ge(s["smax_red"], 4 * (step + 1))
                for t in range(QT_):
                    last = pe.transpose(PS[:, 4, 128 * t:128 * t + 128], rmax[:, t].rearrange("p j d -> p (j d)"),
                                        ident[:])
                last.then_inc(s["mT_ps"], 1)

            def scores(c, step):
                p = c % 2
                for h in range(2):
                    if c > 0:
                        pe.wait_ge(s["p_ready"], 2 * step + h - 1)
                    for t in range(QT_):
                        for j in (2 * h, 2 * h + 1):
                            if t == 0:
                                pe.wait_ge(s["aug_done"], 4 * step + (j + 1))
                            last = pe.matmul(PS[:, j, S * t:S * t + S], KT[:, p, 128 * t:128 * t + 128],
                                             QM[:, p, j, :], start=True, stop=True)
                    last.then_inc(s["st_ps"], 1)

            def weigh(c, step):
                if c > 0:
                    pe.wait_ge(s["o_done"], step)
                pe.wait_ge(s["p_ready"], 2 * (step + 1))
                pe.wait_ge(s["qkv_ev"], 3 * (step + 1))
                for n in range(2 * QT_):
                    hh, t = n // QT_, n % QT_
                    for lo in (0, 64):
                        for pr in range(2):
                            j = 2 * pr + hh
                            w = half_ones[:, hh].rearrange("p h d -> p (h d)") if lo else VA[:, c % G, t, j, :]
                            last = pe.matmul(PS[lo + 32 * pr:lo + 32 * pr + 32, 7, 0:S], w,
                                             P[:, 2 * (c % 2) + j // 2, j % 2, t, :], start=n == 0, stop=n == 2 * QT_ - 1,
                                             skip_group_check=True)
                last.then_inc(s["av_ps"], 1)

            def attention(s0, b0, wq, wk, wv):
                def pj(c, i):
                    proj(c, s0 + 6 * i + c, wq, wk, 2 * (b0 + 2 * i + c // G + 1))

                def turn(c, i):
                    step = s0 + 6 * i + c
                    scores(c, step)
                    if c + 1 < STEPS:
                        smax(c + 1, step + 1)
                    if c > 0:
                        weigh(c - 1, step - 1)
                    if c + 2 < STEPS:
                        pj(c + 2, i)
                    if c + 1 < STEPS:
                        turn_max(c + 1, step + 1)
                    if c + 2 < STEPS:
                        proj_v(c + 2, step + 2, wv)

                pj(0, 0)
                proj_v(0, s0, wv)
                pj(1, 0)
                proj_v(1, s0 + 1, wv)
                smax(0, s0)
                turn_max(0, s0)
                for c in range(3):
                    turn(c, 0)
                with pe.Fori(0, 3) as i:
                    for c in range(3, 9):
                        turn(c, i)
                for c in range(21, STEPS):
                    turn(c, 0)
                weigh(STEPS - 1, s0 + STEPS - 1)

            def linear(w0, w1, x0, x1, done):
                for c in range(NCH):
                    cs = slice(CH * c, CH * c + CH)
                    for k, (lo, n) in enumerate(((0, 128), (128, C1))):
                        pe.matmul(PS[0:n, 2 * c + k, :], w0[:, lo:lo + n], x0[:, cs], start=True, stop=False)
                        pe.matmul(PS[0:n, 2 * c + k, :], w1[:, lo:lo + n], x1[:, cs], start=False, stop=True)\
                          .then_inc(s[done], 1)

            def layer_norm(x0, x1, y0, y1, n, src_ready=None):
                if src_ready:
                    pe.wait_ge(s[src_ready[0]], src_ready[1])
                for c in range(NCH):
                    cs = slice(CH * c, CH * c + CH)
                    pe.matmul(PS[:, c, :], mean_w[:], x0[:, cs], start=True, stop=False)
                    pe.matmul(PS[:, c, :], mean_w[0:C1, :], x1[0:C1, cs], start=False, stop=True).then_inc(s["lnm_ps"], 1)
                for c in range(NCH):
                    pe.wait_ge(s["ln_sq"], 2 * (n * NCH + c + 1))
                    pe.matmul(PS[:, 4 + c, :], mean_w[:], sq[:, c % 2, 0, :], start=True, stop=False)
                    pe.matmul(PS[:, 4 + c, :], mean_w[0:C1, :], sq[0:C1, c % 2, 1, :], start=False, stop=True)\
                      .then_inc(s["lnv_ps"], 1)

            pe.wait_ge(s["weights_in"], WEIGHTS_IN)
            pe.wait_ge(s["pool_set"], MEMSETS)
            with pe.Fori(0, LAYERS) as l:
                attention(l * STEPS, l * B, [(tok_wq, 0)], [(tok_wk, 0)], [(tok_wv, 1)])
                pe.wait_ge(s["bn1_done"], l + 1)
                linear(tok_wf0, tok_wf1, hT0, hT1, "ffn_ps")

            layer_norm(hT0, hT1, nT0, nT1, 0, ("h_ready", LAYERS + 1))
            IN0 = 2 * B * LAYERS
            with pe.Fori(0, B) as b:
                pe.wait_ge(s["in_ready"], b * 2 + IN0 + 2)
                pe.wait_ge(s["rf_done"], b * 2 + 1)
                for t in range(QT_):
                    ts = slice(128 * t, 128 * t + 128)
                    pe.matmul(PS[:, 7, D * t:D * t + D], in0[:, 0, ts], rf_wv0[:], start=True, stop=False)
                    last = pe.matmul(PS[:, 7, D * t:D * t + D], in1[0:C1, 0, ts], rf_wv1[:], start=False, stop=True)
                last.then_inc(s["rf_v"], 1)
                for g, bank in enumerate((6, 3, 4)):
                    for k, (wa, wb) in enumerate(((rf_wq0, rf_wq1), (rf_wk0, rf_wk1))):
                        pe.matmul(PS[:, bank, S * k:S * k + S], wa[:, g].rearrange("c j d -> c (j d)"), in0[:, 0, :],
                                  start=True, stop=False)
                        last = pe.matmul(PS[:, bank, S * k:S * k + S], wb[:, g].rearrange("c j d -> c (j d)"),
                                         in1[0:C1, 0, :], start=False, stop=True)
                    last.then_inc(s["rf_qk"], 1)
                pe.wait_ge(s["rf_qkev"], b * 6 + 6)
                pe.wait_ge(s["rf_vev"], b + 1)
                for k in range(2):
                    for t in range(QT_):
                        for g in range(G):
                            at = (k * QT_ + t) * H + J * g
                            last = pe.matmul(PS[:, 7, at:at + J], SQ[:, g, k, 128 * t:128 * t + 128], head_ones[:],
                                             start=True, stop=True)
                last.then_inc(s["rf_diag"], 1)
                for k, bank0 in ((1, 0), (0, 3)):
                    for t in range(QT_):
                        for g in range(G):
                            blk = G * t + g
                            last = pe.matmul(PS[:, bank0 + blk // 2, S * (blk % 2):S * (blk % 2) + S],
                                      QK[:, g, k, 128 * t:128 * t + 128], rf_proj[:].rearrange("p j m -> p (j m)"),
                                      start=True, stop=True)
                    last.then_inc(s["rf_dd"], 1)
                pe.wait_ge(s["rf_diagev"], b + 1)
                pe.wait_ge(s["rf_fmax"], b + 1)
                for t in range(QT_):
                    last = pe.transpose(PS[0:H, 7, 128 * t:128 * t + 128], fmax[:, 1, t, :], ident[:])
                last.then_inc(s["rf_stT"], 1)
                pe.wait_ge(s["rf_std"], b + 1)
                pe.matmul(PS[:, 7, 256:256 + H], ones12[:], stab_d[:], start=True, stop=True).then_inc(s["rf_stb"], 1)
                pe.wait_ge(s["rf_eps"], b * 2 + 1)
                for p in range(H // 2):
                    for t in range(QT_):
                        last = pe.matmul(PS[:, 0, 34 * p:34 * p + 34],
                                         KP[:, t, 2 * p:2 * p + 2, :].rearrange("p h m -> p (h m)"),
                                         VB[:, t, 2 * p:2 * p + 2, :].rearrange("p h d -> p (h d)"),
                                         start=t == 0, stop=t == QT_ - 1)
                last.then_inc(s["rf_ctx"], 1)
                pe.wait_ge(s["rf_eps"], b * 2 + 2)
                for t, bank0 in enumerate((1, 3)):
                    for p in range(H // 2):
                        last = pe.transpose(PS[:, bank0 + p // 4, 128 * (p % 4):128 * (p % 4) + 128],
                                            QP[:, t, 2 * p:2 * p + 2, :].rearrange("p h m -> p (h m)"), ident[:])
                    last.then_inc(s["rf_qpT"], 1)
                pe.wait_ge(s["rf_ctxev"], b * 2 + 2)
                for t in range(QT_):
                    pe.wait_ge(s["rf_qpTev"], b * 2 + (t + 1))
                    for p in range(H // 2):
                        last = pe.matmul(PS[:, 5, 204 * t + 34 * p:204 * t + 34 * p + 34], QPT[:, t, p, :],
                                         CTX[:, p].rearrange("p h d -> p (h d)"), start=True, stop=True)
                last.then_inc(s["rf_out"], 1)
                pe.wait_ge(s["rf_o"], b + 1)
                for t in range(QT_):
                    pe.transpose(PS[:, 6, 128 * t:128 * t + 128], ob[:, t, 0:128], ident[:])
                    last = pe.transpose(PS[0:C1, 6, S + 128 * t:S + 128 * t + 128], ob[:, t, 128:D], ident[:])
                last.then_inc(s["rf_oT"], 1)
                pe.wait_ge(s["rf_oTev"], b * 2 + 2)
                for k, (lo, n) in enumerate(((0, 128), (128, C1))):
                    pe.matmul(PS[0:n, 7, S * k:S * k + S], rf_wo0[:, lo:lo + n], obT0[:], start=True, stop=False)
                    last = pe.matmul(PS[0:n, 7, S * k:S * k + S], rf_wo1[:, lo:lo + n], obT1[:], start=False, stop=True)
                last.then_inc(s["rf_y"], 1)

            pe.wait_ge(s["rf_done"], 2 * B + 1)
            layer_norm(hT0, hT1, xT0, xT1, 1)
            pe.wait_ge(s["ln_norm"], 2 * 2 * NCH)
            layer_norm(xT0, xT1, nT0, nT1, 2)
            pe.wait_ge(s["ln_aff"], 2 * NCH)
            attention(LAYERS * STEPS, B * LAYERS + B, [(ff_wq0, 0), (ff_wq1, 1)], [(ff_wk0, 0), (ff_wk1, 1)],
                      [(ff_wv0, 0), (ff_wv1, 1)])
            pe.wait_ge(s["o_done"], (LAYERS + 1) * STEPS)
            linear(ff_wp0, ff_wp1, oT0, oT1, "xp_ps")
            pe.wait_ge(s["x2_done"], 2 * NCH)
            layer_norm(xT0, xT1, nT0, nT1, 3)
            pe.wait_ge(s["moe_in"], 16 * (len(moe) + len(late)))
            pe.wait_ge(s["ln_aff"], 4 * NCH)
            for c in range(NCH):
                cs = slice(CH * c, CH * c + CH)
                pe.matmul(PS[0:E, c, :], gate0[:], nT0[:, cs], start=True, stop=False)
                pe.matmul(PS[0:E, c, :], gate1[:], nT1[0:C1, cs], start=False, stop=True).then_inc(s["lg_ps"], 1)
            pe.wait_ge(s["lg_ev"], NCH)
            for t in range(NT):
                last = pe.transpose(PS[:, 4, E * t:E * t + E], lgT[:, 128 * t:128 * t + 128], ident[0:E, 0:E])
            last.then_inc(s["lgT_ps"], 1)
            pe.wait_ge(s["gates_done"], 1)
            for t in range(NT):
                last = pe.transpose(PS[0:E, t // 4, 128 * (t % 4):128 * (t % 4) + 128], gt[:, 5, t, :], ident[:])
            last.then_inc(s["gT_ps"], 1)
            pe.wait_ge(s["gT_ev"], 1)
            with pe.Fori(0, B) as b:
                pe.wait_ge(s["fin_in"], b * 3 + 3)
                pe.wait_ge(s["fin_ev"], b + 1)
                for t in range(QT_):
                    ts = slice(128 * t, 128 * t + 128)
                    pe.matmul(PS[:, 5 + t, 0:D], gT_b[:, ts], b2_s[:], start=True, stop=True)
                    pe.transpose(PS[:, 5 + t, D:D + 128], in0[:, 0, ts], ident[:])
                    last = pe.transpose(PS[:, 5 + t, D + 128:2 * D], in1[0:C1, 0, ts], ident[0:C1, 0:C1])
                last.then_inc(s["fin_ps"], 1)

            def up(c, cs, e):
                for m in range(HT):
                    k = HT * e + m
                    pe.wait_ge(s["hid_ready"], c * (E * HT) + (k + 1))
                    pe.matmul(PS[:, k % 4, :], w1_0[:, e, 128 * m:128 * m + 128], nT0[:, cs], start=True, stop=False)
                    pe.matmul(PS[:, k % 4, :], w1_1[:, e, 128 * m:128 * m + 128], nT1[0:C1, cs], start=False, stop=True)\
                      .then_inc(s["up_ps"], 1)

            def down(c, e):
                pe.wait_ge(s["hid_ready"], c * (E * HT) + (HT * (e + 1) + 4))
                for q in range(4):
                    pe.wait_ge(s["y_done"], c * (4 * E) + (4 * e + q + 1))
                    for m in range(HT):
                        last = pe.matmul(PS[:, 4 + q, 0:D], HB[:, e % 2, m, 128 * q:128 * q + 128], w2_s[:, e, m, :],
                                         start=m == 0, stop=m == HT - 1)
                    last.then_inc(s["down_ps"], 1)

            pe.wait_ge(s["fin_ev"], B + 1)
            with pe.Fori(0, NCH) as c:
                cs = bass.ds(c * CH, CH)
                up(c, cs, 0)
                for e in range(E):
                    if e + 1 < E:
                        up(c, cs, e + 1)
                    down(c, e)

        @block.scalar
        def _(act):
            act.sem_inc(s["hid_ready"], 4)
            act.wait_ge(s["pool_set"], MEMSETS)
            for b in range(B):
                act.wait_ge(s["emb_ps"], b + 1)
                nc.scalar.copy(hT0[:, S * b:S * b + S], PS[:, 2 * (b % 4), 0:S]).then_inc(s["emb_ev"], 1)
                nc.scalar.copy(hT1[0:C1, S * b:S * b + S], PS[0:C1, 2 * (b % 4) + 1, 0:S]).then_inc(s["emb_ev"], 1)

            def exps(c, step, scale):
                for h in range(2):
                    act.wait_ge(s["st_ps"], 2 * step + (h + 1))
                    nc.scalar.activation(P[:, 2 * (c % 2) + h].rearrange("p j t q -> p (j t q)"),
                                         PS[:, 2 * h:2 * h + 2, :].rearrange("p b q -> p (b q)"), ACT.Exp,
                                         scale=scale).then_inc(s["p_ready"], 1)

            def qkv(c, step, func, qb, kb):
                g = c % G
                act.wait_ge(s["proj_ps"], step + 1)
                nc.scalar.activation(QT[:, c % 2, :], PS[:, 6, 0:S], func, bias=qb[:, g:g + 1]).then_inc(s["qkv_ev"], 1)
                nc.scalar.activation(KT[:, c % 2, :], PS[:, 6, S:2 * S], func, bias=kb[:, g:g + 1]).then_inc(s["qkv_ev"], 1)
                act.wait_ge(s["v_ps"], step + 1)
                v = VA[:, g].rearrange("p t (q h) d -> p (t q) (h d)", h=2)
                nc.scalar.activation(bass.AP(tensor=v.tensor, offset=v.offset, ap=[v.ap[0], v.ap[1], [48, 2], [1, HD]]),
                                     PS[:, 5, 0:128].rearrange("p (t h d) -> p t h d", h=2, d=HD), func)\
                  .then_inc(s["qkv_ev"], 1)

            def attention(s0, func, qb, kb, scale):
                def turn(c, i):
                    step = s0 + 6 * i + c
                    exps(c, step, scale)
                    if c + 2 < STEPS:
                        qkv(c + 2, step + 2, func, qb, kb)

                qkv(0, s0, func, qb, kb)
                qkv(1, s0 + 1, func, qb, kb)
                for c in range(3):
                    turn(c, 0)
                with act.Fori(0, 3) as i:
                    for c in range(3, 9):
                        turn(c, i)
                for c in range(21, STEPS):
                    turn(c, 0)

            def layer_norm(y0, y1, n, aff=None):
                for c in range(NCH):
                    cs = slice(CH * c, CH * c + CH)
                    act.wait_ge(s["ln_cent"], 2 * (n * NCH + c + 1))
                    if c >= 2:
                        act.wait_ge(s["lnv_ps"], n * NCH + c - 1)
                    nc.scalar.activation(sq[:, c % 2, 0, :], y0[:, cs], ACT.Square).then_inc(s["ln_sq"], 1)
                    nc.scalar.activation(sq[0:C1, c % 2, 1, :], y1[0:C1, cs], ACT.Square).then_inc(s["ln_sq"], 1)
                for c in range(NCH):
                    act.wait_ge(s["lnv_ps"], n * NCH + c + 1)
                    if c >= 2:
                        act.wait_ge(s["ln_norm"], 2 * (n * NCH + c - 1))
                    nc.scalar.activation(rstd[:, c % 2, :], PS[:, 4 + c, :], ACT.Sqrt, bias=eps_t[:, 0:1])\
                      .then_inc(s["ln_root"], 1)
                if aff is not None:
                    for c in range(NCH):
                        cs = slice(CH * c, CH * c + CH)
                        act.wait_ge(s["ln_norm"], 2 * (n * NCH + c + 1))
                        nc.scalar.activation(y0[:, cs], y0[:, cs], ACT.Identity, bias=ln_b[:, aff, 0:1],
                                             scale=ln_g[:, aff, 0:1]).then_inc(s["ln_aff"], 1)
                        nc.scalar.activation(y1[0:C1, cs], y1[0:C1, cs], ACT.Identity, bias=ln_b[0:C1, aff, 1:2],
                                             scale=ln_g[0:C1, aff, 1:2]).then_inc(s["ln_aff"], 1)

            act.wait_ge(s["weights_in"], WEIGHTS_IN)
            with act.Fori(0, LAYERS) as l:
                attention(l * STEPS, ACT.Relu, tok_qb, tok_kb, float(D) ** -0.5)
                for n in range(2):
                    act.wait_ge(s["bn_var"], l * 4 + 2 * (n + 1))
                    nc.scalar.activation(bn_s[:, 2, :], mv[:, :, 1], ACT.Sqrt, bias=eps_t[:, 0:1])\
                      .then_inc(s["bn_root"], 1)

            layer_norm(nT0, nT1, 0)
            with act.Fori(0, B) as b:
                act.wait_ge(s["rf_v"], b + 1)
                nc.scalar.copy(VB[:, :, :, 0:HD], PS[:, 7, 0:QT_ * D].rearrange("p (t h d) -> p t h d", t=QT_, h=H))\
                  .then_inc(s["rf_vev"], 1)
                for g, bank in enumerate((6, 3, 4)):
                    act.wait_ge(s["rf_qk"], b * 3 + (g + 1))
                    for dst, func in ((QK, ACT.Copy), (SQ, ACT.Square)):
                        nc.scalar.activation(dst[:, g].rearrange("p k q -> p (k q)"), PS[:, bank, :], func,
                                             scale=float(HD) ** -0.25).then_inc(s["rf_qkev"], 1)
                for k, X in enumerate((KP, QP)):
                    act.wait_ge(s["rf_sub"], b * 2 + (k + 1))
                    v = X.rearrange("p t h m -> p (t h m)")
                    nc.scalar.activation(v, v, ACT.Exp).then_inc(s["rf_exp"], 1)
                act.wait_ge(s["rf_ctx"], b + 1)
                for k in range(2):
                    nc.scalar.copy(CTX[64 * k:64 * k + 64, :, k, :],
                                   PS[64 * k:64 * k + 64, 0, 0:204].rearrange("p (q h d) -> p q h d", h=2, d=HD + 1)[:, :, k, :])\
                      .then_inc(s["rf_ctxev"], 1)
                for t, bank0 in enumerate((1, 3)):
                    act.wait_ge(s["rf_qpT"], b * 2 + (t + 1))
                    nc.scalar.copy(QPT[:, t].rearrange("p q n -> p (q n)"),
                                   PS[:, bank0:bank0 + 2, :].rearrange("p b q -> p (b q)")[:, 0:768])\
                      .then_inc(s["rf_qpTev"], 1)
                act.wait_ge(s["rf_oT"], b + 1)
                nc.scalar.copy(obT0[:], PS[:, 6, 0:S]).then_inc(s["rf_oTev"], 1)
                nc.scalar.copy(obT1[:], PS[0:C1, 6, S:2 * S]).then_inc(s["rf_oTev"], 1)

            layer_norm(xT0, xT1, 1)
            layer_norm(nT0, nT1, 2, 0)
            attention(LAYERS * STEPS, ACT.Identity, ff_qb, ff_kb, float(HD) ** -0.5)
            layer_norm(nT0, nT1, 3, 1)
            for c in range(NCH):
                act.wait_ge(s["lg_ps"], c + 1)
                nc.scalar.copy(lgT[:, CH * c:CH * c + CH], PS[0:E, c, :]).then_inc(s["lg_ev"], 1)
            act.wait_ge(s["gate_arg"], 1)
            nc.scalar.activation(gs[:, 2, :], gs[:, 2, :], ACT.Exp).then_inc(s["gate_exp"], 1)
            act.wait_ge(s["gT_ps"], 1)
            nc.scalar.copy(gatesT, PS[0:E, 0:4, :].rearrange("p b q -> p (b q)")).then_inc(s["gT_ev"], 1)
            with act.Fori(0, B) as b:
                act.wait_ge(s["fin_ps"], b + 2)
                nc.scalar.copy(rows[:, bass.ds(b * QT_, QT_), :], PS[:, 5:7, D:2 * D]).then_inc(s["fin_cp"], 1)
            with act.Fori(0, NCH) as c:
                for e in range(E):
                    for m in range(HT):
                        k = HT * e + m
                        act.wait_ge(s["up_ps"], c * (E * HT) + (k + 1))
                        if m == 0:
                            act.wait_ge(s["down_ps"], c * (4 * E) + 4 * (e + 1))
                        nc.scalar.activation(HB[:, e % 2, m, :], PS[:, k % 4, :], ACT.Gelu, bias=b1_s[:, e, m:m + 1])\
                          .then_inc(s["hid_ready"], 1)

        @block.vector
        def _(dve):
            dve.sem_inc(s["rf_done"], 1)
            dve.sem_inc(s["fin_ev"], 1)
            dve.sem_inc(s["y_done"], 4)
            ch = Chain(dve, s["dve_step"])
            tt, ts_, stt = nc.vector.tensor_tensor, nc.vector.tensor_scalar, nc.vector.scalar_tensor_tensor

            dve.wait_ge(s["const_in"], 16 * len(consts))
            ch.link(ts_(idx_b[:], tok_idx[:], 0, V, ALU.is_lt, ALU.mult))
            ch.link(tt(idx_b[:], idx_b[:], tok_idx[:], ALU.add))
            ts_(idx_a[:], idx_b[:], 0, V - 1, ALU.max, ALU.min).then_inc(s["idx_ready"], 1)
            for b in range(B):
                dve.wait_ge(rows_in[b], 32)
                r = rows[:, QT_ * b:QT_ * b + QT_, :]
                if b > 0:
                    dve.wait_ge(s["emb_sum"], b)
                ch.link(tt(ob[:], r, pos[:], ALU.add))
                tt(r, r, ob[:], ALU.add).then_inc(s["emb_sum"], 1)
            dve.wait_ge(s["emb_ev"], 2 * B)
            dve.sem_inc(s["h_ready"], 1)

            def maxima(c, step):
                for j in range(J):
                    dve.wait_ge(s["smax_ps"], 4 * step + (j + 1))
                    nc.vector.tensor_reduce(rmax[:, :, j, HD], PS[:, 4 + j % 2, :].rearrange("p (t k) -> p t k", t=QT_),
                                            AX, ALU.max).then_inc(s["smax_red"], 1)
                dve.wait_ge(s["mT_ps"], step + 1)
                for j in range(J):
                    r = slice(32 * j, 32 * j + 32)
                    tt(QM[r, c % 2, j, :], QT[r, c % 2, :], PS[r, 4, 0:S], ALU.subtract).then_inc(s["aug_done"], 1)

            def normalise(c, step, b, add):
                g = c % G
                lo, cols = 64 * (g % 2), bass.ds(b * S, S)
                rs = slice(lo, lo + 64)
                dve.wait_ge(s["av_ps"], step + 1)
                ch.link(nc.vector.reciprocal(rsum[0:64, :], PS[64:128, 7, 0:S]))
                if add:
                    dst = (hT0, hT1)[g // 2][rs, cols]
                    ch.link(tt(on[rs, :], PS[0:64, 7, 0:S], rsum[0:64, :], ALU.mult))
                    tt(dst, dst, on[rs, :], ALU.add).then_inc(s["o_done"], 1)
                else:
                    tt((oT0, oT1)[g // 2][rs, cols], PS[0:64, 7, 0:S], rsum[0:64, :], ALU.mult).then_inc(s["o_done"], 1)

            def attention(s0, add):
                def turn(c, i):
                    step = s0 + 6 * i + c
                    if c + 1 < STEPS:
                        maxima(c + 1, step + 1)
                    if c > 0:
                        normalise(c - 1, step - 1, 2 * i + (c - 1) // G, add)

                maxima(0, s0)
                for c in range(3):
                    turn(c, 0)
                per = 12 if add else 6
                with dve.Fori(0, 3) as i:
                    mark = ch.enter(i, per)
                    for c in range(3, 9):
                        turn(c, i)
                    ch.leave(mark, 3)
                for c in range(21, STEPS):
                    turn(c, 0)
                normalise(STEPS - 1, s0 + STEPS - 1, B - 1, add)

            def batch_norm(n, done, roots):
                for c in range(NCH):
                    cs = slice(CH * c, CH * c + CH)
                    ch.put(nc.vector.bn_stats(stats[:, 0, c, :], hT0[:, cs]))
                    ch.put(nc.vector.bn_stats(stats[0:C1, 1, c, :], hT1[0:C1, cs]))
                ch.wait()
                ch.put(nc.vector.memset(mv[C1:, 1, :], 0.0))
                nc.vector.bn_aggr(mv[:, 0, :], stats[:, 0].rearrange("p c k -> p (c k)")).then_inc(s["bn_var"], 1)
                nc.vector.bn_aggr(mv[0:C1, 1, :], stats[0:C1, 1].rearrange("p c k -> p (c k)")).then_inc(s["bn_var"], 1)
                scale, shift, part = bn_s[:, 0, :], bn_s[:, 1, :], bn_s[:, 2, :]
                dve.wait_ge(s["bn_root"], roots)
                ch.link(nc.vector.reciprocal(part, part))
                ch.link(tt(scale, part, bn_g[:, n, :], ALU.mult))
                ch.link(tt(part, mv[:, :, 0], scale, ALU.mult))
                ch.link(tt(shift, bn_b[:, n, :], part, ALU.subtract))
                ch.link(ts_(hT0[:], hT0[:], bn_s[:, 0, 0:1], bn_s[:, 1, 0:1], ALU.mult, ALU.add))
                ts_(hT1[0:C1, :], hT1[0:C1, :], bn_s[0:C1, 0, 1:2], bn_s[0:C1, 1, 1:2], ALU.mult, ALU.add)\
                    .then_inc(s[done], 1)

            def add_linear(x0, x1, ps, at):
                for c in range(NCH):
                    cs = slice(CH * c, CH * c + CH)
                    dve.wait_ge(s[ps], at + (2 * c + 2))
                    for k, (x, n) in enumerate(((x0, 128), (x1, C1))):
                        yield tt(x[0:n, cs], x[0:n, cs], PS[0:n, 2 * c + k, :], ALU.add)

            def layer_norm(x0, x1, y0, y1, n):
                for c in range(NCH):
                    cs = slice(CH * c, CH * c + CH)
                    dve.wait_ge(s["lnm_ps"], n * NCH + c + 1)
                    tt(y0[:, cs], x0[:, cs], PS[:, c, :], ALU.subtract).then_inc(s["ln_cent"], 1)
                    tt(y1[0:C1, cs], x1[0:C1, cs], PS[0:C1, c, :], ALU.subtract).then_inc(s["ln_cent"], 1)
                for c in range(NCH):
                    cs = slice(CH * c, CH * c + CH)
                    dve.wait_ge(s["ln_root"], n * NCH + c + 1)
                    ch.link(nc.vector.reciprocal(rstd[:, c % 2, :], rstd[:, c % 2, :]))
                    tt(y0[:, cs], y0[:, cs], rstd[:, c % 2, :], ALU.mult).then_inc(s["ln_norm"], 1)
                    tt(y1[0:C1, cs], y1[0:C1, cs], rstd[0:C1, c % 2, :], ALU.mult).then_inc(s["ln_norm"], 1)

            dve.wait_ge(s["weights_in"], WEIGHTS_IN)
            with dve.Fori(0, LAYERS) as l:
                mark = ch.enter(l, LAYER_LINKS)
                attention(l * STEPS, True)
                dve.wait_ge(s["o_done"], l * STEPS + STEPS)
                batch_norm(0, "bn1_done", l * 2 + 1)
                for ins in add_linear(hT0, hT1, "ffn_ps", l * (2 * NCH)):
                    ch.put(ins)
                ch.wait()
                batch_norm(1, "h_ready", l * 2 + 2)
                ch.leave(mark, LAYERS)

            dve.wait_ge(s["h_ready"], LAYERS + 1)
            layer_norm(hT0, hT1, nT0, nT1, 0)
            dd = [PS[:, 3 * (1 - k):3 * (1 - k) + 3, :].rearrange("p b (h m) -> p (b h) m", m=M) for k in range(2)]
            with dve.Fori(0, B) as b:
                mark = ch.enter(b, 6)
                flat = [fmax[:, k].rearrange("p t h -> p (t h)") for k in range(2)]
                sub = [fsub[:, k].rearrange("p t h -> p (t h)") for k in range(2)]

                def wide(v):
                    return v[:, :, None].broadcast_to([128, QT_ * H, M])

                dve.wait_ge(s["rf_diag"], b + 1)
                nc.vector.tensor_copy(fsub[:].rearrange("p k t h -> p (k t h)"), PS[:, 7, 0:2 * QT_ * H])\
                    .then_inc(s["rf_diagev"], 1)
                dve.wait_ge(s["rf_dd"], b * 2 + 1)
                nc.vector.tensor_reduce(flat[1], dd[1], AX, ALU.max).then_inc(s["rf_fmax"], 1)
                dve.wait_ge(s["rf_stT"], b + 1)
                ch.link(nc.vector.tensor_reduce(stab[:], PS[0:H, 7, 0:S], AX, ALU.max))
                ts_(stab_d[:], ident[0:H, 0:H], stab[:, 0:1], None, ALU.mult).then_inc(s["rf_std"], 1)
                dve.wait_ge(s["rf_dd"], b * 2 + 2)
                ch.link(nc.vector.tensor_reduce(flat[0], dd[0], AX, ALU.max))
                ch.link(tt(sub[0], flat[0], sub[0], ALU.add))
                dve.wait_ge(s["rf_stb"], b + 1)
                ch.link(tt(fsub[:, 1], fsub[:, 1], PS[:, 7, 256:256 + H][:, None, :].broadcast_to([128, QT_, H]), ALU.add))
                for k, X in ((1, KP), (0, QP)):
                    tt(X.rearrange("p t h m -> p (t h) m"), dd[k], wide(sub[k]), ALU.subtract).then_inc(s["rf_sub"], 1)
                for n, X in enumerate((KP, QP)):
                    dve.wait_ge(s["rf_exp"], b * 2 + (n + 1))
                    v = X.rearrange("p t h m -> p (t h m)")
                    ts_(v, v, RF_EPS, None, ALU.add).then_inc(s["rf_eps"], 1)
                dve.wait_ge(s["rf_out"], b + 1)
                o = PS[:, 5, 0:2 * 204].rearrange("p (h d) -> p h d", d=HD + 1)
                oi = oinv[:].rearrange("p t h -> p (t h)")
                ch.link(nc.vector.reciprocal(oi, o[:, :, HD]))
                ch.link(tt(ob[:].rearrange("p t (h d) -> p (t h) d", d=HD), o[:, :, 0:HD],
                           oi[:, :, None].broadcast_to([128, QT_ * H, HD]), ALU.mult))
                dve.sem_inc(s["rf_o"], 1)
                dve.wait_ge(s["rf_y"], b + 1)
                for k, (x, n) in enumerate(((hT0, 128), (hT1, C1))):
                    dst = x[0:n, bass.ds(b * S, S)]
                    tt(dst, dst, PS[0:n, 7, S * k:S * k + S], ALU.add).then_inc(s["rf_done"], 1)
                ch.leave(mark, B)

            dve.wait_ge(s["rf_done"], 2 * B + 1)
            layer_norm(hT0, hT1, xT0, xT1, 1)
            dve.wait_ge(s["ln_norm"], 2 * 2 * NCH)
            layer_norm(xT0, xT1, nT0, nT1, 2)
            attention(LAYERS * STEPS, False)
            for ins in add_linear(xT0, xT1, "xp_ps", 0):
                ins.then_inc(s["x2_done"], 1)
            dve.wait_ge(s["x2_done"], 2 * NCH)
            layer_norm(xT0, xT1, nT0, nT1, 3)
            tt(hT0[:], hT0[:], xT0[:], ALU.add).then_inc(s["res_done"], 1)
            tt(hT1[0:C1, :], hT1[0:C1, :], xT1[:], ALU.add).then_inc(s["res_done"], 1)

            def by_token(v):
                return v[:, :, None].broadcast_to([128, NT, E])

            numbers = expert_no[:, None, :].broadcast_to([128, NT, E])
            dve.wait_ge(s["lgT_ps"], 1)
            ch.link(nc.vector.tensor_copy(lg[:].rearrange("p t e -> p (t e)"), PS[:, 4, 0:NT * E]))
            logits = lg[:]
            for n in range(2):
                top, first, pick = gs[:, n, :], gs[:, 3, :], gt[:, 3 + n]
                ch.link(nc.vector.tensor_reduce(top, logits, AX, ALU.max))
                ch.link(tt(gt[:, 0], logits, by_token(top), ALU.is_equal))
                ch.link(stt(gt[:, 1], gt[:, 0], -float(2 * E), numbers, ALU.mult, ALU.add))
                ch.link(nc.vector.tensor_reduce(first, gt[:, 1], AX, ALU.min))
                ch.link(tt(pick, gt[:, 1], by_token(first), ALU.is_equal))
                if n == 0:
                    ch.link(stt(gt[:, 2], pick, -3e38, lg[:], ALU.mult, ALU.add))
                    logits = gt[:, 2]
            tt(gs[:, 2, :], gs[:, 1, :], gs[:, 0, :], ALU.subtract).then_inc(s["gate_arg"], 1)
            dve.wait_ge(s["gate_exp"], 1)
            ch.link(ts_(gs[:, 4, :], gs[:, 2, :], 1.0, None, ALU.add))
            ch.link(nc.vector.reciprocal(gs[:, 4, :], gs[:, 4, :]))
            ch.link(tt(gs[:, 5, :], gs[:, 2, :], gs[:, 4, :], ALU.mult))
            ch.link(tt(gt[:, 0], gt[:, 3], by_token(gs[:, 4, :]), ALU.mult))
            ch.link(tt(gt[:, 1], gt[:, 4], by_token(gs[:, 5, :]), ALU.mult))
            tt(gt[:, 5], gt[:, 0], gt[:, 1], ALU.add).then_inc(s["gates_done"], 1)
            with dve.Fori(0, B) as b:
                dve.wait_ge(s["fin_cp"], b + 1)
                r = rows[:, bass.ds(b * QT_, QT_), :]
                tt(r, r, PS[:, 5:7, 0:D], ALU.add).then_inc(s["fin_ev"], 1)
            dve.wait_ge(s["fin_ev"], B + 1)
            with dve.Fori(0, NCH) as c:
                for e in range(E):
                    for q in range(4):
                        dve.wait_ge(s["down_ps"], c * (4 * E) + (4 * e + q + 9))
                        r = rows[:, bass.ds(c * 4 + q, 1), :]
                        stt(r, PS[:, 4 + q, 0:D], gt[:, 5, bass.ds(c * 4 + q, 1), e], r, ALU.mult, ALU.add)\
                            .then_inc(s["y_done"], 1)


def constants():
    c = {"c_ident": np.eye(128, dtype=np.float32)}
    c["c_head_mask"] = np.repeat(np.eye(J, dtype=np.float32), 32, axis=0)
    ho = np.zeros((128, J), np.float32)
    kones = np.zeros((128, G), np.float32)
    for j in range(J):
        ho[32 * j:32 * j + HD, j] = 0.5
        kones[32 * j + HD, :] = 1
    c["c_head_ones"], c["c_kones"] = ho, kones
    p, i = np.meshgrid(np.arange(S), np.arange(D // 2))
    pe = np.zeros((S, D), dtype=np.float32)
    pe[:, ::2] = np.sin(p / 2500 ** (2 * i / D)).T
    pe[:, 1::2] = np.cos(p / 2500 ** (2 * i / D)).T
    c["c_pos"] = pe
    c["c_expert_no"] = np.tile(np.arange(E, dtype=np.float32), (128, 1))
    return c


def kernel(**inputs):
    import concourse.bacc as bacc
    from concourse.bass_utils import run_bass_kernel_spmd

    nc = bacc.Bacc("TRN2", target_bir_lowering=False, num_devices=1)
    arrays, aps = {}, {}
    given = {n: np.ascontiguousarray(v) for n, v in inputs.items()}
    given["c_projT"] = np.ascontiguousarray(given["L0_attn_proj"].T)
    given.update(constants())
    for name, v in given.items():
        if name == "L0_attn_proj":
            continue
        arrays[f"in_{name}"] = v
        aps[name] = nc.dram_tensor(f"in_{name}", v.shape, mybir.dt.from_np(v.dtype), kind="ExternalInput").ap()
    out = nc.dram_tensor("out_0", (B, S, D), F32, kind="ExternalOutput").ap()
    build(nc, aps, out)
    r = run_bass_kernel_spmd(nc, [arrays], core_ids=[0])
    return r.results[0]["out_0"]
```

```python
from contextlib import ExitStack

import numpy as np

import concourse.bass as bass
from concourse import mybir

F32 = mybir.dt.float32
BF16 = mybir.dt.bfloat16
I32 = mybir.dt.int32
ALU = mybir.AluOpType
ACT = mybir.ActivationFunctionType
AX = mybir.AxisListType.X

B, S, D, V = 8, 256, 192, 8000
T = B * S
H, HD = 12, 16
G, J = 3, 4
DC = D // 3
C1 = D - 128
M = 64
E, HID = 8, 768
HT = HID // 128
NT = T // 128
QT_ = S // 128
CH = 512
NCH = T // CH
TK = 2
TILES = TK * NT + E - 1
UN = 6
TURNS = (TILES - TILES % UN) // UN
ROW = D + 2
LAYERS = 2
LAYER_LINKS = 92
STEPS = B * G
BN_EPS, LN_EPS, RF_EPS = 1e-5, 1e-5, 1e-4


class Chain:

    def __init__(self, eng, sem):
        self.eng, self.sem, self.base, self.k = eng, sem, 0, 0

    def put(self, ins):
        ins.then_inc(self.sem, 1)
        self.k += 1

    def wait(self):
        self.eng.wait_ge(self.sem, self.base + self.k)

    def link(self, ins):
        self.put(ins)
        self.wait()

    def enter(self, i, per):
        saved = self.base, self.k
        self.base, self.k = i * per + self.base + self.k, 0
        return saved, per

    def leave(self, mark, turns):
        (base, k), per = mark
        assert self.k == per, (self.k, per)
        self.base, self.k = base, k + turns * per


def build(nc, a, out):
    with ExitStack() as ctx:
        def sb(name, shape, dt=F32):
            return ctx.enter_context(nc.sbuf_tensor(name, shape, dt))

        def sem(name):
            return ctx.enter_context(nc.semaphore(name))

        PS = ctx.enter_context(nc.psum_tensor("PS", [128, 8, CH], F32))

        ident = sb("ident", [128, 128])
        ident_b = sb("ident_b", [128, 128], BF16)
        half_ones = sb("half_ones", [128, 2, 2, HD])
        head_mask = sb("head_mask", [128, J])
        head_half = sb("head_half", [128, 32])
        pos = sb("pos", [128, QT_, D])
        expert_no = sb("expert_no", [128, E])
        upper = sb("upper", [128, 128])
        ones = sb("ones", [128, 128])
        token_no = sb("token_no", [128, NT], I32)
        marks = sb("marks", [128, NT + TILES])
        mean_w = sb("mean_w", [128, 128])
        ones12 = sb("ones12", [H, 128])

        tok_wq = sb("tok_wq", [128, G, J, 32])
        tok_wk = sb("tok_wk", [128, G, J, 32])
        tok_wv = sb("tok_wv", [C1 + 1, D])
        tok_qb = sb("tok_qb", [128, G])
        tok_kb = sb("tok_kb", [128, G])
        tok_wf0 = sb("tok_wf0", [128, D])
        tok_wf1 = sb("tok_wf1", [C1 + 1, D])
        bn_g = sb("bn_g", [128, 2, 2])
        bn_b = sb("bn_b", [128, 2, 2])
        rf_wq0 = sb("rf_wq0", [128, G, J, 32])
        rf_wq1 = sb("rf_wq1", [C1, G, J, 32])
        rf_wk0 = sb("rf_wk0", [128, G, J, 32])
        rf_wk1 = sb("rf_wk1", [C1, G, J, 32])
        rf_wv0 = sb("rf_wv0", [128, D])
        rf_wv1 = sb("rf_wv1", [C1, D])
        rf_wo0 = sb("rf_wo0", [128, D])
        rf_wo1 = sb("rf_wo1", [C1, D])
        rf_proj = sb("rf_proj", [128, J, M])
        ff_wq0 = sb("ff_wq0", [128, G, J, 32])
        ff_wq1 = sb("ff_wq1", [C1, G, J, 32])
        ff_wk0 = sb("ff_wk0", [128, G, J, 32])
        ff_wk1 = sb("ff_wk1", [C1, G, J, 32])
        ff_wv0 = sb("ff_wv0", [128, D])
        ff_wv1 = sb("ff_wv1", [C1 + 1, D])
        ff_qb = sb("ff_qb", [128, G])
        ff_kb = sb("ff_kb", [128, G])
        ff_wp0 = sb("ff_wp0", [128, D])
        ff_wp1 = sb("ff_wp1", [C1 + 1, D])
        ln_g = sb("ln_g", [128, 2, 2])
        ln_b = sb("ln_b", [128, 2, 2])
        gate0 = sb("gate0", [128, E])
        gate1 = sb("gate1", [C1, E])
        w1_0 = sb("w1_0", [128, E, HID])
        w1_1_all = sb("w1_1_all", [128, E, HID])
        w1_1 = w1_1_all[0:C1]
        w2_s = sb("w2_s", [128, E, HT, D])
        b1_s = sb("b1_s", [128, E, HT])
        b2_s = sb("b2_s", [E, D])

        tok_idx = sb("tok_idx", [128, NT], I32)
        idx_a = sb("idx_a", [128, NT], I32)
        idx_b = sb("idx_b", [128, NT], I32)
        rows = sb("rows", [128, NT, D])
        hT0 = sb("hT0", [128, T])
        hT1 = sb("hT1", [C1 + 1, T])
        nT0 = sb("nT0", [128, T])
        nT1 = sb("nT1", [C1 + 1, T])
        xT0 = sb("xT0", [128, T])
        xT1 = sb("xT1", [C1, T])
        oT0, oT1 = nT0, nT1
        in0 = sb("in0", [128, 2, S])
        in1 = sb("in1", [C1 + 1, 2, S])
        carved = [0]

        def carve(n, dt=F32):
            flat = w2_s[:].rearrange("p e t d -> p (e t d)")[:, carved[0]:carved[0] + n]
            carved[0] += n
            assert carved[0] <= E * HT * D
            return flat if dt == F32 else flat.bitcast(dt)

        QT = carve(2 * S).rearrange("p (k q) -> p k q", k=2)
        KT = carve(2 * S).rearrange("p (k q) -> p k q", k=2)
        QTb = carve(S, BF16).rearrange("p (k q) -> p k q", k=2)
        QM = carve(2 * J * S).rearrange("p (k j q) -> p k j q", k=2, j=J)
        KMb = carve(J * S, BF16).rearrange("p (k j q) -> p k j q", k=2, j=J)
        VA = carve(2 * QT_ * G * J * 32).rearrange("p (k t g j d) -> p k t g j d", k=2, t=QT_, g=G, j=J)
        rmax = carve(QT_ * J * 16, BF16).rearrange("p (t j d) -> p t j d", t=QT_, j=J)
        FW = QT_ * H * M
        early = w1_1_all[:].rearrange("p e n -> p (e n)")
        P = early[:, 0:8 * QT_ * S].rearrange("p (n j t q) -> p n j t q", n=4, j=2, t=QT_)
        KP, QP = (early[:, n * FW:(n + 1) * FW].rearrange("p (t h m) -> p t h m", t=QT_, h=H) for n in range(2))
        QPT = early[:, 2 * FW:3 * FW].rearrange("p (q t n) -> p q t n", t=QT_, n=128)
        QK = early[:, 3 * FW:4 * FW].rearrange("p (g k q) -> p g k q", g=G, k=2)
        rsum = carve(S)
        on = carve(S)
        stats = sb("stats", [128, 2, B, 6])
        mv = sb("mv", [128, 2, 2])
        eps_t = sb("eps_t", [128, 1])
        bn_s = sb("bn_s", [128, 3, 2])
        HB = sb("HB", [128, 2 * HT * CH])
        sq = HB[:, 6 * CH:10 * CH].rearrange("p (k c q) -> p k c q", k=2, q=CH)
        rstd = HB[:, 10 * CH:10 * CH + T // 4].rearrange("p (c q) -> p c q", c=NCH)
        quarter = HB[:, 4 * CH:5 * CH].rearrange("p (q n) -> p q n", q=4)
        SQ = carve(G * 2 * S).rearrange("p (g k q) -> p g k q", g=G, k=2)
        VB = carve(QT_ * D).rearrange("p (t d) -> p t d", t=QT_)
        fmax = sb("fmax", [128, 2, QT_, H])
        fsub = sb("fsub", [128, 2, QT_, H])
        stab = sb("stab", [H, 1])
        stab_d = sb("stab_d", [H, H])
        CTX = carve(2 * H * HD).rearrange("p (n h d) -> p n h d", h=2, d=HD)
        ob = carve(QT_ * D).rearrange("p (t d) -> p t d", t=QT_)
        diagT = HB[0:32 * G, 0:2 * S]
        rden = HB[:, 2 * S:4 * S]
        obT0, obT1 = HB[:, 4 * S:5 * S], HB[0:C1, 5 * S:6 * S]
        CT = HB[:, 6 * S:6 * S + 384]
        lgT, gatesT = HB[0:E, 0:T], xT1[0:E, :]
        gt = sb("gt", [128, 6, NT, E])
        gs = sb("gs", [128, 6, NT])
        def area(t, at, *dims):
            n = int(np.prod(dims))
            names = " ".join(f"d{k}" for k in range(len(dims)))
            return t[:, at:at + n].rearrange(f"p ({names}) -> p {names}", **{f"d{k}": v for k, v in enumerate(dims)})

        XR = area(HB, 0, NT, ROW)
        RUN = NT * ROW
        run = [area(HB, RUN + k * (8 + NT) * E, 8 + NT, E) for k in range(2)]
        lg = area(HB, RUN + 512, NT, E)
        more = area(HB, RUN + 2 * (8 + NT) * E, E, NT)
        told = HB[0:1, RUN + 1024:RUN + 1024 + TILES * E].rearrange("p (n e) -> p n e", e=E)
        erun = sb("erun", [128, 2, 8 + E + 1])
        count = sb("count", [128, E])
        slot = sb("slot", [128, TK, NT], I32)
        tile_f = sb("tile_f", [1, TILES])
        tile_e = sb("tile_e", [1, TILES], I32)
        W1S = [area(xT0, 0, 2, HID), area(HB, RUN, 2, HID)]
        XT = area(xT0, 2 * HID, 2, 2, 128)
        XL = area(HB, RUN + 2 * HID, UN, ROW)
        HD_ = area(nT0, 0, 2, HT, 128)
        YS = area(nT0, 2 * HID, 2, D)
        B1S = sb("B1S", [128, 2, HT])
        slots_d = nc.dram_tensor("slots_d", (TILES * 128, ROW), F32).ap()
        sums_d = nc.dram_tensor("sums_d", (T + 128, D), F32).ap()

        names = """idx_in const_in tok_in weights_in moe_in pad_done out_done
            idx_ready dve_set pool_set pool_turn dve_step emb_sum emb_ps emb_ev h_ready
            in_ready proj_ps v_ps qkv_ev v_ev cast_done smax_ps smax_red mT_ps aug_done st_ps p_ready av_ps o_done
            bn_var bn_root bn1_done ffn_ps lnm_ps ln_cent ln_sq lnv_ps ln_root ln_inv ln_all ln_norm ln_aff
            rf_v rf_vev rf_qk rf_qkev rf_diag rf_dgT_ev rf_dgT rf_diagev rf_dd rf_fmax rf_stT rf_std rf_stb rf_stbev
            rf_sub rf_exp rf_eps rf_ctT rf_ctTev rf_ctx rf_ctxev rf_qpT rf_qpTev rf_out rf_den rf_o rf_y rf_done
            xp_ps x2_done res_done lg_ps lg_ev lgT_ps gate_arg gate_exp gates_done gT_ps gT_ev
            picks_done count_ps slots_done meta_done xr_ps xr_ev scatter_a scatter_b fill_done tile_e_done
            sum_ps sum_ev sums_in w1_in xt_ps xt_ev l1_ps hid_ready y_ps y_scaled y_added y_free""".split()
        s = {n: sem(n) for n in names}
        rows_in = [sem(f"rows_in{b}") for b in range(B)]
        tile_in = [sem(f"tile_in{c}") for c in range(UN)]

        ctx.enter_context(nc.allow_non_contiguous_dma(reason="small vectors laid onto partitions once"))
        block = ctx.enter_context(nc.Block())

        consts = [(ident, a["c_ident"]), (head_mask, a["c_head_mask"]), (head_half, a["c_head_half"]),
                  (pos, a["c_pos"].rearrange("(t p) d -> p t d", p=128)), (expert_no, a["c_expert_no"]),
                  (upper, a["c_upper"]), (ones, a["c_ones"]), (token_no, a["c_token_no"]), (marks, a["c_marks"]),
                  (quarter, a["c_quarter"])]
        pads = []

        def by_head(w):
            return w.rearrange("c (g j d) -> c g j d", g=G, j=J)

        heads = []
        tok_heads = []
        for w, src, lo, n, r0 in ((tok_wq, a["L0_tok_Wq"], 0, DC, 0), (tok_wk, a["L0_tok_Wk"], 0, DC, DC),
                                  (rf_wq0, a["L0_attn_Wq"], 0, 128, 0), (rf_wq1, a["L0_attn_Wq"], 128, C1, 0),
                                  (rf_wk0, a["L0_attn_Wk"], 0, 128, 0), (rf_wk1, a["L0_attn_Wk"], 128, C1, 0)):
            for g in range(G):
                (tok_heads if w in (tok_wq, tok_wk) else heads).append((w[r0:r0 + n, g, :, 0:HD], by_head(src)[lo:lo + n, g]))
        qkv_w = a["L0_ffn_qkv_w"]
        for w, part, lo, n in ((ff_wq0, 0, 0, 128), (ff_wq1, 0, 128, C1), (ff_wk0, 1, 0, 128), (ff_wk1, 1, 128, C1)):
            for g in range(G):
                heads.append((w[0:n, g, :, 0:HD], by_head(qkv_w[:, part * D:(part + 1) * D])[lo:lo + n, g]))

        def bias_cols(t, v):
            return [(t[32 * j:32 * j + HD, :], v.rearrange("(g j d) -> j d g", g=G, j=J)[j]) for j in range(J)]

        qkv_b = a["L0_ffn_qkv_b"]
        tok_heads += bias_cols(tok_qb, a["L0_tok_bq"]) + bias_cols(tok_kb, a["L0_tok_bk"])
        heads += bias_cols(ff_qb, qkv_b[0:D]) + bias_cols(ff_kb, qkv_b[D:2 * D])
        heads += [(rf_proj[32 * j:32 * j + HD, j, :], a["c_projT"]) for j in range(J)]

        def row(v):
            return v.rearrange("(a d) -> a d", a=1)

        def cols(t, k, v):
            return [(t[:, k, 0:1], v[0:128].rearrange("(p a) -> p a", a=1)),
                    (t[0:C1, k, 1:2], v[128:D].rearrange("(p a) -> p a", a=1))]

        tok_plain = [(tok_wv[0:C1, :], a["L0_tok_Wv"]), (tok_wv[C1:, :], row(a["L0_tok_bv"])),
                 (tok_wf0[:], a["L0_tok_Wf"][0:128, :]), (tok_wf1[0:C1, :], a["L0_tok_Wf"][128:D, :]),
                 (tok_wf1[C1:, :], row(a["L0_tok_bf"]))]
        plain = [(rf_wv0[:], a["L0_attn_Wv"][0:128, :]), (rf_wv1[:], a["L0_attn_Wv"][128:D, :]),
                 (rf_wo0[:], a["L0_attn_Wo"][0:128, :]), (rf_wo1[:], a["L0_attn_Wo"][128:D, :]),
                 (ff_wv0[:], qkv_w[0:128, 2 * D:]), (ff_wv1[0:C1, :], qkv_w[128:D, 2 * D:]),
                 (ff_wv1[C1:, :], row(qkv_b[2 * D:])),
                 (ff_wp0[:], a["L0_ffn_proj_w"][0:128, :]), (ff_wp1[0:C1, :], a["L0_ffn_proj_w"][128:D, :]),
                 (ff_wp1[C1:, :], row(a["L0_ffn_proj_b"])),
                 (gate0[:], a["L0_ffn_gate_w"][0:128, :]), (gate1[:], a["L0_ffn_gate_w"][128:D, :])]
        tok_plain += cols(bn_g, 0, a["L0_tok_g1"]) + cols(bn_b, 0, a["L0_tok_b1"])
        tok_plain += cols(bn_g, 1, a["L0_tok_g2"]) + cols(bn_b, 1, a["L0_tok_b2"])
        plain += cols(ln_g, 0, a["L0_ffn_ln1_g"]) + cols(ln_b, 0, a["L0_ffn_ln1_b"])
        plain += cols(ln_g, 1, a["L0_ffn_ln2_g"]) + cols(ln_b, 1, a["L0_ffn_ln2_b"])
        moe = [(w1_0[:], a["L0_ffn_w1"][:, 0:128, :].rearrange("e c n -> c e n")),
               (b1_s[:], a["L0_ffn_b1"].rearrange("e (t p) -> p e t", p=128)),
               (b2_s[:], a["L0_ffn_b2"])]
        late = [(w1_1, a["L0_ffn_w1"][:, 128:D, :].rearrange("e c n -> c e n"))]
        late += [(w2_s[:, e], a["L0_ffn_w2"][e].rearrange("(t p) d -> p t d", p=128)) for e in range(E)]
        zeroed = [tok_wq, tok_wk, tok_qb, rf_wq0, rf_wq1, rf_wk0, rf_wk1, ff_wq0, ff_wq1, ff_wk0, ff_wk1, rf_proj, ff_qb]
        TOK_ZEROED = 3
        DVE_SETS = len(zeroed) + 2
        MEMSETS = 12
        TOK_IN = 16 * (len(tok_plain) + len(tok_heads))
        WEIGHTS_IN = 16 * (len(plain) + len(heads))

        @block.sync
        def _(sp):
            sp.dma_start(tok_idx[:], a["x"].rearrange("b (t p) -> p (b t)", p=128)).then_inc(s["idx_in"], 16)
            for dst, src in consts:
                sp.dma_start(dst[:], src).then_inc(s["const_in"], 16)
            sp.dma_start(tok_kb[:], a["c_kones"]).then_inc(s["pad_done"], 16)
            sp.dma_start(ff_kb[:], a["c_kones"]).then_inc(s["pad_done"], 16)
            for dst, src in tok_plain:
                sp.dma_start(dst, src).then_inc(s["tok_in"], 16)
            sp.wait_ge(s["pad_done"], 32)
            sp.wait_ge(s["dve_set"], TOK_ZEROED)
            for dst, src in tok_heads:
                sp.dma_start(dst, src).then_inc(s["tok_in"], 16)
            for dst, src in plain:
                sp.dma_start(dst, src).then_inc(s["weights_in"], 16)
            sp.wait_ge(s["dve_set"], len(zeroed))
            for dst, src in heads:
                sp.dma_start(dst, src).then_inc(s["weights_in"], 16)
            for dst, src in moe:
                sp.dma_start(dst, src).then_inc(s["moe_in"], 16)
            sp.dma_start(slots_d.rearrange("(n p) c -> p n c", p=128),
                         a["c_empty"][:, None, :].broadcast_to([128, TILES, ROW])).then_inc(s["fill_done"], 16)
            sp.dma_start(sums_d[T:], a["c_empty"][:, 0:D]).then_inc(s["fill_done"], 16)
            sp.wait_ge(s["o_done"], (LAYERS + 1) * STEPS)
            for dst, src in late:
                sp.dma_start(dst, src).then_inc(s["moe_in"], 16)
            sp.wait_ge(s["sum_ev"], NT)
            sp.dma_start(sums_d[0:T].rearrange("(t p) d -> p t d", p=128), rows[:]).then_inc(s["sums_in"], 16)
            sp.wait_ge(s["fill_done"], 32)
            sp.wait_ge(s["scatter_a"], 16 * NT)
            sp.wait_ge(s["scatter_b"], 16 * NT)

            def load(n, c):
                sp.dma_start(XL[:, c, :], slots_d[bass.ds(n * 128, 128), :]).then_inc(tile_in[c], 16)

            for c in range(UN):
                load(c, c)
            with sp.Fori(0, TURNS - 1) as i:
                for c in range(UN):
                    sp.wait_ge(s["y_free"], i * UN + (c + 3))
                    load(i * UN + (c + UN), c)
            for n in range(UN * TURNS, TILES):
                sp.wait_ge(s["y_free"], n - UN + 3)
                load(n, n % UN)
            sp.wait_ge(s["y_added"], 16 * TILES)
            sp.dma_start(out.rearrange("b s d -> (b s) d"), sums_d[0:T]).then_inc(s["out_done"], 16)
            sp.wait_ge(s["out_done"], 16)

        @block.gpsimd
        def _(pool):
            pool.wait_ge(s["idx_ready"], 1)
            for t in range(NT):
                pool.indirect_dma_start(rows[:, t, :], None, a["L0_tok_emb"],
                                        bass.IndirectOffsetOnAxis(ap=idx_a[:, t:t + 1], axis=0)).then_inc(rows_in[t // QT_], 16)
            k = 0
            for t, v in ((mean_w[:], 1.0 / D), (ones12[:], 1.0), (eps_t[:], BN_EPS), (VA, 0.0), (QM, 0.0), (rmax, 0.0),
                         (half_ones[:], 0.0), (half_ones[:, 0, 0], 1.0), (half_ones[:, 1, 1], 1.0), (CTX, 0.0),
                         (bn_g[64:, :, 1:2], 0.0), (bn_b[64:, :, 1:2], 0.0)):
                if k:
                    pool.wait_ge(s["pool_set"], k)
                nc.gpsimd.memset(t, v).then_inc(s["pool_set"], 1)
                k += 1
            assert k == MEMSETS
            pool.wait_ge(s["pool_set"], MEMSETS)

            def then(value, name):
                pool.wait_ge(s[name], value)
                pool.sem_inc(s["pool_turn"], 1)

            def copy_in(src0, src1, b, slot):
                cols = bass.ds(b * S, S)
                nc.gpsimd.tensor_copy(in0[:, slot, :], src0[:, cols]).then_inc(s["in_ready"], 1)
                nc.gpsimd.tensor_copy(in1[:, slot, :], src1[:, cols]).then_inc(s["in_ready"], 1)

            def attention(src0, src1, s0):
                def turn(c, i):
                    then(2 * s0 + 12 * i + (2 * c + 2), "qkv_ev")
                    nc.gpsimd.tensor_copy(QTb[:, c % 2, :], QT[:, c % 2, :]).then_inc(s["cast_done"], 1)
                    nc.gpsimd.tensor_tensor(KMb[:, c % 2], KT[:, c % 2, :][:, None, :].broadcast_to([128, J, S]),
                                            head_mask[:, :, None].broadcast_to([128, J, S]), ALU.mult)\
                      .then_inc(s["cast_done"], 1)
                    if c % G == 0 and c // G + 1 < B:
                        copy_in(src0, src1, 2 * i + c // G + 1, (c // G + 1) % 2)

                copy_in(src0, src1, 0, 0)
                for c in range(3):
                    turn(c, 0)
                with pool.Fori(0, 3) as i:
                    for c in range(3, 9):
                        turn(c, i)
                for c in range(21, STEPS):
                    turn(c, 0)

            with pool.Fori(0, LAYERS) as l:
                then(l + 1, "h_ready")
                attention(hT0, hT1, l * STEPS)
            pool.wait_ge(s["ln_norm"], 2 * NCH)
            copy_in(nT0, nT1, 0, 0)
            with pool.Fori(0, B - 1) as b:
                then(b + 1, "rf_v")
                copy_in(nT0, nT1, b + 1, 0)
            pool.wait_ge(s["ln_aff"], 2 * NCH)
            attention(nT0, nT1, LAYERS * STEPS)
            pool.wait_ge(s["fill_done"], 32)
            pool.wait_ge(s["slots_done"], 1)
            for k in range(TK):
                pool.wait_ge(s["meta_done"], k + 1)
                for t in range(NT):
                    if k == 0:
                        pool.wait_ge(s["xr_ev"], t + 1)
                    pool.indirect_dma_start(slots_d, bass.IndirectOffsetOnAxis(ap=slot[:, k, t:t + 1], axis=0),
                                            XR[:, t, :], None).then_inc(s["scatter_b" if k else "scatter_a"], 16)
            pool.wait_ge(s["sums_in"], 16)

            def add_tile(n, c):
                then(n + 3, "y_scaled")
                pool.indirect_dma_start(sums_d, bass.IndirectOffsetOnAxis(ap=XL[:, c, D:D + 1].bitcast(I32), axis=0),
                                        YS[:, c % 2, :], None, compute_op=ALU.add).then_inc(s["y_added"], 16)
                pool.wait_ge(s["y_added"], n * 16 + 16)
                pool.sem_inc(s["y_free"], 1)

            pool.sem_inc(s["y_free"], 2)
            with pool.Fori(0, TURNS) as i:
                for c in range(UN):
                    add_tile(i * UN + c, c)
            for n in range(UN * TURNS, TILES):
                add_tile(n, n % UN)

        @block.tensor
        def _(pe):
            pe.sem_inc(s["y_ps"], 2)
            pe.wait_ge(s["const_in"], 16 * len(consts))
            for b in range(B):
                pe.wait_ge(s["emb_sum"], b + 1)
                if b >= 4:
                    pe.wait_ge(s["emb_ev"], 2 * (b - 3))
                for t in range(QT_):
                    pe.transpose(PS[:, 2 * (b % 4), 128 * t:128 * t + 128], rows[:, QT_ * b + t, 0:128], ident[:])
                    last = pe.transpose(PS[0:C1, 2 * (b % 4) + 1, 128 * t:128 * t + 128], rows[:, QT_ * b + t, 128:D],
                                        ident[:])
                last.then_inc(s["emb_ps"], 1)

            def proj(c, step, wq, wk, batch2):
                g, pb = c % G, (c // G) % 2
                if c % G == 0:
                    pe.wait_ge(s["in_ready"], batch2)
                if c > 0:
                    pe.wait_ge(s["qkv_ev"], 2 * step)
                ins = (in0[:, pb, :], in1[:, pb, :])
                for w, lo in ((wq, 0), (wk, S)):
                    for n, (wt, ch) in enumerate(w):
                        last = pe.matmul(PS[:, 6, lo:lo + S], wt[:, g].rearrange("c j d -> c (j d)"),
                                  ins[ch][0:wt.shape[0]], start=n == 0, stop=n == len(w) - 1)
                last.then_inc(s["proj_ps"], 1)

            def proj_v(c, step, wv):
                pb = (c // G) % 2
                ins = (in0[:, pb, :], in1[:, pb, :])
                if c > 0:
                    pe.wait_ge(s["smax_red"], 4 * step)
                for t in range(QT_):
                    for n, (wt, ch) in enumerate(wv):
                        last = pe.matmul(PS[:, 5, D * t:D * t + D], ins[ch][0:wt.shape[0], 128 * t:128 * t + 128],
                                         wt[:], start=n == 0, stop=n == len(wv) - 1)
                last.then_inc(s["v_ps"], 1)

            def smax(c, step, batch, half):
                p = c % 2
                if half == 0:
                    pe.wait_ge(s["cast_done"], 2 * (step + 1))
                for j in (2 * half, 2 * half + 1):
                    if j == 0 and c > 0:
                        pe.wait_ge(s["aug_done"], 4 * step)
                    if j == 1 and c % G == 0:
                        pe.wait_ge(s["v_ev"], batch)
                    if j >= 2:
                        pe.wait_ge(s["smax_red"], 4 * step + j - 1)
                    for t in range(QT_):
                        last = pe.matmul(PS[:, 4 + j % 2, S * t:S * t + S],
                                         QTb[:, p, 128 * t:128 * t + 128], KMb[:, p, j, :], start=True, stop=True)
                    last.then_inc(s["smax_ps"], 1)

            def turn_max(c, step):
                pe.wait_ge(s["smax_red"], 4 * (step + 1))
                for t in range(QT_):
                    last = pe.transpose(PS[:, 4, :].bitcast(BF16)[:, 128 * t:128 * t + 128],
                                        rmax[:, t].rearrange("p j d -> p (j d)"), ident_b[:])
                last.then_inc(s["mT_ps"], 1)

            def scores(c, step):
                p = c % 2
                for h in range(2):
                    if c > 0:
                        pe.wait_ge(s["p_ready"], 2 * step + h - 1)
                    for t in range(QT_):
                        for j in (2 * h, 2 * h + 1):
                            if t == 0:
                                pe.wait_ge(s["aug_done"], 4 * step + (j + 1))
                            last = pe.matmul(PS[:, j, S * t:S * t + S], KT[:, p, 128 * t:128 * t + 128],
                                             QM[:, p, j, :], start=True, stop=True)
                    last.then_inc(s["st_ps"], 1)

            def weigh(c, step, batch, half):
                if half == 0:
                    if c > 0:
                        pe.wait_ge(s["o_done"], step)
                    pe.wait_ge(s["p_ready"], 2 * (step + 1))
                    pe.wait_ge(s["v_ev"], batch)
                for n in range(QT_ * half, QT_ * half + QT_):
                    hh, t = n // QT_, n % QT_
                    for lo in (0, 64):
                        for pr in range(2):
                            j = 2 * pr + hh
                            w = half_ones[:, hh].rearrange("p h d -> p (h d)") if lo else VA[:, (c // G) % 2, t, c % G, j, :]
                            last = pe.matmul(PS[lo + 32 * pr:lo + 32 * pr + 32, 7, 0:S], w,
                                             P[:, 2 * (c % 2) + j // 2, j % 2, t, :], start=n == 0, stop=n == 2 * QT_ - 1,
                                             skip_group_check=True)
                if half:
                    last.then_inc(s["av_ps"], 1)

            def attention(s0, b0, v0, wq, wk, wv):
                def pj(c, i):
                    proj(c, s0 + 6 * i + c, wq, wk, 2 * (b0 + 2 * i + c // G + 1))

                def turn(c, i):
                    step = s0 + 6 * i + c
                    n1, w1 = (c + 1, step + 1, v0 + 2 * i + ((c + 1) // G + 1)), (c - 1, step - 1, v0 + 2 * i + ((c - 1) // G + 1))
                    scores(c, step)
                    if c + 1 < STEPS:
                        smax(*n1, 0)
                    if c + 2 < STEPS:
                        pj(c + 2, i)
                    if c + 1 < STEPS:
                        smax(*n1, 1)
                    if c > 0:
                        weigh(*w1, 0)
                    if c + 1 < STEPS:
                        turn_max(c + 1, step + 1)
                    if c > 0:
                        weigh(*w1, 1)
                    if c + 2 < STEPS and (c + 2) % G == 0:
                        proj_v(c + 2, step + 2, wv)

                pj(0, 0)
                proj_v(0, s0, wv)
                pj(1, 0)
                smax(0, s0, v0 + 1, 0)
                smax(0, s0, v0 + 1, 1)
                turn_max(0, s0)
                for c in range(3):
                    turn(c, 0)
                with pe.Fori(0, 3) as i:
                    for c in range(3, 9):
                        turn(c, i)
                for c in range(21, STEPS):
                    turn(c, 0)
                weigh(STEPS - 1, s0 + STEPS - 1, v0 + B, 0)
                weigh(STEPS - 1, s0 + STEPS - 1, v0 + B, 1)

            def linear(w0, w1, x0, x1, done):
                for c in range(NCH):
                    cs = slice(CH * c, CH * c + CH)
                    for k, (lo, n) in enumerate(((0, 128), (128, C1))):
                        pe.matmul(PS[0:n, 2 * c + k, :], w0[:, lo:lo + n], x0[:, cs], start=True, stop=False)
                        pe.matmul(PS[0:n, 2 * c + k, :], w1[:, lo:lo + n], x1[:, cs], start=False, stop=True)\
                          .then_inc(s[done], 1)

            def layer_norm(x0, x1, n, src_ready=None):
                def spread(c):
                    pe.wait_ge(s["ln_inv"], n * NCH + c + 1)
                    for q in range(4):
                        last = pe.matmul(PS[:, 4 + c, 128 * q:128 * q + 128], quarter[:, q], rstd[:, c, :], start=True, stop=True)
                    last.then_inc(s["ln_all"], 1)

                def means(c):
                    cs = slice(CH * c, CH * c + CH)
                    if src_ready:
                        name, at, per = src_ready
                        pe.wait_ge(s[name], at + per * c)
                    pe.matmul(PS[:, c, :], mean_w[:], x0[:, cs], start=True, stop=False)
                    pe.matmul(PS[:, c, :], mean_w[0:C1, :], x1[0:C1, cs], start=False, stop=True).then_inc(s["lnm_ps"], 1)

                def variances(c):
                    pe.wait_ge(s["ln_sq"], 2 * (n * NCH + c + 1))
                    for k, rows_k in enumerate((128, C1)):
                        for q in range(4):
                            last = pe.matmul(PS[32 * q:32 * q + 32, 4 + c, 0:128], mean_w[0:rows_k, 0:32],
                                             sq[0:rows_k, c % 2, k, 128 * q:128 * q + 128], start=k == 0, stop=k == 1,
                                             skip_group_check=True)
                    last.then_inc(s["lnv_ps"], 1)

                means(0)
                means(1)
                means(2)
                variances(0)
                means(3)
                variances(1)
                spread(0)
                variances(2)
                spread(1)
                variances(3)
                spread(2)
                spread(3)

            pe.wait_ge(s["tok_in"], TOK_IN)
            pe.wait_ge(s["dve_set"], DVE_SETS)
            pe.wait_ge(s["pool_set"], MEMSETS)
            with pe.Fori(0, LAYERS) as l:
                attention(l * STEPS, l * B, l * B, [(tok_wq, 0)], [(tok_wk, 0)], [(tok_wv, 1)])
                pe.wait_ge(s["bn1_done"], l + 1)
                linear(tok_wf0, tok_wf1, hT0, hT1, "ffn_ps")

            pe.wait_ge(s["weights_in"], WEIGHTS_IN)
            layer_norm(hT0, hT1, 0, ("h_ready", LAYERS + 1, 0))
            IN0 = 2 * B * LAYERS
            PAIRS = H // 2

            def rf_proj_qk(b, g, bank):
                for k, (wa, wb) in enumerate(((rf_wq0, rf_wq1), (rf_wk0, rf_wk1))):
                    pe.matmul(PS[:, bank, S * k:S * k + S], wa[:, g].rearrange("c j d -> c (j d)"), in0[:, 0, :],
                              start=True, stop=False)
                    last = pe.matmul(PS[:, bank, S * k:S * k + S], wb[:, g].rearrange("c j d -> c (j d)"),
                                     in1[0:C1, 0, :], start=False, stop=True)
                last.then_inc(s["rf_qk"], 1)

            def rf_values():
                for t in range(QT_):
                    ts = slice(128 * t, 128 * t + 128)
                    pe.matmul(PS[:, 7, D * t:D * t + D], in0[:, 0, ts], rf_wv0[:], start=True, stop=False)
                    last = pe.matmul(PS[:, 7, D * t:D * t + D], in1[0:C1, 0, ts], rf_wv1[:], start=False, stop=True)
                last.then_inc(s["rf_v"], 1)

            def rf_squares():
                for g in range(G):
                    last = pe.matmul(PS[32 * g:32 * g + 32, 6, :], head_half[:], SQ[:, g].rearrange("p k q -> p (k q)"),
                                     start=True, stop=True, skip_group_check=True)
                last.then_inc(s["rf_diag"], 1)

            def rf_turn_squares(b):
                pe.wait_ge(s["rf_dgT_ev"], b + 1)
                for n in range(2 * QT_):
                    last = pe.transpose(PS[:, 4, 96 * n:96 * n + 96], diagT[:, 128 * n:128 * n + 128], ident[0:96, 0:96])
                last.then_inc(s["rf_dgT"], 1)

            def rf_features(k):
                for t in range(QT_):
                    for g in range(G):
                        blk = G * t + g
                        last = pe.matmul(PS[:, 3 * (1 - k) + blk // 2, S * (blk % 2):S * (blk % 2) + S],
                                         QK[:, g, k, 128 * t:128 * t + 128], rf_proj[:].rearrange("p j m -> p (j m)"),
                                         start=True, stop=True)
                last.then_inc(s["rf_dd"], 1)

            def rf_turn(b, more):
                pe.wait_ge(s["rf_fmax"], b + 1)
                for t in range(QT_):
                    last = pe.transpose(PS[0:H, 6, 128 * t:128 * t + 128], fmax[:, 1, t, :], ident[:])
                last.then_inc(s["rf_stT"], 1)
                pe.wait_ge(s["rf_done"], b * 2 + 1)
                if more:
                    pe.wait_ge(s["in_ready"], b * 2 + IN0 + 4)
                    rf_proj_qk(b, 0, 7)
                pe.wait_ge(s["rf_std"], b + 1)
                pe.matmul(PS[:, 6, 256:256 + H], ones12[:], stab_d[:], start=True, stop=True).then_inc(s["rf_stb"], 1)
                pe.wait_ge(s["rf_stbev"], b + 1)
                if more:
                    rf_proj_qk(b, 1, 6)
                    pe.wait_ge(s["rf_qkev"], b * 6 + 8)
                    rf_proj_qk(b, 2, 7)
                    pe.wait_ge(s["rf_qkev"], b * 6 + 10)
                pe.wait_ge(s["rf_vev"], b + 1)
                pe.wait_ge(s["rf_eps"], b * 2 + 1)
                for blk in range(2 * PAIRS // 4):
                    for t, k in [(t, k) for t in range(QT_) for k in range(4)]:
                        n, p, r = 4 * blk + k, (4 * blk + k) % PAIRS, 32 * k
                        last = pe.matmul(PS[r:r + 32, 6, 128 * blk:128 * blk + 128],
                                         VB[:, t, 32 * p:32 * p + 32] if n < PAIRS else ones[:, 0:32],
                                         KP[:, t, 2 * p:2 * p + 2, :].rearrange("p h m -> p (h m)"),
                                         start=t == 0, stop=t == QT_ - 1, skip_group_check=True)
                last.then_inc(s["rf_ctT"], 1)
                if more:
                    pe.wait_ge(s["rf_qkev"], b * 6 + 12)
                    rf_values()
                pe.wait_ge(s["rf_eps"], b * 2 + 2)
                for g in range(G):
                    for n in range(4):
                        p, t = 2 * g + n // 2, n % 2
                        last = pe.transpose(PS[:, g, 128 * n:128 * n + 128],
                                            QP[:, t, 2 * p:2 * p + 2, :].rearrange("p h m -> p (h m)"), ident[:])
                    last.then_inc(s["rf_qpT"], 1)
                pe.wait_ge(s["rf_ctTev"], b + 1)
                if more:
                    rf_squares()
                for n in range(3):
                    last = pe.transpose(PS[:, 3, 128 * n:128 * n + 128], CT[:, 128 * n:128 * n + 128], ident[:])
                last.then_inc(s["rf_ctx"], 1)
                if more:
                    rf_turn_squares(b + 1)
                    pe.wait_ge(s["rf_vev"], b + 2)
                pe.wait_ge(s["rf_ctxev"], b * 2 + 2)
                pe.wait_ge(s["rf_qpTev"], b * 3 + 3)
                for n in range(2 * PAIRS):
                    p, item = n % PAIRS, (n + PAIRS) % (2 * PAIRS)
                    last = pe.matmul(PS[32 * (p % 4):32 * (p % 4) + 32, 5 if n < PAIRS else 7, S * (p // 4):S * (p // 4) + S],
                                     CTX[:, item].rearrange("p h d -> p (h d)"), QPT[:, p].rearrange("p t n -> p (t n)"),
                                     start=True, stop=True, skip_group_check=True)
                last.then_inc(s["rf_out"], 1)
                if more:
                    rf_features(1)
                    pe.wait_ge(s["rf_diagev"], b + 2)
                    pe.wait_ge(s["rf_den"], b * 2 + 2)
                    rf_features(0)
                pe.wait_ge(s["rf_o"], b * 2 + 2)
                for k, (lo, n) in enumerate(((0, 128), (128, C1))):
                    pe.matmul(PS[0:n, 7, S * k:S * k + S], rf_wo0[:, lo:lo + n], obT0[:], start=True, stop=False)
                    last = pe.matmul(PS[0:n, 7, S * k:S * k + S], rf_wo1[:, lo:lo + n], obT1[:], start=False, stop=True)
                last.then_inc(s["rf_y"], 1)

            pe.wait_ge(s["in_ready"], IN0 + 2)
            for g, bank in enumerate((7, 6, 5)):
                rf_proj_qk(0, g, bank)
            pe.wait_ge(s["rf_qkev"], 6)
            rf_values()
            rf_squares()
            rf_turn_squares(0)
            rf_features(1)
            pe.wait_ge(s["rf_diagev"], 1)
            rf_features(0)
            with pe.Fori(0, B - 1) as b:
                rf_turn(b, True)
            rf_turn(B - 1, False)

            pe.wait_ge(s["rf_done"], 2 * B + 1)
            layer_norm(hT0, hT1, 1)
            layer_norm(xT0, xT1, 2, ("ln_norm", 2 * NCH + 2, 2))
            pe.wait_ge(s["ln_aff"], 2 * NCH)
            attention(LAYERS * STEPS, B * LAYERS + B, B * LAYERS, [(ff_wq0, 0), (ff_wq1, 1)], [(ff_wk0, 0), (ff_wk1, 1)],
                      [(ff_wv0, 0), (ff_wv1, 1)])
            pe.wait_ge(s["o_done"], (LAYERS + 1) * STEPS)
            linear(ff_wp0, ff_wp1, oT0, oT1, "xp_ps")
            layer_norm(xT0, xT1, 3, ("x2_done", 2, 2))
            pe.wait_ge(s["moe_in"], 16 * (len(moe) + len(late)))
            pe.wait_ge(s["ln_aff"], 4 * NCH)
            for c in range(NCH):
                cs = slice(CH * c, CH * c + CH)
                pe.matmul(PS[0:E, c, :], gate0[:], nT0[:, cs], start=True, stop=False)
                pe.matmul(PS[0:E, c, :], gate1[:], nT1[0:C1, cs], start=False, stop=True).then_inc(s["lg_ps"], 1)
            pe.wait_ge(s["lg_ev"], NCH)
            for t in range(NT):
                last = pe.transpose(PS[:, 4, E * t:E * t + E], lgT[:, 128 * t:128 * t + 128], ident[0:E, 0:E])
            last.then_inc(s["lgT_ps"], 1)
            def turn_x(t):
                if t >= 2:
                    pe.wait_ge(s["xr_ev"], t - 1)
                pe.transpose(PS[:, 5 + t % 2, 0:128], nT0[:, 128 * t:128 * t + 128], ident[:])
                pe.transpose(PS[:, 5 + t % 2, 128:D], nT1[0:C1, 128 * t:128 * t + 128], ident[0:C1, 0:C1])\
                  .then_inc(s["xr_ps"], 1)

            for t in range(NT // 2):
                turn_x(t)
            pe.wait_ge(s["picks_done"], 1)
            picks = gt[:, 2].rearrange("p t e -> p (t e)")
            pe.matmul(PS[:, 7, 0:NT * E], upper[:], picks, start=True, stop=True)
            pe.matmul(PS[:, 7, NT * E:2 * NT * E], ones[:], picks, start=True, stop=True).then_inc(s["count_ps"], 1)
            for t in range(NT // 2, NT):
                turn_x(t)
            pe.wait_ge(s["gates_done"], 1)
            for t in range(NT):
                last = pe.transpose(PS[0:E, t // 4, 128 * (t % 4):128 * (t % 4) + 128], gt[:, 5, t, :], ident[:])
            last.then_inc(s["gT_ps"], 1)
            pe.wait_ge(s["gT_ev"], 1)
            pe.wait_ge(s["xr_ev"], NT)
            pe.wait_ge(s["res_done"], 2)
            for t in range(NT):
                ts = slice(128 * t, 128 * t + 128)
                if t >= 2:
                    pe.wait_ge(s["sum_ev"], t - 1)
                o = PS[:, 5 + t % 2, 0:D]
                pe.matmul(o, gatesT[:, ts], b2_s[:], start=True, stop=False, skip_group_check=True)
                pe.matmul(o[:, 0:128], hT0[:, ts], ident[:], start=False, stop=False, skip_group_check=True)
                pe.matmul(o[:, 128:D], hT1[0:C1, ts], ident[0:C1, 0:C1], start=False, stop=True, skip_group_check=True)\
                  .then_inc(s["sum_ps"], 1)

            def turn_tile(n, c, i):
                pe.wait_ge(tile_in[c % UN], i * 16 + 16 * (c // UN + 1))
                pe.wait_ge(s["xt_ev"], n * 2 + 2)
                x = XL[:, c % UN, :]
                pe.transpose(PS[:, 4 + c % 2, 0:128], x[:, 0:128], ident[:])
                pe.transpose(PS[0:C1, 4 + c % 2, 128:256], x[:, 128:D], ident[:]).then_inc(s["xt_ps"], 1)

            def up(n, c):
                pe.wait_ge(s["w1_in"], n * 3 + 3)
                pe.wait_ge(s["xt_ev"], n * 2 + 6)
                pe.wait_ge(s["hid_ready"], n * HT + HT)
                for m in range(HT):
                    o = PS[:, 2 * (c % 2) + m // 3, 128 * (m % 3):128 * (m % 3) + 128]
                    w = W1S[c % 2]
                    pe.matmul(o, w[:, 0, 128 * m:128 * m + 128], XT[:, c % 2, 0], start=True, stop=False)
                    last = pe.matmul(o, w[0:C1, 1, 128 * m:128 * m + 128], XT[0:C1, c % 2, 1], start=False, stop=True)
                    if m % 3 == 2:
                        last.then_inc(s["l1_ps"], 1)

            def down(n, c):
                e = pe.value_load(tile_e[0:1, bass.ds(n, 1)], min_val=0, max_val=E - 1)
                pe.wait_ge(s["hid_ready"], n * HT + 3 * HT)
                pe.wait_ge(s["y_scaled"], n + 1)
                for m in range(HT):
                    last = pe.matmul(PS[:, 6 + c % 2, 0:D], HD_[:, c % 2, m], w2_s[:, bass.ds(e, 1), m, :],
                                     start=m == 0, stop=m == HT - 1)
                last.then_inc(s["y_ps"], 1)

            pe.wait_ge(s["tile_e_done"], 1)
            pe.wait_ge(s["sum_ev"], NT)
            turn_tile(0, 0, 0)
            up(0, 0)
            turn_tile(1, 1, 0)

            def step(n, c, i):
                if not (isinstance(n, int) and n + 1 >= TILES):
                    up(n + 1, c + 1)
                if not (isinstance(n, int) and n + 2 >= TILES):
                    turn_tile(n + 2, c + 2, i)
                down(n, c)

            with pe.Fori(0, TURNS) as i:
                for c in range(UN):
                    step(i * UN + c, c, i)
            for n in range(UN * TURNS, TILES):
                step(n, n % UN, TURNS)

        @block.scalar
        def _(act):
            act.sem_inc(s["hid_ready"], 2 * HT)
            act.sem_inc(s["xt_ev"], 4)
            act.sem_inc(s["y_scaled"], 2)
            act.wait_ge(s["dve_set"], DVE_SETS)
            for b in range(B):
                act.wait_ge(s["emb_ps"], b + 1)
                nc.scalar.copy(hT0[:, S * b:S * b + S], PS[:, 2 * (b % 4), 0:S]).then_inc(s["emb_ev"], 1)
                nc.scalar.copy(hT1[0:C1, S * b:S * b + S], PS[0:C1, 2 * (b % 4) + 1, 0:S]).then_inc(s["emb_ev"], 1)

            def exps(c, step, scale):
                for h in range(2):
                    act.wait_ge(s["st_ps"], 2 * step + (h + 1))
                    nc.scalar.activation(P[:, 2 * (c % 2) + h].rearrange("p j t q -> p (j t q)"),
                                         PS[:, 2 * h:2 * h + 2, :].rearrange("p b q -> p (b q)"), ACT.Exp,
                                         scale=scale).then_inc(s["p_ready"], 1)

            def qkv(c, step, batch, func, qb, kb):
                g = c % G
                act.wait_ge(s["proj_ps"], step + 1)
                nc.scalar.activation(QT[:, c % 2, :], PS[:, 6, 0:S], func, bias=qb[:, g:g + 1]).then_inc(s["qkv_ev"], 1)
                nc.scalar.activation(KT[:, c % 2, :], PS[:, 6, S:2 * S], func, bias=kb[:, g:g + 1]).then_inc(s["qkv_ev"], 1)
                if c % G == 0:
                    act.wait_ge(s["v_ps"], batch)
                    v = VA[:, (c // G) % 2].rearrange("p t g j d -> p (t g j d)")
                    nc.scalar.activation(bass.AP(tensor=v.tensor, offset=v.offset, ap=[v.ap[0], [64, QT_ * H // 2], [48, 2], [1, HD]]),
                                         PS[:, 5, 0:QT_ * D].rearrange("p (n h d) -> p n h d", h=2, d=HD), func)\
                      .then_inc(s["v_ev"], 1)

            def attention(s0, v0, func, qb, kb, scale):
                def turn(c, i):
                    step = s0 + 6 * i + c
                    exps(c, step, scale)
                    if c + 2 < STEPS:
                        qkv(c + 2, step + 2, v0 + 2 * i + ((c + 2) // G + 1), func, qb, kb)

                qkv(0, s0, v0 + 1, func, qb, kb)
                qkv(1, s0 + 1, v0 + 1, func, qb, kb)
                for c in range(3):
                    turn(c, 0)
                with act.Fori(0, 3) as i:
                    for c in range(3, 9):
                        turn(c, i)
                for c in range(21, STEPS):
                    turn(c, 0)

            def layer_norm(y0, y1, n, aff=None):
                for c in range(NCH):
                    cs = slice(CH * c, CH * c + CH)
                    act.wait_ge(s["ln_cent"], 2 * (n * NCH + c + 1))
                    if c >= 2:
                        act.wait_ge(s["lnv_ps"], n * NCH + c - 1)
                    nc.scalar.activation(sq[:, c % 2, 0, :], y0[:, cs], ACT.Square).then_inc(s["ln_sq"], 1)
                    nc.scalar.activation(sq[0:C1, c % 2, 1, :], y1[0:C1, cs], ACT.Square).then_inc(s["ln_sq"], 1)
                for c in range(NCH):
                    act.wait_ge(s["lnv_ps"], n * NCH + c + 1)
                    nc.scalar.activation(rstd[:, c, :], PS[:, 4 + c, 0:128], ACT.Sqrt, bias=eps_t[:, 0:1])\
                      .then_inc(s["ln_root"], 1)
                if aff is not None:
                    for c in range(NCH):
                        cs = slice(CH * c, CH * c + CH)
                        act.wait_ge(s["ln_norm"], 2 * (n * NCH + c + 1))
                        nc.scalar.activation(y0[:, cs], y0[:, cs], ACT.Identity, bias=ln_b[:, aff, 0:1],
                                             scale=ln_g[:, aff, 0:1]).then_inc(s["ln_aff"], 1)
                        nc.scalar.activation(y1[0:C1, cs], y1[0:C1, cs], ACT.Identity, bias=ln_b[0:C1, aff, 1:2],
                                             scale=ln_g[0:C1, aff, 1:2]).then_inc(s["ln_aff"], 1)

            act.wait_ge(s["tok_in"], TOK_IN)
            act.wait_ge(s["pool_set"], MEMSETS)
            with act.Fori(0, LAYERS) as l:
                attention(l * STEPS, l * B, ACT.Relu, tok_qb, tok_kb, float(D) ** -0.5)
                for n in range(2):
                    act.wait_ge(s["bn_var"], l * 4 + 2 * (n + 1))
                    nc.scalar.activation(bn_s[:, 2, :], mv[:, :, 1], ACT.Sqrt, bias=eps_t[:, 0:1])\
                      .then_inc(s["bn_root"], 1)

            act.wait_ge(s["weights_in"], WEIGHTS_IN)
            layer_norm(nT0, nT1, 0)

            def rf_qk(b, g, bank):
                act.wait_ge(s["rf_qk"], b * G + (g + 1))
                for dst, func in ((QK, ACT.Copy), (SQ, ACT.Square)):
                    nc.scalar.activation(dst[:, g].rearrange("p k q -> p (k q)"), PS[:, bank, :], func,
                                         scale=float(HD) ** -0.25).then_inc(s["rf_qkev"], 1)

            def rf_values(b):
                act.wait_ge(s["rf_v"], b + 1)
                nc.scalar.copy(VB, PS[:, 7, 0:QT_ * D].rearrange("p (t d) -> p t d", t=QT_)).then_inc(s["rf_vev"], 1)

            def rf_squares(b):
                act.wait_ge(s["rf_diag"], b + 1)
                nc.scalar.copy(diagT, PS[0:32 * G, 6, :]).then_inc(s["rf_dgT_ev"], 1)

            def rf_exp(b, k, X):
                act.wait_ge(s["rf_sub"], b * 2 + (k + 1))
                v = X.rearrange("p t h m -> p (t h m)")
                nc.scalar.activation(v, v, ACT.Exp).then_inc(s["rf_exp"], 1)

            def rf_turn(b, more):
                if more:
                    rf_qk(b + 1, 0, 7)
                    rf_qk(b + 1, 1, 6)
                rf_exp(b, 0, KP)
                if more:
                    rf_qk(b + 1, 2, 7)
                rf_exp(b, 1, QP)
                act.wait_ge(s["rf_ctT"], b + 1)
                nc.scalar.copy(CT, PS[:, 6, 0:384]).then_inc(s["rf_ctTev"], 1)
                if more:
                    rf_values(b + 1)
                for g in range(G):
                    act.wait_ge(s["rf_qpT"], b * 3 + (g + 1))
                    nc.scalar.copy(QPT[:, 2 * g:2 * g + 2].rearrange("p q t n -> p (q t n)"), PS[:, g, :])\
                      .then_inc(s["rf_qpTev"], 1)
                if more:
                    rf_squares(b + 1)
                act.wait_ge(s["rf_ctx"], b + 1)
                for k in range(2):
                    r = slice(64 * k, 64 * k + 64)
                    nc.scalar.copy(CTX[r, :, k, :], PS[r, 3, 0:384].rearrange("p (n h d) -> p n h d", h=2, d=HD)[:, :, k, :])\
                      .then_inc(s["rf_ctxev"], 1)

            for g, bank in enumerate((7, 6, 5)):
                rf_qk(0, g, bank)
            rf_values(0)
            rf_squares(0)
            with act.Fori(0, B - 1) as b:
                rf_turn(b, True)
            rf_turn(B - 1, False)

            layer_norm(xT0, xT1, 1)
            layer_norm(nT0, nT1, 2, 0)
            attention(LAYERS * STEPS, LAYERS * B, ACT.Identity, ff_qb, ff_kb, float(HD) ** -0.5)
            layer_norm(nT0, nT1, 3, 1)
            for c in range(NCH):
                act.wait_ge(s["lg_ps"], c + 1)
                nc.scalar.copy(lgT[:, CH * c:CH * c + CH], PS[0:E, c, :]).then_inc(s["lg_ev"], 1)
            def turned_x(t):
                act.wait_ge(s["xr_ps"], t + 1)
                nc.scalar.copy(XR[:, t, 0:D], PS[:, 5 + t % 2, 0:D]).then_inc(s["xr_ev"], 1)

            act.wait_ge(s["lgT_ps"], 1)
            for t in range(2):
                turned_x(t)
            act.wait_ge(s["gate_arg"], 1)
            nc.scalar.activation(gs[:, 2, :], gs[:, 2, :], ACT.Exp).then_inc(s["gate_exp"], 1)
            for t in range(2, NT):
                turned_x(t)
            act.wait_ge(s["res_done"], 2)
            act.wait_ge(s["gT_ps"], 1)
            nc.scalar.copy(gatesT, PS[0:E, 0:4, :].rearrange("p b q -> p (b q)")).then_inc(s["gT_ev"], 1)
            for t in range(NT):
                act.wait_ge(s["sum_ps"], t + 1)
                nc.scalar.copy(rows[:, t, :], PS[:, 5 + t % 2, 0:D]).then_inc(s["sum_ev"], 1)

            def turned(n, c):
                act.wait_ge(s["xt_ps"], n + 1)
                nc.scalar.copy(XT[:, c % 2, 0], PS[:, 4 + c % 2, 0:128]).then_inc(s["xt_ev"], 1)
                nc.scalar.copy(XT[0:C1, c % 2, 1], PS[0:C1, 4 + c % 2, 128:256]).then_inc(s["xt_ev"], 1)

            def hidden(n, c):
                for m in range(HT):
                    if m % 3 == 0:
                        act.wait_ge(s["l1_ps"], n * 2 + (m // 3 + 1))
                    if m == 0:
                        act.wait_ge(s["y_ps"], n + 1)
                    nc.scalar.activation(HD_[:, c % 2, m], PS[:, 2 * (c % 2) + m // 3, 128 * (m % 3):128 * (m % 3) + 128],
                                         ACT.Gelu, bias=B1S[:, c % 2, m:m + 1]).then_inc(s["hid_ready"], 1)

            def scaled(n, c):
                act.wait_ge(s["y_ps"], n + 3)
                act.wait_ge(s["y_free"], n + 1)
                nc.scalar.activation(YS[:, c % 2], PS[:, 6 + c % 2, 0:D], ACT.Copy, scale=XL[:, c % UN, D + 1:D + 2])\
                  .then_inc(s["y_scaled"], 1)

            act.wait_ge(s["xr_ps"], NT)
            turned(0, 0)
            hidden(0, 0)
            turned(1, 1)

            def step(n, c):
                if not (isinstance(n, int) and n + 1 >= TILES):
                    hidden(n + 1, c + 1)
                if not (isinstance(n, int) and n + 2 >= TILES):
                    turned(n + 2, c + 2)
                scaled(n, c)

            with act.Fori(0, TURNS) as i:
                for c in range(UN):
                    step(i * UN + c, c)
            for n in range(UN * TURNS, TILES):
                step(n, n % UN)

        @block.vector
        def _(dve):
            dve.sem_inc(s["rf_done"], 1)
            ch = Chain(dve, s["dve_step"])
            tt, ts_, stt = nc.vector.tensor_tensor, nc.vector.tensor_scalar, nc.vector.scalar_tensor_tensor

            for t in zeroed[0:TOK_ZEROED]:
                nc.vector.memset(t[:], 0.0).then_inc(s["dve_set"], 1)
            dve.wait_ge(s["idx_in"], 16)
            ch.link(ts_(idx_b[:], tok_idx[:], 0, V, ALU.is_lt, ALU.mult))
            ch.link(tt(idx_b[:], idx_b[:], tok_idx[:], ALU.add))
            ts_(idx_a[:], idx_b[:], 0, V - 1, ALU.max, ALU.min).then_inc(s["idx_ready"], 1)
            for t in zeroed[TOK_ZEROED:]:
                nc.vector.memset(t[:], 0.0).then_inc(s["dve_set"], 1)
            for t in (hT1, nT1):
                nc.vector.memset(t[C1:, :], 1.0).then_inc(s["dve_set"], 1)
            dve.wait_ge(s["const_in"], 16 * len(consts))
            ch.link(nc.vector.tensor_copy(ident_b[:], ident[:]))
            for b in range(B):
                dve.wait_ge(rows_in[b], 32)
                r = rows[:, QT_ * b:QT_ * b + QT_, :]
                if b > 0:
                    dve.wait_ge(s["emb_sum"], b)
                ch.link(tt(ob[:], r, pos[:], ALU.add))
                tt(r, r, ob[:], ALU.add).then_inc(s["emb_sum"], 1)
            dve.wait_ge(s["emb_ev"], 2 * B)
            dve.sem_inc(s["h_ready"], 1)

            def maxima(c, step):
                for j in range(J):
                    dve.wait_ge(s["smax_ps"], 4 * step + (j + 1))
                    nc.vector.tensor_reduce(rmax[:, :, j, HD], PS[:, 4 + j % 2, :].rearrange("p (t k) -> p t k", t=QT_),
                                            AX, ALU.max).then_inc(s["smax_red"], 1)
                dve.wait_ge(s["mT_ps"], step + 1)
                for j in range(J):
                    r = slice(32 * j, 32 * j + 32)
                    tt(QM[r, c % 2, j, :], QT[r, c % 2, :], PS[:, 4, :].bitcast(BF16)[r, 0:S], ALU.subtract).then_inc(s["aug_done"], 1)

            def normalise(c, step, b, add):
                g = c % G
                lo, cols = 64 * (g % 2), bass.ds(b * S, S)
                rs = slice(lo, lo + 64)
                dve.wait_ge(s["av_ps"], step + 1)
                ch.link(nc.vector.reciprocal(rsum[0:64, :], PS[64:128, 7, 0:S]))
                if add:
                    dst = (hT0, hT1)[g // 2][rs, cols]
                    ch.link(tt(on[rs, :], PS[0:64, 7, 0:S], rsum[0:64, :], ALU.mult))
                    tt(dst, dst, on[rs, :], ALU.add).then_inc(s["o_done"], 1)
                else:
                    tt((oT0, oT1)[g // 2][rs, cols], PS[0:64, 7, 0:S], rsum[0:64, :], ALU.mult).then_inc(s["o_done"], 1)

            def attention(s0, add):
                def turn(c, i):
                    step = s0 + 6 * i + c
                    if c + 1 < STEPS:
                        maxima(c + 1, step + 1)
                    if c > 0:
                        normalise(c - 1, step - 1, 2 * i + (c - 1) // G, add)
                    if add and c > G and c % G == 1:
                        b = 2 * i + (c // G - 1)
                        dve.wait_ge(s["o_done"], step - 1)
                        part_stats(bass.ds(b, 1), bass.ds(b * S, S))

                maxima(0, s0)
                for c in range(3):
                    turn(c, 0)
                per = 16 if add else 6
                with dve.Fori(0, 3) as i:
                    mark = ch.enter(i, per)
                    for c in range(3, 9):
                        turn(c, i)
                    ch.leave(mark, 3)
                for c in range(21, STEPS):
                    turn(c, 0)
                normalise(STEPS - 1, s0 + STEPS - 1, B - 1, add)

            def part_stats(k, cs):
                ch.put(nc.vector.bn_stats(stats[:, 0, k, :], hT0[:, cs]))
                ch.put(nc.vector.bn_stats(stats[0:C1, 1, k, :], hT1[0:C1, cs]))

            def batch_norm(n, parts, done, roots):
                ch.wait()
                ch.put(nc.vector.memset(mv[C1:, 1, :], 0.0))
                nc.vector.bn_aggr(mv[:, 0, :], stats[:, 0, 0:parts].rearrange("p c k -> p (c k)")).then_inc(s["bn_var"], 1)
                nc.vector.bn_aggr(mv[0:C1, 1, :], stats[0:C1, 1, 0:parts].rearrange("p c k -> p (c k)")).then_inc(s["bn_var"], 1)
                scale, shift, part = bn_s[:, 0, :], bn_s[:, 1, :], bn_s[:, 2, :]
                dve.wait_ge(s["bn_root"], roots)
                ch.link(nc.vector.reciprocal(part, part))
                ch.link(tt(scale, part, bn_g[:, n, :], ALU.mult))
                ch.link(tt(part, mv[:, :, 0], scale, ALU.mult))
                ch.link(tt(shift, bn_b[:, n, :], part, ALU.subtract))
                ch.link(ts_(hT0[:], hT0[:], bn_s[:, 0, 0:1], bn_s[:, 1, 0:1], ALU.mult, ALU.add))
                ts_(hT1[0:C1, :], hT1[0:C1, :], bn_s[0:C1, 0, 1:2], bn_s[0:C1, 1, 1:2], ALU.mult, ALU.add)\
                    .then_inc(s[done], 1)

            def add_linear(x0, x1, ps, at):
                for c in range(NCH):
                    cs = slice(CH * c, CH * c + CH)
                    dve.wait_ge(s[ps], at + (2 * c + 2))
                    for k, (x, n) in enumerate(((x0, 128), (x1, C1))):
                        yield tt(x[0:n, cs], x[0:n, cs], PS[0:n, 2 * c + k, :], ALU.add)

            def layer_norm(x0, x1, y0, y1, n):
                for c in range(NCH):
                    cs = slice(CH * c, CH * c + CH)
                    dve.wait_ge(s["lnm_ps"], n * NCH + c + 1)
                    tt(y0[:, cs], x0[:, cs], PS[:, c, :], ALU.subtract).then_inc(s["ln_cent"], 1)
                    tt(y1[0:C1, cs], x1[0:C1, cs], PS[0:C1, c, :], ALU.subtract).then_inc(s["ln_cent"], 1)
                def invert(c):
                    dve.wait_ge(s["ln_root"], n * NCH + c + 1)
                    nc.vector.reciprocal(rstd[:, c, :], rstd[:, c, :]).then_inc(s["ln_inv"], 1)

                invert(0)
                for c in range(NCH):
                    cs = slice(CH * c, CH * c + CH)
                    if c + 1 < NCH:
                        invert(c + 1)
                    dve.wait_ge(s["ln_all"], n * NCH + c + 1)
                    tt(y0[:, cs], y0[:, cs], PS[:, 4 + c, :], ALU.mult).then_inc(s["ln_norm"], 1)
                    tt(y1[0:C1, cs], y1[0:C1, cs], PS[0:C1, 4 + c, :], ALU.mult).then_inc(s["ln_norm"], 1)

            dve.wait_ge(s["tok_in"], TOK_IN)
            dve.wait_ge(s["pool_set"], MEMSETS)
            with dve.Fori(0, LAYERS) as l:
                mark = ch.enter(l, LAYER_LINKS)
                attention(l * STEPS, True)
                dve.wait_ge(s["o_done"], l * STEPS + STEPS)
                part_stats(B - 1, slice(S * (B - 1), T))
                batch_norm(0, B, "bn1_done", l * 2 + 1)
                for c in range(NCH):
                    cs = slice(CH * c, CH * c + CH)
                    dve.wait_ge(s["ffn_ps"], l * (2 * NCH) + (2 * c + 2))
                    for k, (x, n) in enumerate(((hT0, 128), (hT1, C1))):
                        ch.put(tt(x[0:n, cs], x[0:n, cs], PS[0:n, 2 * c + k, :], ALU.add))
                    ch.wait()
                    part_stats(c, cs)
                batch_norm(1, NCH, "h_ready", l * 2 + 2)
                ch.leave(mark, LAYERS)

            dve.wait_ge(s["h_ready"], LAYERS + 1)
            layer_norm(hT0, hT1, nT0, nT1, 0)
            dd = [PS[:, 3 * (1 - k):3 * (1 - k) + 3, :].rearrange("p b (h m) -> p (b h) m", m=M) for k in range(2)]
            flat = [fmax[:, k].rearrange("p t h -> p (t h)") for k in range(2)]
            sub = [fsub[:, k].rearrange("p t h -> p (t h)") for k in range(2)]

            def wide(v):
                return v[:, :, None].broadcast_to([128, QT_ * H, M])

            def rf_squares(b):
                dve.wait_ge(s["rf_dgT"], b + 1)
                nc.vector.tensor_copy(fsub[:].rearrange("p k t (g j) -> p (k t) g j", j=J),
                                      PS[:, 4, 0:384].rearrange("p (n g r) -> p n g r", g=G, r=32)[:, :, :, 0:J])\
                    .then_inc(s["rf_diagev"], 1)

            def rf_key_maxima(b):
                dve.wait_ge(s["rf_dd"], b * 2 + 1)
                nc.vector.tensor_reduce(flat[1], dd[1], AX, ALU.max).then_inc(s["rf_fmax"], 1)

            def rf_turn(b, more):
                dve.wait_ge(s["rf_stT"], b + 1)
                ch.link(nc.vector.tensor_reduce(stab[:], PS[0:H, 6, 0:S], AX, ALU.max))
                ts_(stab_d[:], ident[0:H, 0:H], stab[:, 0:1], None, ALU.mult).then_inc(s["rf_std"], 1)
                dve.wait_ge(s["rf_dd"], b * 2 + 2)
                ch.link(nc.vector.tensor_reduce(flat[0], dd[0], AX, ALU.max))
                ch.link(tt(sub[0], flat[0], sub[0], ALU.add))
                dve.wait_ge(s["rf_stb"], b + 1)
                tt(fsub[:, 1], fsub[:, 1], PS[:, 6, 256:256 + H][:, None, :].broadcast_to([128, QT_, H]), ALU.add)\
                    .then_inc(s["rf_stbev"], 1)
                dve.wait_ge(s["rf_stbev"], b + 1)
                for k, X in ((1, KP), (0, QP)):
                    tt(X.rearrange("p t h m -> p (t h) m"), dd[k], wide(sub[k]), ALU.subtract).then_inc(s["rf_sub"], 1)
                for n, X in enumerate((KP, QP)):
                    dve.wait_ge(s["rf_exp"], b * 2 + (n + 1))
                    v = X.rearrange("p t h m -> p (t h m)")
                    ts_(v, v, RF_EPS, None, ALU.add).then_inc(s["rf_eps"], 1)
                if more:
                    rf_squares(b + 1)
                dve.wait_ge(s["rf_out"], b + 1)
                parts = ((obT0, 128, slice(0, S)), (obT1, C1, slice(S, 2 * S)))
                for o, n, cs in parts:
                    nc.vector.reciprocal(rden[0:n, cs], PS[0:n, 5, cs]).then_inc(s["rf_den"], 1)
                dve.wait_ge(s["rf_den"], b * 2 + 2)
                for o, n, cs in parts:
                    tt(o, PS[0:n, 7, cs], rden[0:n, cs], ALU.mult).then_inc(s["rf_o"], 1)
                if more:
                    rf_key_maxima(b + 1)
                dve.wait_ge(s["rf_y"], b + 1)
                for k, (x, n) in enumerate(((hT0, 128), (hT1, C1))):
                    dst = x[0:n, bass.ds(b * S, S)]
                    tt(dst, dst, PS[0:n, 7, S * k:S * k + S], ALU.add).then_inc(s["rf_done"], 1)

            rf_squares(0)
            rf_key_maxima(0)
            with dve.Fori(0, B - 1) as b:
                mark = ch.enter(b, 3)
                rf_turn(b, True)
                ch.leave(mark, B - 1)
            rf_turn(B - 1, False)

            dve.wait_ge(s["rf_done"], 2 * B + 1)
            layer_norm(hT0, hT1, xT0, xT1, 1)
            dve.wait_ge(s["ln_norm"], 2 * 2 * NCH)
            layer_norm(xT0, xT1, nT0, nT1, 2)
            attention(LAYERS * STEPS, False)
            for ins in add_linear(xT0, xT1, "xp_ps", 0):
                ins.then_inc(s["x2_done"], 1)
            dve.wait_ge(s["x2_done"], 2 * NCH)
            layer_norm(xT0, xT1, nT0, nT1, 3)
            tt(hT0[:], hT0[:], xT0[:], ALU.add).then_inc(s["res_done"], 1)
            tt(hT1[0:C1, :], hT1[0:C1, :], xT1[:], ALU.add).then_inc(s["res_done"], 1)

            def by_token(v):
                return v[:, :, None].broadcast_to([128, NT, E])

            numbers = expert_no[:, None, :].broadcast_to([128, NT, E])
            dve.wait_ge(s["lgT_ps"], 1)
            ch.link(nc.vector.tensor_copy(lg.rearrange("p t e -> p (t e)"), PS[:, 4, 0:NT * E]))
            logits = lg
            for n in range(2):
                top, first, pick = gs[:, n, :], gs[:, 3, :], gt[:, 3 + n]
                ch.link(nc.vector.tensor_reduce(top, logits, AX, ALU.max))
                ch.link(tt(gt[:, 0], logits, by_token(top), ALU.is_equal))
                ch.link(stt(gt[:, 1], gt[:, 0], -float(2 * E), numbers, ALU.mult, ALU.add))
                ch.link(nc.vector.tensor_reduce(first, gt[:, 1], AX, ALU.min))
                ch.link(tt(pick, gt[:, 1], by_token(first), ALU.is_equal))
                if n == 0:
                    ch.link(stt(gt[:, 2], pick, -3e38, lg, ALU.mult, ALU.add))
                    logits = gt[:, 2]
            tt(gt[:, 2], gt[:, 3], gt[:, 4], ALU.add).then_inc(s["picks_done"], 1)
            tt(gs[:, 2, :], gs[:, 1, :], gs[:, 0, :], ALU.subtract).then_inc(s["gate_arg"], 1)
            for r in run:
                ch.put(nc.vector.memset(r, 0.0))
            ch.put(nc.vector.memset(erun[:], 0.0))
            dve.wait_ge(s["gate_exp"], 1)
            ch.link(ts_(gs[:, 4, :], gs[:, 2, :], 1.0, None, ALU.add))
            ch.link(nc.vector.reciprocal(gs[:, 4, :], gs[:, 4, :]))
            ch.link(tt(gs[:, 5, :], gs[:, 2, :], gs[:, 4, :], ALU.mult))
            ch.link(tt(gt[:, 0], gt[:, 3], by_token(gs[:, 4, :]), ALU.mult))
            ch.link(tt(gt[:, 1], gt[:, 4], by_token(gs[:, 5, :]), ALU.mult))
            tt(gt[:, 5], gt[:, 0], gt[:, 1], ALU.add).then_inc(s["gates_done"], 1)

            dve.wait_ge(s["gates_done"], 1)
            dve.wait_ge(s["count_ps"], 1)
            inside, total = (PS[:, 7, k * NT * E:(k + 1) * NT * E].rearrange("p (t e) -> p t e", e=E) for k in range(2))
            ch.link(nc.vector.tensor_copy(run[0][:, 9:8 + NT, :], total[:, 0:NT - 1, :]))
            for k in range(4):
                x, y = run[k % 2], run[(k + 1) % 2]
                ch.link(tt(y[:, 8:8 + NT, :], x[:, 8:8 + NT, :], x[:, 8 - 2 ** k:8 + NT - 2 ** k, :], ALU.add))
            before = run[0][:, 8:8 + NT, :]
            ch.link(tt(count[:], before[:, NT - 1, :], total[:, NT - 1, :], ALU.add))
            ch.link(tt(more, count[:, :, None].broadcast_to([128, E, NT]),
                       marks[:, None, 0:NT].broadcast_to([128, E, NT]), ALU.is_gt))
            ch.link(nc.vector.tensor_reduce(erun[:, 0, 9:9 + E], more, AX, ALU.add))
            for k in range(3):
                x, y = erun[:, k % 2, :], erun[:, (k + 1) % 2, :]
                ch.link(tt(y[:, 8:9 + E], x[:, 8:9 + E], x[:, 8 - 2 ** k:9 + E - 2 ** k], ALU.add))
            first, end = erun[:, 1, 8:8 + E], erun[:, 1, 9:9 + E]
            ch.link(stt(gt[:, 2], first[:, None, :].broadcast_to([128, NT, E]), 128.0, before, ALU.mult, ALU.add))
            ch.link(tt(gt[:, 2], gt[:, 2], inside, ALU.add))
            ch.link(tt(gt[:, 0:2], gt[:, 3:5], gt[:, 2:3].broadcast_to([128, TK, NT, E]), ALU.mult))
            ch.link(nc.vector.tensor_reduce(gs[:, 0:2, :], gt[:, 0:2], AX, ALU.add))
            nc.vector.tensor_copy(slot[:], gs[:, 0:2, :]).then_inc(s["slots_done"], 1)
            dve.wait_ge(s["lgT_ps"], 1)
            ch.link(nc.vector.tensor_copy(XR[:, :, D].bitcast(I32), token_no[:]))
            nc.vector.tensor_copy(XR[:, :, D + 1], gs[:, 4, :]).then_inc(s["meta_done"], 1)
            ch.link(tt(told, end[0:1, None, :].broadcast_to([1, TILES, E]),
                       marks[0:1, NT:, None].broadcast_to([1, TILES, E]), ALU.is_le))
            ch.link(nc.vector.tensor_reduce(tile_f[:], told, AX, ALU.add))
            ts_(tile_e[:], tile_f[:], float(E - 1), None, ALU.min).then_inc(s["tile_e_done"], 1)

            def stage(n, c):
                e = dve.value_load(tile_e[0:1, bass.ds(n, 1)], min_val=0, max_val=E - 1)
                if not isinstance(n, int) or n >= 2:
                    dve.wait_ge(s["l1_ps"], n * 2 - 2)
                w = W1S[c % 2]
                nc.vector.tensor_copy(w[:, 0], w1_0[:, bass.ds(e, 1), :].rearrange("p a n -> p (a n)")).then_inc(s["w1_in"], 1)
                nc.vector.tensor_copy(w[0:C1, 1], w1_1[:, bass.ds(e, 1), :].rearrange("p a n -> p (a n)")).then_inc(s["w1_in"], 1)
                if not isinstance(n, int) or n >= 2:
                    dve.wait_ge(s["hid_ready"], n * HT + HT)
                nc.vector.tensor_copy(B1S[:, c % 2], b1_s[:, bass.ds(e, 1), :].rearrange("p a n -> p (a n)")).then_inc(s["w1_in"], 1)

            dve.wait_ge(s["moe_in"], 16 * (len(moe) + len(late)))
            dve.wait_ge(s["tile_e_done"], 1)
            stage(0, 0)
            stage(1, 1)
            dve.wait_ge(s["scatter_a"], 16 * NT)
            nc.vector.tensor_copy(XR[:, :, D + 1], gs[:, 5, :]).then_inc(s["meta_done"], 1)
            with dve.Fori(0, TURNS) as i:
                for c in range(UN):
                    stage(i * UN + (c + 2), c)
            stage(TILES - 1, UN * TURNS)


def constants():
    c = {"c_ident": np.eye(128, dtype=np.float32)}
    quarter = np.zeros((128, 4, 128), np.float32)
    for q in range(4):
        quarter[32 * q, q, :] = 1
    c["c_quarter"] = quarter
    c["c_head_mask"] = np.repeat(np.eye(J, dtype=np.float32), 32, axis=0)
    ho = np.zeros((128, 32), np.float32)
    kones = np.zeros((128, G), np.float32)
    for j in range(J):
        ho[32 * j:32 * j + HD, j] = 0.5
        kones[32 * j + HD, :] = 1
    c["c_head_half"], c["c_kones"] = ho, kones
    p, i = np.meshgrid(np.arange(S), np.arange(D // 2))
    pe = np.zeros((S, D), dtype=np.float32)
    pe[:, ::2] = np.sin(p / 2500 ** (2 * i / D)).T
    pe[:, 1::2] = np.cos(p / 2500 ** (2 * i / D)).T
    c["c_pos"] = pe
    c["c_upper"] = np.triu(np.ones((128, 128), np.float32), 1)
    c["c_ones"] = np.ones((128, 128), np.float32)
    c["c_token_no"] = np.arange(T, dtype=np.int32).reshape(NT, 128).T.copy()
    marks = np.concatenate([128 * np.arange(NT), np.arange(TILES)]).astype(np.float32)
    c["c_marks"] = np.tile(marks, (128, 1))
    empty = np.zeros((128, ROW), np.int32)
    empty[:, D] = T + np.arange(128)
    c["c_empty"] = empty.view(np.float32)
    c["c_expert_no"] = np.tile(np.arange(E, dtype=np.float32), (128, 1))
    return c


def kernel(**inputs):
    import concourse.bacc as bacc
    from concourse.bass_utils import run_bass_kernel_spmd

    nc = bacc.Bacc("TRN2", target_bir_lowering=False, num_devices=1)
    arrays, aps = {}, {}
    given = {n: np.ascontiguousarray(v) for n, v in inputs.items()}
    given["c_projT"] = np.ascontiguousarray(given["L0_attn_proj"].T)
    given.update(constants())
    for name, v in given.items():
        if name == "L0_attn_proj":
            continue
        arrays[f"in_{name}"] = v
        aps[name] = nc.dram_tensor(f"in_{name}", v.shape, mybir.dt.from_np(v.dtype), kind="ExternalInput").ap()
    out = nc.dram_tensor("out_0", (B, S, D), F32, kind="ExternalOutput").ap()
    build(nc, aps, out)
    r = run_bass_kernel_spmd(nc, [arrays], core_ids=[0])
    return r.results[0]["out_0"]
```

```python
from contextlib import ExitStack

import numpy as np

import concourse.bass as bass
from concourse import mybir

F32 = mybir.dt.float32
BF16 = mybir.dt.bfloat16
I32 = mybir.dt.int32
ALU = mybir.AluOpType
ACT = mybir.ActivationFunctionType
AX = mybir.AxisListType.X

B, S, D, V = 8, 256, 192, 8000
T = B * S
H, HD = 12, 16
G, J = 3, 4
DC = D // 3
C1 = D - 128
M = 64
E, HID = 8, 768
HT = HID // 128
NT = T // 128
QT_ = S // 128
CH = 512
NCH = T // CH
TK = 2
TILES = TK * NT + E - 1
UN = 6
LEAD = 4
TURNS = (TILES - LEAD) // UN
LAYERS = 2
LAYER_LINKS = 90
STEPS = B * G
BN_EPS, LN_EPS, RF_EPS = 1e-5, 1e-5, 1e-4


class Chain:

    def __init__(self, eng, sem):
        self.eng, self.sem, self.base, self.k = eng, sem, 0, 0

    def put(self, ins):
        ins.then_inc(self.sem, 1)
        self.k += 1

    def wait(self):
        self.eng.wait_ge(self.sem, self.base + self.k)

    def link(self, ins):
        self.put(ins)
        self.wait()

    def enter(self, i, per):
        saved = self.base, self.k
        self.base, self.k = i * per + self.base + self.k, 0
        return saved, per

    def leave(self, mark, turns):
        (base, k), per = mark
        assert self.k == per, (self.k, per)
        self.base, self.k = base, k + turns * per


def build(nc, a, out):
    with ExitStack() as ctx:
        def sb(name, shape, dt=F32):
            return ctx.enter_context(nc.sbuf_tensor(name, shape, dt))

        def sem(name):
            return ctx.enter_context(nc.semaphore(name))

        PS = ctx.enter_context(nc.psum_tensor("PS", [128, 8, CH], F32))

        ident = sb("ident", [128, 128])
        ident_b = sb("ident_b", [128, 128], BF16)
        head_half = sb("head_half", [128, 32])
        pos = sb("pos", [128, QT_, D])
        expert_no = sb("expert_no", [128, E])
        upper = sb("upper", [128, 128])
        ones = sb("ones", [128, 128])
        token_no = sb("token_no", [128, NT + 1])
        mean_w = sb("mean_w", [128, 128])
        ones12 = sb("ones12", [H, 128])

        tok_wq = sb("tok_wq", [128, G, J, 32])
        tok_wk = sb("tok_wk", [128, G, J, 32])
        tok_wv = sb("tok_wv", [C1 + 1, D])
        tok_qb = sb("tok_qb", [128, G])
        tok_kb = sb("tok_kb", [128, G])
        tok_wf0 = sb("tok_wf0", [128, D])
        tok_wf1 = sb("tok_wf1", [C1 + 1, D])
        bn_g = sb("bn_g", [128, 2, 2])
        bn_b = sb("bn_b", [128, 2, 2])
        rf_wq0 = sb("rf_wq0", [128, G, J, 32])
        rf_wq1 = sb("rf_wq1", [C1, G, J, 32])
        rf_wk0 = sb("rf_wk0", [128, G, J, 32])
        rf_wk1 = sb("rf_wk1", [C1, G, J, 32])
        rf_wv0 = sb("rf_wv0", [128, D])
        rf_wv1 = sb("rf_wv1", [C1, D])
        rf_wo0 = sb("rf_wo0", [128, D])
        rf_wo1 = sb("rf_wo1", [C1, D])
        rf_proj = sb("rf_proj", [128, J, M])
        ff_wq0 = sb("ff_wq0", [128, G, J, 32])
        ff_wq1 = sb("ff_wq1", [C1, G, J, 32])
        ff_wk0 = sb("ff_wk0", [128, G, J, 32])
        ff_wk1 = sb("ff_wk1", [C1, G, J, 32])
        ff_wv0 = sb("ff_wv0", [128, D])
        ff_wv1 = sb("ff_wv1", [C1 + 1, D])
        ff_qb = sb("ff_qb", [128, G])
        ff_kb = sb("ff_kb", [128, G])
        ff_wp0 = sb("ff_wp0", [128, D])
        ff_wp1 = sb("ff_wp1", [C1 + 1, D])
        ln_g = sb("ln_g", [128, 2, 2])
        ln_b = sb("ln_b", [128, 2, 2])
        gate0 = sb("gate0", [128, E])
        gate1 = sb("gate1", [C1, E])
        w1_0 = sb("w1_0", [128, E, HID])
        w1_1_all = sb("w1_1_all", [128, E, HID])
        w1_1 = w1_1_all[0:C1]
        w2_s = sb("w2_s", [128, E, HT, D])
        b1_s = sb("b1_s", [128, E, HT])

        tok_idx = sb("tok_idx", [128, NT], I32)
        idx_a = sb("idx_a", [128, NT], I32)
        idx_b = sb("idx_b", [128, NT], I32)
        rows = sb("rows", [128, NT, D])
        hT0 = sb("hT0", [128, T])
        hT1 = sb("hT1", [C1 + 1, T])
        nT0 = sb("nT0", [128, T])
        nT1 = sb("nT1", [C1 + 1, T])
        xT0 = sb("xT0", [128, T])
        xT1 = sb("xT1", [C1, T])
        oT0, oT1 = nT0, nT1
        in0 = sb("in0", [128, 2, S])
        in1 = sb("in1", [C1 + 1, 2, S])
        carved = [0]

        def carve(n, dt=F32):
            flat = w2_s[:].rearrange("p e t d -> p (e t d)")[:, carved[0]:carved[0] + n]
            carved[0] += n
            assert carved[0] <= E * HT * D
            return flat if dt == F32 else flat.bitcast(dt)

        QT = carve(3 * S).rearrange("p (k q) -> p k q", k=3)
        QTb = carve(S, BF16).rearrange("p (k q) -> p k q", k=2)
        KM = carve(3 * J * S).rearrange("p (k j q) -> p k j q", k=3, j=J)
        KMb = carve(J * S, BF16).rearrange("p (k j q) -> p k j q", k=2, j=J)
        VA = carve(2 * QT_ * G * J * 32).rearrange("p (k t g j d) -> p k t g j d", k=2, t=QT_, g=G, j=J)
        rmax = carve(QT_ * J * 16, BF16).rearrange("p (t j d) -> p t j d", t=QT_, j=J)
        FW = QT_ * H * M
        early = w1_1_all[:].rearrange("p e n -> p (e n)")
        P = early[:, 0:8 * QT_ * S].rearrange("p (n j t q) -> p n j t q", n=4, j=2, t=QT_)
        KP, QP = (early[:, n * FW:(n + 1) * FW].rearrange("p (t h m) -> p t h m", t=QT_, h=H) for n in range(2))
        QPT = early[:, 2 * FW:3 * FW].rearrange("p (q t n) -> p q t n", t=QT_, n=128)
        QK = early[:, 3 * FW:4 * FW].rearrange("p (g k q) -> p g k q", g=G, k=2)
        av, rsum, on = (early[:, 4 * FW - (n + 1) * S:4 * FW - n * S] for n in range(3))
        stats = sb("stats", [128, 2, B, 6])
        mv = sb("mv", [128, 2, 2])
        eps_t = sb("eps_t", [128, 1])
        rf_eps_t = sb("rf_eps_t", [128, 1])
        bn_s = sb("bn_s", [128, 3, 2])
        HB = sb("HB", [128, 2 * HT * CH])
        sq = HB[:, 6 * CH:10 * CH].rearrange("p (k c q) -> p k c q", k=2, q=CH)
        rstd = HB[:, 10 * CH:10 * CH + T // 4].rearrange("p (c q) -> p c q", c=NCH)
        regroup = HB[:, 4 * CH - 128:4 * CH]
        quarter = HB[:, 4 * CH:5 * CH].rearrange("p (q n) -> p q n", q=4)
        SQ = carve(G * 2 * S).rearrange("p (g k q) -> p g k q", g=G, k=2)
        VB = carve(QT_ * D).rearrange("p (t d) -> p t d", t=QT_)
        fmax = sb("fmax", [128, 2, QT_, H])
        fsub = sb("fsub", [128, 2, QT_, H])
        stab = sb("stab", [H, 1])
        stab_d = sb("stab_d", [H, H])
        CTX = carve(2 * H * HD).rearrange("p (n h d) -> p n h d", h=2, d=HD)
        ob = early[:, 0:QT_ * D].rearrange("p (t d) -> p t d", t=QT_)
        diagT = HB[0:32 * G, 0:2 * S]
        rden = HB[:, 2 * S:4 * S]
        obT0, obT1 = HB[:, 4 * S:5 * S], HB[0:C1, 5 * S:6 * S]
        CT = HB[:, 6 * S:6 * S + 384]
        yT = HB[:, 5 * CH:6 * CH]
        lgT = HB[0:E, 0:T]
        gt = sb("gt", [128, 5, NT, E])
        gs = sb("gs", [128, 6, NT])
        def area(t, at, *dims):
            n = int(np.prod(dims))
            names = " ".join(f"d{k}" for k in range(len(dims)))
            return t[:, at:at + n].rearrange(f"p ({names}) -> p {names}", **{f"d{k}": v for k, v in enumerate(dims)})

        XR = area(HB, 0, NT, D)
        RUN = NT * D
        run = [area(HB, RUN + k * (8 + NT) * E, 8 + NT, E) for k in range(2)]
        more = area(HB, RUN + 2 * (8 + NT) * E, E, NT)
        lg = area(HB, RUN + 512, NT, E)
        told = HB[0:1, RUN + 640:RUN + 640 + TILES * E].rearrange("p (n e) -> p n e", e=E)
        place = area(HB, RUN + 952, 2, TK, NT)
        in_row = area(HB, RUN + 1024, 2, 4, 128)
        in_tile = [area(v, 0, NT, 2, TILES) for v in (xT0, nT0)]
        none = HB[:, RUN + 2048:RUN + 2048 + TILES]
        tile_f = HB[0:1, RUN + 2112:RUN + 2112 + TILES]
        slot = area(HB, RUN + 2176, 3, TK, NT).bitcast(I32)
        count_up = HB[:, RUN + 2560:RUN + 2560 + 128]
        erun = sb("erun", [128, 2, 8 + E + 1])
        count = sb("count", [128, E])
        tile_e = sb("tile_e", [1, TILES], I32)
        ids = sb("ids", [128, TILES], I32)
        id_gates = sb("id_gates", [128, TILES])
        id_c = sb("id_c", [128, UN], I32)
        gate_c = sb("gate_c", [128, UN])
        W1S = [area(xT0, 0, 2, HID), area(HB, RUN, 2, HID)]
        XT = area(xT0, 2 * HID, 2, 2, 128)
        XL = area(HB, RUN + 2 * HID, UN, D)
        HD_ = area(nT0, 0, 2, HT, 128)
        YS = area(nT0, 2 * HID, 2, D)
        B1S = sb("B1S", [128, 2, HT])
        b2_all = area(hT0, 0, E, D)
        B2S = [pos[:, 0, :], pos[:, 1, :], HB[:, RUN + 2 * HID + UN * D:RUN + 2 * HID + (UN + 1) * D]]
        rows_d = nc.dram_tensor("rows_d", (T + 128, D), F32).ap()
        sums_d = nc.dram_tensor("sums_d", (T + 128, D), F32).ap()

        names = """idx_in const_in tok_in weights_in moe_in pad_done out_done
            idx_ready dve_set pool_set pool_turn dve_step emb_sum emb_ps emb_ev h_ready
            in_ready proj_ps v_ps qkv_ev v_ev cast_done smax_ps smax_red mT_ps aug_done st_ps p_ready
            av_ps av_ev regrouped o_done
            bn_var bn_root bn1_done ffn_ps lnm_ps ln_cent ln_sq lnv_ps ln_root ln_inv ln_all ln_norm ln_aff
            rf_v rf_vev rf_qk rf_qkev rf_diag rf_dgT_ev rf_dgT rf_diagev rf_dd rf_fmax rf_stT rf_std rf_stb rf_stbev
            rf_sub rf_exp rf_eps rf_ctT rf_ctTev rf_ctx rf_ctxev rf_qpT rf_qpTev rf_out rf_den rf_o rf_y rf_yev rf_done
            xp_ps x2_done res_done lg_ps lg_ev lgT_ps gate_arg gate_exp
            picks_done count_ps xr_ps xr_ev fill_done tile_e_done in_row_set in_row_used ids_done
            xn_in sums_in b2_in id_in w1_in xt_ps xt_ev l1_ps hid_ready y_ps y_biased y_scaled y_added y_free""".split()
        s = {n: sem(n) for n in names}
        rows_in = [sem(f"rows_in{b}") for b in range(B)]
        tile_in = [sem(f"tile_in{c}") for c in range(UN)]

        ctx.enter_context(nc.allow_non_contiguous_dma(reason="small vectors laid onto partitions once"))
        block = ctx.enter_context(nc.Block())

        consts = [(ident, a["c_ident"]), (head_half, a["c_head_half"]),
                  (pos, a["c_pos"].rearrange("(t p) d -> p t d", p=128)), (expert_no, a["c_expert_no"]),
                  (upper, a["c_upper"]), (ones, a["c_ones"]), (token_no, a["c_token_no"]), (count_up, a["c_count_up"]),
                  (quarter, a["c_quarter"]), (regroup, a["c_regroup"])]

        def by_head(w):
            return w.rearrange("c (g j d) -> c g j d", g=G, j=J)

        heads = []
        tok_heads = []
        for w, src, lo, n, r0 in ((tok_wq, a["L0_tok_Wq"], 0, DC, 0), (tok_wk, a["L0_tok_Wk"], 0, DC, DC),
                                  (rf_wq0, a["L0_attn_Wq"], 0, 128, 0), (rf_wq1, a["L0_attn_Wq"], 128, C1, 0),
                                  (rf_wk0, a["L0_attn_Wk"], 0, 128, 0), (rf_wk1, a["L0_attn_Wk"], 128, C1, 0)):
            for g in range(G):
                group = tok_heads if w in (tok_wq, tok_wk) else heads
                group.append((w[r0:r0 + n, g, :, 0:HD], by_head(src)[lo:lo + n, g]))
        qkv_w = a["L0_ffn_qkv_w"]
        for w, part, lo, n in ((ff_wq0, 0, 0, 128), (ff_wq1, 0, 128, C1), (ff_wk0, 1, 0, 128), (ff_wk1, 1, 128, C1)):
            for g in range(G):
                heads.append((w[0:n, g, :, 0:HD], by_head(qkv_w[:, part * D:(part + 1) * D])[lo:lo + n, g]))

        def bias_cols(t, v):
            return [(t[32 * j:32 * j + HD, :], v.rearrange("(g j d) -> j d g", g=G, j=J)[j]) for j in range(J)]

        qkv_b = a["L0_ffn_qkv_b"]
        tok_heads += bias_cols(tok_qb, a["L0_tok_bq"]) + bias_cols(tok_kb, a["L0_tok_bk"])
        heads += bias_cols(ff_qb, qkv_b[0:D]) + bias_cols(ff_kb, qkv_b[D:2 * D])
        heads += [(rf_proj[32 * j:32 * j + HD, j, :], a["c_projT"]) for j in range(J)]

        def row(v):
            return v.rearrange("(a d) -> a d", a=1)

        def cols(t, k, v):
            return [(t[:, k, 0:1], v[0:128].rearrange("(p a) -> p a", a=1)),
                    (t[0:C1, k, 1:2], v[128:D].rearrange("(p a) -> p a", a=1))]

        tok_plain = [(tok_wv[0:C1, :], a["L0_tok_Wv"]), (tok_wv[C1:, :], row(a["L0_tok_bv"])),
                 (tok_wf0[:], a["L0_tok_Wf"][0:128, :]), (tok_wf1[0:C1, :], a["L0_tok_Wf"][128:D, :]),
                 (tok_wf1[C1:, :], row(a["L0_tok_bf"]))]
        plain = [(rf_wv0[:], a["L0_attn_Wv"][0:128, :]), (rf_wv1[:], a["L0_attn_Wv"][128:D, :]),
                 (rf_wo0[:], a["L0_attn_Wo"][0:128, :]), (rf_wo1[:], a["L0_attn_Wo"][128:D, :]),
                 (ff_wv0[:], qkv_w[0:128, 2 * D:]), (ff_wv1[0:C1, :], qkv_w[128:D, 2 * D:]),
                 (ff_wv1[C1:, :], row(qkv_b[2 * D:])),
                 (ff_wp0[:], a["L0_ffn_proj_w"][0:128, :]), (ff_wp1[0:C1, :], a["L0_ffn_proj_w"][128:D, :]),
                 (ff_wp1[C1:, :], row(a["L0_ffn_proj_b"])),
                 (gate0[:], a["L0_ffn_gate_w"][0:128, :]), (gate1[:], a["L0_ffn_gate_w"][128:D, :])]
        tok_plain += cols(bn_g, 0, a["L0_tok_g1"]) + cols(bn_b, 0, a["L0_tok_b1"])
        tok_plain += cols(bn_g, 1, a["L0_tok_g2"]) + cols(bn_b, 1, a["L0_tok_b2"])
        plain += cols(ln_g, 0, a["L0_ffn_ln1_g"]) + cols(ln_b, 0, a["L0_ffn_ln1_b"])
        plain += cols(ln_g, 1, a["L0_ffn_ln2_g"]) + cols(ln_b, 1, a["L0_ffn_ln2_b"])
        moe = [(w1_0[:], a["L0_ffn_w1"][:, 0:128, :].rearrange("e c n -> c e n")),
               (b1_s[:], a["L0_ffn_b1"].rearrange("e (t p) -> p e t", p=128))]
        late = [(w1_1, a["L0_ffn_w1"][:, 128:D, :].rearrange("e c n -> c e n"))]
        late += [(w2_s[:, e], a["L0_ffn_w2"][e].rearrange("(t p) d -> p t d", p=128)) for e in range(E)]
        zeroed = [tok_wq, tok_wk, tok_qb, rf_wq0, rf_wq1, rf_wk0, rf_wk1, ff_wq0, ff_wq1, ff_wk0, ff_wk1, rf_proj, ff_qb]
        TOK_ZEROED = 3
        DVE_SETS = len(zeroed) + 2
        MEMSETS = 10
        TOK_IN = 16 * (len(tok_plain) + len(tok_heads))
        WEIGHTS_IN = 16 * (len(plain) + len(heads))

        @block.sync
        def _(sp):
            sp.dma_start(tok_idx[:], a["x"].rearrange("b (t p) -> p (b t)", p=128)).then_inc(s["idx_in"], 16)
            for dst, src in consts:
                sp.dma_start(dst[:], src).then_inc(s["const_in"], 16)
            sp.dma_start(tok_kb[:], a["c_kones"]).then_inc(s["pad_done"], 16)
            sp.dma_start(ff_kb[:], a["c_kones"]).then_inc(s["pad_done"], 16)
            for dst, src in tok_plain:
                sp.dma_start(dst, src).then_inc(s["tok_in"], 16)
            sp.wait_ge(s["pad_done"], 32)
            sp.wait_ge(s["dve_set"], TOK_ZEROED)
            for dst, src in tok_heads:
                sp.dma_start(dst, src).then_inc(s["tok_in"], 16)
            for dst, src in plain:
                sp.dma_start(dst, src).then_inc(s["weights_in"], 16)
            sp.wait_ge(s["dve_set"], len(zeroed))
            for dst, src in heads:
                sp.dma_start(dst, src).then_inc(s["weights_in"], 16)
            for dst, src in moe:
                sp.dma_start(dst, src).then_inc(s["moe_in"], 16)
            for v in (rows_d, sums_d):
                sp.dma_start(v[T:], a["c_zeros"]).then_inc(s["fill_done"], 16)
            sp.wait_ge(s["o_done"], (LAYERS + 1) * STEPS)
            for dst, src in late:
                sp.dma_start(dst, src).then_inc(s["moe_in"], 16)
            sp.wait_ge(s["xr_ev"], 2 * NT)
            sp.dma_start(rows_d[0:T].rearrange("(t p) d -> p t d", p=128), XR).then_inc(s["xn_in"], 16)
            sp.dma_start(sums_d[0:T].rearrange("(t p) d -> p t d", p=128), rows[:]).then_inc(s["sums_in"], 16)
            sp.dma_start(b2_all, a["L0_ffn_b2"].rearrange("(a e) d -> a e d", a=1).broadcast_to([128, E, D]))\
                .then_inc(s["b2_in"], 16)
            sp.wait_ge(s["y_added"], 16 * TILES)
            sp.dma_start(out.rearrange("b s d -> (b s) d"), sums_d[0:T]).then_inc(s["out_done"], 16)
            sp.wait_ge(s["out_done"], 16)

        @block.gpsimd
        def _(pool):
            sets = ((mean_w[:], 1.0 / D), (ones12[:], 1.0), (eps_t[:], BN_EPS), (rf_eps_t[:], RF_EPS),
                    (VA, 1.0), (rmax, 0.0), (CTX, 0.0), (KM, 0.0), (bn_g[64:, :, 1:2], 0.0), (bn_b[64:, :, 1:2], 0.0))
            assert len(sets) == MEMSETS
            for k, (t, v) in enumerate(sets):
                if k == MEMSETS - 3:
                    pool.wait_ge(s["idx_ready"], 1)
                    for n in range(NT):
                        pool.indirect_dma_start(rows[:, n, :], None, a["L0_tok_emb"],
                                                bass.IndirectOffsetOnAxis(ap=idx_a[:, n:n + 1], axis=0))\
                            .then_inc(rows_in[n // QT_], 16)
                if k:
                    pool.wait_ge(s["pool_set"], k)
                nc.gpsimd.memset(t, v).then_inc(s["pool_set"], 1)
            pool.wait_ge(s["pool_set"], MEMSETS)

            def then(value, name):
                pool.wait_ge(s[name], value)
                pool.sem_inc(s["pool_turn"], 1)

            def copy_in(src0, src1, b, slot):
                cols = bass.ds(b * S, S)
                nc.gpsimd.tensor_copy(in0[:, slot, :], src0[:, cols]).then_inc(s["in_ready"], 1)
                nc.gpsimd.tensor_copy(in1[:, slot, :], src1[:, cols]).then_inc(s["in_ready"], 1)

            def attention(src0, src1, s0):
                def turn(c, i):
                    if c == 2:
                        then(4 * s0 + 4, "smax_ps")
                    then(5 * s0 + 30 * i + (5 * c + 1), "qkv_ev")
                    nc.gpsimd.tensor_copy(QTb[:, c % 2, :], QT[:, c % 3, :]).then_inc(s["cast_done"], 1)
                    then(5 * s0 + 30 * i + (5 * c + 5), "qkv_ev")
                    nc.gpsimd.tensor_tensor(KMb[:, c % 2], KM[:, c % 3],
                                            ones[:, 0:J, None].broadcast_to([128, J, S]), ALU.mult)\
                        .then_inc(s["cast_done"], 1)
                    if c % G == 0 and c // G + 1 < B:
                        copy_in(src0, src1, 2 * i + c // G + 1, (c // G + 1) % 2)

                for c in range(3):
                    turn(c, 0)
                with pool.Fori(0, 3) as i:
                    for c in range(3, 9):
                        turn(c, i)
                for c in range(21, STEPS):
                    turn(c, 0)

            with pool.Fori(0, LAYERS) as l:
                then(l * (2 * NCH) + 2 * NCH, "h_ready")
                attention(hT0, hT1, l * STEPS)
            pool.wait_ge(s["ln_norm"], 2 * NCH)
            pool.sem_inc(s["rf_done"], 1)

            def rf_add(b):
                for k, (x, n) in enumerate(((hT0, 128), (hT1, C1))):
                    dst = x[0:n, bass.ds(b * S, S)]
                    nc.gpsimd.tensor_tensor(dst, dst, yT[0:n, S * k:S * k + S], ALU.add).then_inc(s["rf_done"], 1)

            copy_in(nT0, nT1, 0, 0)
            pool.wait_ge(s["rf_v"], 1)
            copy_in(nT0, nT1, 1, 0)
            with pool.Fori(0, B - 2) as b:
                then(b + 2, "rf_v")
                copy_in(nT0, nT1, b + 2, 0)
                then(b * 2 + 3, "rf_yev")
                rf_add(b)
            for b in (B - 2, B - 1):
                pool.wait_ge(s["rf_yev"], b * 2 + 3)
                rf_add(b)
            pool.wait_ge(s["ln_aff"], 2 * NCH)
            attention(nT0, nT1, LAYERS * STEPS)

            def gather(n, c):
                if not isinstance(n, int) or n >= LEAD:
                    then(n - LEAD + 1, "xt_ps")
                nc.gpsimd.tensor_copy(id_c[:, c:c + 1], ids[:, bass.ds(n, 1)]).then_inc(s["id_in"], 1)
                nc.gpsimd.tensor_copy(gate_c[:, c:c + 1], id_gates[:, bass.ds(n, 1)]).then_inc(s["id_in"], 1)
                then(n * 2 + 2, "id_in")
                pool.indirect_dma_start(XL[:, c, :], None, rows_d,
                                        bass.IndirectOffsetOnAxis(ap=id_c[:, c:c + 1], axis=0)).then_inc(tile_in[c], 16)

            def add_tile(n, c):
                then(n + 3, "y_scaled")
                pool.indirect_dma_start(sums_d, bass.IndirectOffsetOnAxis(ap=id_c[:, c:c + 1], axis=0),
                                        YS[:, c % 2, :], None, compute_op=ALU.add).then_inc(s["y_added"], 16)
                if not isinstance(n, int) or n + LEAD < TILES:
                    gather(n + LEAD, (c + LEAD) % UN)
                pool.wait_ge(s["y_added"], n * 16 + 16)
                pool.sem_inc(s["y_free"], 1)

            pool.sem_inc(s["y_free"], 2)
            pool.wait_ge(s["ids_done"], 2)
            pool.wait_ge(s["fill_done"], 32)
            pool.wait_ge(s["xn_in"], 16)
            for n in range(LEAD):
                gather(n, n)
            pool.wait_ge(s["sums_in"], 16)
            with pool.Fori(0, TURNS) as i:
                for c in range(UN):
                    add_tile(i * UN + c, c)
            for n in range(UN * TURNS, TILES):
                add_tile(n, n % UN)

        @block.tensor
        def _(pe):
            pe.sem_inc(s["y_ps"], 2)
            pe.sem_inc(s["xt_ps"], 2)
            pe.wait_ge(s["const_in"], 16 * len(consts))
            for b in range(B):
                pe.wait_ge(s["emb_sum"], b + 1)
                if b >= 4:
                    pe.wait_ge(s["emb_ev"], 2 * (b - 3))
                for t in range(QT_):
                    pe.transpose(PS[:, 2 * (b % 4), 128 * t:128 * t + 128], rows[:, QT_ * b + t, 0:128], ident[:])
                    last = pe.transpose(PS[0:C1, 2 * (b % 4) + 1, 128 * t:128 * t + 128], rows[:, QT_ * b + t, 128:D],
                                        ident[:])
                last.then_inc(s["emb_ps"], 1)

            def proj(c, step, w, keys, batch2):
                g, pb = c % G, (c // G) % 2
                if c % G == 0 and not keys:
                    pe.wait_ge(s["in_ready"], batch2)
                if c > 0 and not keys:
                    pe.wait_ge(s["qkv_ev"], 5 * step)
                ins = (in0[:, pb, :], in1[:, pb, :])
                lo = S if keys else 0
                for n, (wt, ch) in enumerate(w):
                    last = pe.matmul(PS[:, 6, lo:lo + S], wt[:, g].rearrange("c j d -> c (j d)"),
                                     ins[ch][0:wt.shape[0]], start=n == 0, stop=n == len(w) - 1)
                if keys:
                    last.then_inc(s["proj_ps"], 1)

            def proj_v(c, step, wv):
                pb = (c // G) % 2
                ins = (in0[:, pb, :], in1[:, pb, :])
                if c > 0:
                    pe.wait_ge(s["smax_red"], 4 * step)
                for t in range(QT_):
                    for n, (wt, ch) in enumerate(wv):
                        last = pe.matmul(PS[:, 5, D * t:D * t + D], ins[ch][0:wt.shape[0], 128 * t:128 * t + 128],
                                         wt[:], start=n == 0, stop=n == len(wv) - 1)
                last.then_inc(s["v_ps"], 1)

            def smax(c, step, batch, half):
                p = c % 2
                if half == 0:
                    pe.wait_ge(s["cast_done"], 2 * (step + 1))
                for j in (2 * half, 2 * half + 1):
                    if j == 0 and c > 0:
                        pe.wait_ge(s["aug_done"], step)
                    if j == 1 and c % G == 0:
                        pe.wait_ge(s["v_ev"], batch)
                    if j >= 2:
                        pe.wait_ge(s["smax_red"], 4 * step + j - 1)
                    for t in range(QT_):
                        last = pe.matmul(PS[:, 4 + j % 2, S * t:S * t + S],
                                         QTb[:, p, 128 * t:128 * t + 128], KMb[:, p, j, :], start=True, stop=True)
                    last.then_inc(s["smax_ps"], 1)

            def turn_max(c, step):
                pe.wait_ge(s["smax_red"], 4 * (step + 1))
                for t in range(QT_):
                    last = pe.transpose(PS[:, 4, :].bitcast(BF16)[:, 128 * t:128 * t + 128],
                                        rmax[:, t].rearrange("p j d -> p (j d)"), ident_b[:])
                last.then_inc(s["mT_ps"], 1)

            def scores(c, step, h):
                if c > 0:
                    pe.wait_ge(s["p_ready"], 2 * step + h - 1)
                if h == 0:
                    pe.wait_ge(s["aug_done"], step + 1)
                for t in range(QT_):
                    for j in (2 * h, 2 * h + 1):
                        last = pe.matmul(PS[:, j, S * t:S * t + S], KM[:, c % 3, j, 128 * t:128 * t + 128],
                                         QT[:, c % 3, :], start=True, stop=True)
                last.then_inc(s["st_ps"], 1)

            def weigh(c, step, batch):
                if c > 0:
                    pe.wait_ge(s["o_done"], step)
                pe.wait_ge(s["p_ready"], 2 * (step + 1))
                pe.wait_ge(s["v_ev"], batch)
                for t in range(QT_):
                    for j in range(J):
                        last = pe.matmul(PS[32 * j:32 * j + 32, 7, 0:S], VA[:, (c // G) % 2, t, c % G, j, :],
                                         P[:, 2 * (c % 2) + j // 2, j % 2, t, :], start=t == 0, stop=t == QT_ - 1,
                                         skip_group_check=True)
                last.then_inc(s["av_ps"], 1)

            def group(step):
                pe.wait_ge(s["av_ev"], step + 1)
                pe.matmul(PS[:, 7, S:2 * S], regroup, av, start=True, stop=True).then_inc(s["regrouped"], 1)

            def attention(s0, b0, v0, wq, wk, wv):
                def pj(c, i, parts=(0, 1)):
                    for k in parts:
                        proj(c, s0 + 6 * i + c, (wq, wk)[k], k, 2 * (b0 + 2 * i + c // G + 1))

                def turn(c, i):
                    step = s0 + 6 * i + c
                    n1 = (c + 1, step + 1, v0 + 2 * i + ((c + 1) // G + 1))
                    w1 = (c - 1, step - 1, v0 + 2 * i + ((c - 1) // G + 1))
                    scores(c, step, 0)
                    if c + 1 < STEPS:
                        smax(*n1, 0)
                    scores(c, step, 1)
                    if c + 1 < STEPS:
                        smax(*n1, 1)
                    if c > 0:
                        weigh(*w1)
                    if c + 3 < STEPS:
                        pj(c + 3, i, (0,))
                    if c + 1 < STEPS:
                        turn_max(c + 1, step + 1)
                    if c + 3 < STEPS:
                        pj(c + 3, i, (1,))
                    if c > 0:
                        group(step - 1)
                    if c + 2 < STEPS and (c + 2) % G == 0:
                        proj_v(c + 2, step + 2, wv)

                pj(0, 0)
                proj_v(0, s0, wv)
                pj(1, 0)
                smax(0, s0, v0 + 1, 0)
                smax(0, s0, v0 + 1, 1)
                pj(2, 0)
                turn_max(0, s0)
                for c in range(3):
                    turn(c, 0)
                with pe.Fori(0, 3) as i:
                    for c in range(3, 9):
                        turn(c, i)
                for c in range(21, STEPS):
                    turn(c, 0)
                weigh(STEPS - 1, s0 + STEPS - 1, v0 + B)
                group(s0 + STEPS - 1)

            def linear(w0, w1, x0, x1, done, ready=None):
                for c in range(NCH):
                    cs = slice(CH * c, CH * c + CH)
                    if ready:
                        name, at, per = ready
                        pe.wait_ge(s[name], at + per * c)
                    for k, (lo, n) in enumerate(((0, 128), (128, C1))):
                        pe.matmul(PS[0:n, 2 * c + k, :], w0[:, lo:lo + n], x0[:, cs], start=True, stop=False)
                        pe.matmul(PS[0:n, 2 * c + k, :], w1[:, lo:lo + n], x1[:, cs], start=False, stop=True)\
                          .then_inc(s[done], 1)

            def layer_norm(x0, x1, n, src_ready=None):
                def spread(c):
                    pe.wait_ge(s["ln_inv"], n * NCH + c + 1)
                    for q in range(4):
                        last = pe.matmul(PS[:, 4 + c, 128 * q:128 * q + 128], quarter[:, q], rstd[:, c, :], start=True, stop=True)
                    last.then_inc(s["ln_all"], 1)

                def means(c):
                    cs = slice(CH * c, CH * c + CH)
                    if src_ready:
                        name, at, per = src_ready
                        pe.wait_ge(s[name], at + per * c)
                    pe.matmul(PS[:, c, :], mean_w[:], x0[:, cs], start=True, stop=False)
                    pe.matmul(PS[:, c, :], mean_w[0:C1, :], x1[0:C1, cs], start=False, stop=True).then_inc(s["lnm_ps"], 1)

                def variances(c):
                    pe.wait_ge(s["ln_sq"], 2 * (n * NCH + c + 1))
                    for k, rows_k in enumerate((128, C1)):
                        for q in range(4):
                            last = pe.matmul(PS[32 * q:32 * q + 32, 4 + c, 0:128], mean_w[0:rows_k, 0:32],
                                             sq[0:rows_k, c % 2, k, 128 * q:128 * q + 128], start=k == 0, stop=k == 1,
                                             skip_group_check=True)
                    last.then_inc(s["lnv_ps"], 1)

                means(0)
                means(1)
                means(2)
                variances(0)
                means(3)
                variances(1)
                spread(0)
                variances(2)
                spread(1)
                variances(3)
                spread(2)
                spread(3)

            pe.wait_ge(s["tok_in"], TOK_IN)
            pe.wait_ge(s["dve_set"], DVE_SETS)
            pe.wait_ge(s["pool_set"], MEMSETS)
            with pe.Fori(0, LAYERS) as l:
                attention(l * STEPS, l * B, l * B, [(tok_wq, 0)], [(tok_wk, 0)], [(tok_wv, 1)])
                linear(tok_wf0, tok_wf1, hT0, hT1, "ffn_ps", ("bn1_done", l * (2 * NCH) + 2, 2))

            pe.wait_ge(s["weights_in"], WEIGHTS_IN)
            layer_norm(hT0, hT1, 0, ("h_ready", LAYERS * 2 * NCH + 2, 2))
            IN0 = 2 * B * LAYERS
            PAIRS = H // 2

            def rf_proj_qk(b, g, bank):
                for k, (wa, wb) in enumerate(((rf_wq0, rf_wq1), (rf_wk0, rf_wk1))):
                    pe.matmul(PS[:, bank, S * k:S * k + S], wa[:, g].rearrange("c j d -> c (j d)"), in0[:, 0, :],
                              start=True, stop=False)
                    last = pe.matmul(PS[:, bank, S * k:S * k + S], wb[:, g].rearrange("c j d -> c (j d)"),
                                     in1[0:C1, 0, :], start=False, stop=True)
                last.then_inc(s["rf_qk"], 1)

            def rf_values():
                for t in range(QT_):
                    ts = slice(128 * t, 128 * t + 128)
                    pe.matmul(PS[:, 7, D * t:D * t + D], in0[:, 0, ts], rf_wv0[:], start=True, stop=False)
                    last = pe.matmul(PS[:, 7, D * t:D * t + D], in1[0:C1, 0, ts], rf_wv1[:], start=False, stop=True)
                last.then_inc(s["rf_v"], 1)

            def rf_squares():
                for g in range(G):
                    last = pe.matmul(PS[32 * g:32 * g + 32, 6, :], head_half[:], SQ[:, g].rearrange("p k q -> p (k q)"),
                                     start=True, stop=True, skip_group_check=True)
                last.then_inc(s["rf_diag"], 1)

            def rf_turn_squares(b):
                pe.wait_ge(s["rf_dgT_ev"], b + 1)
                for n in range(2 * QT_):
                    last = pe.transpose(PS[:, 4, 96 * n:96 * n + 96], diagT[:, 128 * n:128 * n + 128], ident[0:96, 0:96])
                last.then_inc(s["rf_dgT"], 1)

            def rf_features(k):
                for t in range(QT_):
                    for g in range(G):
                        blk = G * t + g
                        last = pe.matmul(PS[:, 3 * (1 - k) + blk // 2, S * (blk % 2):S * (blk % 2) + S],
                                         QK[:, g, k, 128 * t:128 * t + 128], rf_proj[:].rearrange("p j m -> p (j m)"),
                                         start=True, stop=True)
                last.then_inc(s["rf_dd"], 1)

            def rf_turn(b, more):
                pe.wait_ge(s["rf_fmax"], b + 1)
                for t in range(QT_):
                    last = pe.transpose(PS[0:H, 6, 128 * t:128 * t + 128], fmax[:, 1, t, :], ident[:])
                last.then_inc(s["rf_stT"], 1)
                pe.wait_ge(s["rf_std"], b + 1)
                pe.matmul(PS[:, 6, 256:256 + H], ones12[:], stab_d[:], start=True, stop=True).then_inc(s["rf_stb"], 1)
                pe.wait_ge(s["rf_yev"], b * 2 + 1)
                if more:
                    pe.wait_ge(s["in_ready"], b * 2 + IN0 + 4)
                    rf_proj_qk(b, 0, 7)
                pe.wait_ge(s["rf_stbev"], b + 1)
                if more:
                    rf_proj_qk(b, 1, 6)
                    pe.wait_ge(s["rf_qkev"], b * 6 + 8)
                    rf_proj_qk(b, 2, 7)
                    pe.wait_ge(s["rf_qkev"], b * 6 + 10)
                pe.wait_ge(s["rf_vev"], b + 1)
                pe.wait_ge(s["rf_eps"], b + 1)
                for blk in range(2 * PAIRS // 4):
                    for t, k in [(t, k) for t in range(QT_) for k in range(4)]:
                        n, p, r = 4 * blk + k, (4 * blk + k) % PAIRS, 32 * k
                        last = pe.matmul(PS[r:r + 32, 6, 128 * blk:128 * blk + 128],
                                         VB[:, t, 32 * p:32 * p + 32] if n < PAIRS else ones[:, 0:32],
                                         KP[:, t, 2 * p:2 * p + 2, :].rearrange("p h m -> p (h m)"),
                                         start=t == 0, stop=t == QT_ - 1, skip_group_check=True)
                last.then_inc(s["rf_ctT"], 1)
                if more:
                    pe.wait_ge(s["rf_qkev"], b * 6 + 12)
                    rf_values()
                pe.wait_ge(s["rf_exp"], b * 2 + 2)
                for g in range(G):
                    for n in range(4):
                        p, t = 2 * g + n // 2, n % 2
                        last = pe.transpose(PS[:, g, 128 * n:128 * n + 128],
                                            QP[:, t, 2 * p:2 * p + 2, :].rearrange("p h m -> p (h m)"), ident[:])
                    last.then_inc(s["rf_qpT"], 1)
                pe.wait_ge(s["rf_ctTev"], b + 1)
                if more:
                    rf_squares()
                for n in range(3):
                    last = pe.transpose(PS[:, 3, 128 * n:128 * n + 128], CT[:, 128 * n:128 * n + 128], ident[:])
                last.then_inc(s["rf_ctx"], 1)
                if more:
                    rf_turn_squares(b + 1)
                    pe.wait_ge(s["rf_vev"], b + 2)
                pe.wait_ge(s["rf_ctxev"], b * 2 + 2)
                pe.wait_ge(s["rf_qpTev"], b * 3 + 3)
                for n in range(2 * PAIRS):
                    p, item = n % PAIRS, (n + PAIRS) % (2 * PAIRS)
                    last = pe.matmul(PS[32 * (p % 4):32 * (p % 4) + 32, 6 if n < PAIRS else 7, S * (p // 4):S * (p // 4) + S],
                                     CTX[:, item].rearrange("p h d -> p (h d)"), QPT[:, p].rearrange("p t n -> p (t n)"),
                                     start=True, stop=True, skip_group_check=True)
                last.then_inc(s["rf_out"], 1)
                if more:
                    rf_features(1)
                    pe.wait_ge(s["rf_diagev"], b + 2)
                    rf_features(0)
                pe.wait_ge(s["rf_o"], b * 2 + 2)
                for k, (lo, n) in enumerate(((0, 128), (128, C1))):
                    pe.matmul(PS[0:n, 7, S * k:S * k + S], rf_wo0[:, lo:lo + n], obT0[:], start=True, stop=False)
                    last = pe.matmul(PS[0:n, 7, S * k:S * k + S], rf_wo1[:, lo:lo + n], obT1[:], start=False, stop=True)
                last.then_inc(s["rf_y"], 1)

            pe.wait_ge(s["in_ready"], IN0 + 2)
            for g, bank in enumerate((7, 6, 5)):
                rf_proj_qk(0, g, bank)
            pe.wait_ge(s["rf_qkev"], 6)
            rf_values()
            rf_squares()
            rf_turn_squares(0)
            rf_features(1)
            pe.wait_ge(s["rf_diagev"], 1)
            rf_features(0)
            with pe.Fori(0, B - 1) as b:
                rf_turn(b, True)
            rf_turn(B - 1, False)

            per = 2 * B // NCH
            layer_norm(hT0, hT1, 1, ("rf_done", 1 + per, per))
            layer_norm(xT0, xT1, 2, ("ln_norm", 2 * NCH + 2, 2))
            pe.wait_ge(s["ln_aff"], 2 * NCH)
            attention(LAYERS * STEPS, B * LAYERS + B, B * LAYERS, [(ff_wq0, 0), (ff_wq1, 1)], [(ff_wk0, 0), (ff_wk1, 1)],
                      [(ff_wv0, 0), (ff_wv1, 1)])
            per = STEPS // NCH
            linear(ff_wp0, ff_wp1, oT0, oT1, "xp_ps", ("o_done", LAYERS * STEPS + per, per))
            layer_norm(xT0, xT1, 3, ("x2_done", 2, 2))
            pe.wait_ge(s["moe_in"], 16 * (len(moe) + len(late)))
            for c in range(NCH):
                cs = slice(CH * c, CH * c + CH)
                pe.wait_ge(s["ln_aff"], 2 * (NCH + c + 1))
                pe.matmul(PS[0:E, c, :], gate0[:], nT0[:, cs], start=True, stop=False)
                pe.matmul(PS[0:E, c, :], gate1[:], nT1[0:C1, cs], start=False, stop=True).then_inc(s["lg_ps"], 1)
            pe.wait_ge(s["lg_ev"], NCH)
            for t in range(NT):
                last = pe.transpose(PS[:, 4, E * t:E * t + E], lgT[:, 128 * t:128 * t + 128], ident[0:E, 0:E])
            last.then_inc(s["lgT_ps"], 1)
            pe.wait_ge(s["res_done"], 2)

            def turn_x(t):
                if t >= 2:
                    pe.wait_ge(s["xr_ev"], 2 * (t - 1))
                for k, (x0, x1) in enumerate(((nT0, nT1), (hT0, hT1))):
                    ts, at = slice(128 * t, 128 * t + 128), D * k
                    pe.transpose(PS[:, 5 + t % 2, at:at + 128], x0[:, ts], ident[:])
                    last = pe.transpose(PS[:, 5 + t % 2, at + 128:at + D], x1[0:C1, ts], ident[0:C1, 0:C1])
                last.then_inc(s["xr_ps"], 1)

            for t in range(NT // 2):
                turn_x(t)
            pe.wait_ge(s["picks_done"], 1)
            picks = gt[:, 2].rearrange("p t e -> p (t e)")
            pe.matmul(PS[:, 7, 0:NT * E], upper[:], picks, start=True, stop=True)
            pe.matmul(PS[:, 7, NT * E:2 * NT * E], ones[:], picks, start=True, stop=True).then_inc(s["count_ps"], 1)
            for t in range(NT // 2, NT):
                turn_x(t)
            pe.wait_ge(s["xr_ev"], 2 * NT)
            for g in range(TK * NT // 4):
                pe.wait_ge(s["in_row_set"], g + 1)
                for n in range(4 * g, 4 * g + 4):
                    k, t = n // NT, n % NT
                    last = pe.matmul(PS[:, 4, 0:2 * TILES], in_row[:, g % 2, n % 4, :],
                                     in_tile[k][:, t].rearrange("p a n -> p (a n)"), start=n == 0, stop=n == TK * NT - 1)
                last.then_inc(s["in_row_used"], 1)

            def turn_tile(n, c, i):
                pe.wait_ge(tile_in[c % UN], i * 16 + 16 * (c // UN + 1))
                pe.wait_ge(s["xt_ev"], n * 2 + 2)
                x = XL[:, c % UN, :]
                pe.transpose(PS[:, 4 + c % 2, 0:128], x[:, 0:128], ident[:])
                pe.transpose(PS[0:C1, 4 + c % 2, 128:256], x[:, 128:D], ident[:]).then_inc(s["xt_ps"], 1)

            def up(n, c):
                pe.wait_ge(s["w1_in"], n * 4 + 4)
                pe.wait_ge(s["xt_ev"], n * 2 + 6)
                pe.wait_ge(s["hid_ready"], n * HT + HT)
                for m in range(HT):
                    o = PS[:, 2 * (c % 2) + m // 3, 128 * (m % 3):128 * (m % 3) + 128]
                    w = W1S[c % 2]
                    pe.matmul(o, w[:, 0, 128 * m:128 * m + 128], XT[:, c % 2, 0], start=True, stop=False)
                    last = pe.matmul(o, w[0:C1, 1, 128 * m:128 * m + 128], XT[0:C1, c % 2, 1], start=False, stop=True)
                    if m % 3 == 2:
                        last.then_inc(s["l1_ps"], 1)

            def down(n, c):
                e = pe.value_load(tile_e[0:1, bass.ds(n, 1)], min_val=0, max_val=E - 1)
                pe.wait_ge(s["hid_ready"], n * HT + 3 * HT)
                pe.wait_ge(s["y_scaled"], n + 1)
                for m in range(HT):
                    last = pe.matmul(PS[:, 6 + c % 2, 0:D], HD_[:, c % 2, m], w2_s[:, bass.ds(e, 1), m, :],
                                     start=m == 0, stop=m == HT - 1)
                last.then_inc(s["y_ps"], 1)

            pe.wait_ge(s["tile_e_done"], 1)
            turn_tile(0, 0, 0)
            up(0, 0)
            turn_tile(1, 1, 0)

            def step(n, c, i):
                if not (isinstance(n, int) and n + 1 >= TILES):
                    up(n + 1, c + 1)
                if not (isinstance(n, int) and n + 2 >= TILES):
                    turn_tile(n + 2, c + 2, i)
                down(n, c)

            with pe.Fori(0, TURNS) as i:
                for c in range(UN):
                    step(i * UN + c, c, i)
            for n in range(UN * TURNS, TILES):
                step(n, n % UN, n // UN)

        @block.scalar
        def _(act):
            act.sem_inc(s["hid_ready"], 2 * HT)
            act.sem_inc(s["rf_yev"], 1)
            act.sem_inc(s["xt_ev"], 4)
            act.wait_ge(s["dve_set"], DVE_SETS)
            for b in range(B):
                act.wait_ge(s["emb_ps"], b + 1)
                nc.scalar.copy(hT0[:, S * b:S * b + S], PS[:, 2 * (b % 4), 0:S]).then_inc(s["emb_ev"], 1)
                nc.scalar.copy(hT1[0:C1, S * b:S * b + S], PS[0:C1, 2 * (b % 4) + 1, 0:S]).then_inc(s["emb_ev"], 1)

            def exps(c, step, h, scale):
                act.wait_ge(s["st_ps"], 2 * step + (h + 1))
                nc.scalar.activation(P[:, 2 * (c % 2) + h].rearrange("p j t q -> p (j t q)"),
                                     PS[:, 2 * h:2 * h + 2, :].rearrange("p b q -> p (b q)"), ACT.Exp,
                                     scale=scale).then_inc(s["p_ready"], 1)

            def queries(c, step, func, qb):
                act.wait_ge(s["proj_ps"], step + 1)
                nc.scalar.activation(QT[:, c % 3, :], PS[:, 6, 0:S], func, bias=qb[:, c % G:c % G + 1])\
                    .then_inc(s["qkv_ev"], 1)

            def keys(c, func, kb):
                for j in range(J):
                    r = slice(32 * j, 32 * j + 32)
                    nc.scalar.activation(KM[r, c % 3, j, :], PS[r, 6, S:2 * S], func, bias=kb[r, c % G:c % G + 1])\
                      .then_inc(s["qkv_ev"], 1)

            def batch_values(c, batch, func):
                act.wait_ge(s["v_ps"], batch)
                v = VA[:, (c // G) % 2].rearrange("p t g j d -> p (t g j) d")
                nc.scalar.activation(v[:, :, 0:HD], PS[:, 5, 0:QT_ * D].rearrange("p (n d) -> p n d", d=HD), func)\
                  .then_inc(s["v_ev"], 1)

            def values(step):
                act.wait_ge(s["av_ps"], step + 1)
                nc.scalar.copy(av, PS[:, 7, 0:S]).then_inc(s["av_ev"], 1)

            def attention(s0, v0, func, qb, kb, scale):
                def turn(c, i):
                    step = s0 + 6 * i + c
                    exps(c, step, 0, scale)
                    exps(c, step, 1, scale)
                    if c > 0:
                        values(step - 1)
                    if c + 3 < STEPS:
                        queries(c + 3, step + 3, func, qb)
                        keys(c + 3, func, kb)
                    if c + 2 < STEPS and (c + 2) % G == 0:
                        batch_values(c + 2, v0 + 2 * i + ((c + 2) // G + 1), func)

                queries(0, s0, func, qb)
                keys(0, func, kb)
                batch_values(0, v0 + 1, func)
                for c in (1, 2):
                    queries(c, s0 + c, func, qb)
                    keys(c, func, kb)
                for c in range(3):
                    turn(c, 0)
                with act.Fori(0, 3) as i:
                    for c in range(3, 9):
                        turn(c, i)
                for c in range(21, STEPS):
                    turn(c, 0)
                values(s0 + STEPS - 1)

            def layer_norm(y0, y1, n, aff=None):
                for c in range(NCH):
                    cs = slice(CH * c, CH * c + CH)
                    act.wait_ge(s["ln_cent"], 2 * (n * NCH + c + 1))
                    if c >= 2:
                        act.wait_ge(s["lnv_ps"], n * NCH + c - 1)
                    nc.scalar.activation(sq[:, c % 2, 0, :], y0[:, cs], ACT.Square).then_inc(s["ln_sq"], 1)
                    nc.scalar.activation(sq[0:C1, c % 2, 1, :], y1[0:C1, cs], ACT.Square).then_inc(s["ln_sq"], 1)
                def affine(c):
                    cs = slice(CH * c, CH * c + CH)
                    act.wait_ge(s["ln_norm"], 2 * (n * NCH + c + 1))
                    nc.scalar.activation(y0[:, cs], y0[:, cs], ACT.Identity, bias=ln_b[:, aff, 0:1],
                                         scale=ln_g[:, aff, 0:1]).then_inc(s["ln_aff"], 1)
                    nc.scalar.activation(y1[0:C1, cs], y1[0:C1, cs], ACT.Identity, bias=ln_b[0:C1, aff, 1:2],
                                         scale=ln_g[0:C1, aff, 1:2]).then_inc(s["ln_aff"], 1)

                for c in range(NCH):
                    act.wait_ge(s["lnv_ps"], n * NCH + c + 1)
                    nc.scalar.activation(rstd[:, c, :], PS[:, 4 + c, 0:128], ACT.Sqrt, bias=eps_t[:, 0:1])\
                      .then_inc(s["ln_root"], 1)
                    if aff is not None and c >= 2:
                        affine(c - 2)
                if aff is not None:
                    affine(NCH - 2)
                    affine(NCH - 1)

            act.wait_ge(s["tok_in"], TOK_IN)
            act.wait_ge(s["pool_set"], MEMSETS)
            with act.Fori(0, LAYERS) as l:
                attention(l * STEPS, l * B, ACT.Relu, tok_qb, tok_kb, float(D) ** -0.5)
                for n in range(2):
                    act.wait_ge(s["bn_var"], l * 4 + 2 * (n + 1))
                    nc.scalar.activation(bn_s[:, 2, :], mv[:, :, 1], ACT.Sqrt, bias=eps_t[:, 0:1])\
                      .then_inc(s["bn_root"], 1)

            act.wait_ge(s["weights_in"], WEIGHTS_IN)
            layer_norm(nT0, nT1, 0)

            def rf_qk(b, g, bank):
                act.wait_ge(s["rf_qk"], b * G + (g + 1))
                for dst, func in ((QK, ACT.Copy), (SQ, ACT.Square)):
                    nc.scalar.activation(dst[:, g].rearrange("p k q -> p (k q)"), PS[:, bank, :], func,
                                         scale=float(HD) ** -0.25).then_inc(s["rf_qkev"], 1)

            def rf_values(b):
                act.wait_ge(s["rf_v"], b + 1)
                nc.scalar.copy(VB, PS[:, 7, 0:QT_ * D].rearrange("p (t d) -> p t d", t=QT_)).then_inc(s["rf_vev"], 1)

            def rf_squares(b):
                act.wait_ge(s["rf_diag"], b + 1)
                nc.scalar.copy(diagT, PS[0:32 * G, 6, :]).then_inc(s["rf_dgT_ev"], 1)

            def rf_exp(b, k, X):
                act.wait_ge(s["rf_sub"], b * 2 + (k + 1))
                v = X.rearrange("p t h m -> p (t h m)")
                nc.scalar.activation(v, v, ACT.Exp).then_inc(s["rf_exp"], 1)

            def rf_turn(b, more):
                if more:
                    rf_qk(b + 1, 0, 7)
                rf_exp(b, 0, KP)
                if more:
                    rf_qk(b + 1, 1, 6)
                    rf_qk(b + 1, 2, 7)
                rf_exp(b, 1, QP)
                act.wait_ge(s["rf_ctT"], b + 1)
                nc.scalar.copy(CT, PS[:, 6, 0:384]).then_inc(s["rf_ctTev"], 1)
                if more:
                    rf_values(b + 1)
                for g in range(G):
                    act.wait_ge(s["rf_qpT"], b * 3 + (g + 1))
                    nc.scalar.activation(QPT[:, 2 * g:2 * g + 2].rearrange("p q t n -> p (q t n)"), PS[:, g, :],
                                         ACT.Identity, bias=rf_eps_t[:, 0:1])\
                      .then_inc(s["rf_qpTev"], 1)
                if more:
                    rf_squares(b + 1)
                act.wait_ge(s["rf_ctx"], b + 1)
                for k in range(2):
                    r = slice(64 * k, 64 * k + 64)
                    nc.scalar.copy(CTX[r, :, k, :], PS[r, 3, 0:384].rearrange("p (n h d) -> p n h d", h=2, d=HD)[:, :, k, :])\
                      .then_inc(s["rf_ctxev"], 1)
                act.wait_ge(s["rf_y"], b + 1)
                act.wait_ge(s["rf_done"], b * 2 + 1)
                for k, n in enumerate((128, C1)):
                    nc.scalar.copy(yT[0:n, S * k:S * k + S], PS[0:n, 7, S * k:S * k + S]).then_inc(s["rf_yev"], 1)

            for g, bank in enumerate((7, 6, 5)):
                rf_qk(0, g, bank)
            rf_values(0)
            rf_squares(0)
            with act.Fori(0, B - 1) as b:
                rf_turn(b, True)
            rf_turn(B - 1, False)

            layer_norm(xT0, xT1, 1)
            layer_norm(nT0, nT1, 2, 0)
            attention(LAYERS * STEPS, LAYERS * B, ACT.Identity, ff_qb, ff_kb, float(HD) ** -0.5)
            layer_norm(nT0, nT1, 3, 1)
            for c in range(NCH):
                act.wait_ge(s["lg_ps"], c + 1)
                nc.scalar.copy(lgT[:, CH * c:CH * c + CH], PS[0:E, c, :]).then_inc(s["lg_ev"], 1)

            def turned_x(t):
                act.wait_ge(s["xr_ps"], t + 1)
                nc.scalar.copy(XR[:, t, :], PS[:, 5 + t % 2, 0:D]).then_inc(s["xr_ev"], 1)
                nc.scalar.copy(rows[:, t, :], PS[:, 5 + t % 2, D:2 * D]).then_inc(s["xr_ev"], 1)

            act.wait_ge(s["lgT_ps"], 1)
            for t in range(2):
                turned_x(t)
            act.wait_ge(s["gate_arg"], 1)
            nc.scalar.activation(gs[:, 2, :], gs[:, 2, :], ACT.Exp).then_inc(s["gate_exp"], 1)
            for t in range(2, NT):
                turned_x(t)

            def turned(n, c):
                act.wait_ge(s["xt_ps"], n + 3)
                nc.scalar.copy(XT[:, c % 2, 0], PS[:, 4 + c % 2, 0:128]).then_inc(s["xt_ev"], 1)
                nc.scalar.copy(XT[0:C1, c % 2, 1], PS[0:C1, 4 + c % 2, 128:256]).then_inc(s["xt_ev"], 1)

            def hidden(n, c):
                for m in range(HT):
                    if m % 3 == 0:
                        act.wait_ge(s["l1_ps"], n * 2 + (m // 3 + 1))
                    if m == 0:
                        act.wait_ge(s["y_ps"], n + 1)
                    nc.scalar.activation(HD_[:, c % 2, m], PS[:, 2 * (c % 2) + m // 3, 128 * (m % 3):128 * (m % 3) + 128],
                                         ACT.Gelu, bias=B1S[:, c % 2, m:m + 1]).then_inc(s["hid_ready"], 1)

            act.wait_ge(s["xr_ps"], NT)
            turned(0, 0)
            hidden(0, 0)
            turned(1, 1)

            def step(n, c):
                if not (isinstance(n, int) and n + 1 >= TILES):
                    hidden(n + 1, c + 1)
                if not (isinstance(n, int) and n + 2 >= TILES):
                    turned(n + 2, c + 2)

            with act.Fori(0, TURNS) as i:
                for c in range(UN):
                    step(i * UN + c, c)
            for n in range(UN * TURNS, TILES):
                step(n, n % UN)

        @block.vector
        def _(dve):
            dve.sem_inc(s["y_scaled"], 2)
            ch = Chain(dve, s["dve_step"])
            tt, ts_, stt = nc.vector.tensor_tensor, nc.vector.tensor_scalar, nc.vector.scalar_tensor_tensor

            for t in zeroed[0:TOK_ZEROED]:
                nc.vector.memset(t[:], 0.0).then_inc(s["dve_set"], 1)
            dve.wait_ge(s["idx_in"], 16)
            ch.link(ts_(idx_b[:], tok_idx[:], 0, V, ALU.is_lt, ALU.mult))
            ch.link(tt(idx_b[:], idx_b[:], tok_idx[:], ALU.add))
            ts_(idx_a[:], idx_b[:], 0, V - 1, ALU.max, ALU.min).then_inc(s["idx_ready"], 1)
            for t in zeroed[TOK_ZEROED:]:
                nc.vector.memset(t[:], 0.0).then_inc(s["dve_set"], 1)
            for t in (hT1, nT1):
                nc.vector.memset(t[C1:, :], 1.0).then_inc(s["dve_set"], 1)
            dve.wait_ge(s["const_in"], 16 * len(consts))
            ch.link(nc.vector.tensor_copy(ident_b[:], ident[:]))
            for b in range(B):
                dve.wait_ge(rows_in[b], 32)
                r = rows[:, QT_ * b:QT_ * b + QT_, :]
                if b > 0:
                    dve.wait_ge(s["emb_sum"], b)
                ch.link(tt(ob[:], r, pos[:], ALU.add))
                tt(r, r, ob[:], ALU.add).then_inc(s["emb_sum"], 1)
            dve.wait_ge(s["emb_ev"], 2 * B)
            dve.sem_inc(s["h_ready"], 2 * NCH)

            def maxima(c, step):
                for j in range(J):
                    dve.wait_ge(s["smax_ps"], 4 * step + (j + 1))
                    nc.vector.tensor_reduce(rmax[:, :, j, HD], PS[:, 4 + j % 2, :].rearrange("p (t k) -> p t k", t=QT_),
                                            AX, ALU.max).then_inc(s["smax_red"], 1)
                dve.wait_ge(s["mT_ps"], step + 1)
                tt(QT[:, c % 3, :], QT[:, c % 3, :], PS[:, 4, :].bitcast(BF16)[:, 0:S], ALU.subtract)\
                    .then_inc(s["aug_done"], 1)

            def normalise(c, step, b, add):
                g = c % G
                lo, cols = 64 * (g % 2), bass.ds(b * S, S)
                rs = slice(lo, lo + 64)
                dve.wait_ge(s["regrouped"], step + 1)
                ch.link(nc.vector.reciprocal(rsum[0:64, :], PS[64:128, 7, S:2 * S]))
                if add:
                    dst = (hT0, hT1)[g // 2][rs, cols]
                    ch.link(tt(on[rs, :], PS[0:64, 7, S:2 * S], rsum[0:64, :], ALU.mult))
                    tt(dst, dst, on[rs, :], ALU.add).then_inc(s["o_done"], 1)
                else:
                    tt((oT0, oT1)[g // 2][rs, cols], PS[0:64, 7, S:2 * S], rsum[0:64, :], ALU.mult).then_inc(s["o_done"], 1)

            def copy_first(src0, src1, name, value):
                dve.wait_ge(s[name], value)
                nc.vector.tensor_copy(in0[:, 0, :], src0[:, 0:S]).then_inc(s["in_ready"], 1)
                nc.vector.tensor_copy(in1[:, 0, :], src1[:, 0:S]).then_inc(s["in_ready"], 1)

            def attention(s0, add):
                def turn(c, i):
                    step = s0 + 6 * i + c
                    if c + 1 < STEPS:
                        maxima(c + 1, step + 1)
                    if c > 0:
                        normalise(c - 1, step - 1, 2 * i + (c - 1) // G, add)
                    if add and c > G and c % G == 1:
                        b = 2 * i + (c // G - 1)
                        dve.wait_ge(s["o_done"], step - 1)
                        part_stats(bass.ds(b, 1), bass.ds(b * S, S))

                maxima(0, s0)
                for c in range(3):
                    turn(c, 0)
                per = 16 if add else 6
                with dve.Fori(0, 3) as i:
                    mark = ch.enter(i, per)
                    for c in range(3, 9):
                        turn(c, i)
                    ch.leave(mark, 3)
                for c in range(21, STEPS):
                    turn(c, 0)
                normalise(STEPS - 1, s0 + STEPS - 1, B - 1, add)

            def part_stats(k, cs):
                ch.put(nc.vector.bn_stats(stats[:, 0, k, :], hT0[:, cs]))
                ch.put(nc.vector.bn_stats(stats[0:C1, 1, k, :], hT1[0:C1, cs]))

            def batch_norm(n, parts, done, roots):
                ch.wait()
                ch.put(nc.vector.memset(mv[C1:, 1, :], 0.0))
                nc.vector.bn_aggr(mv[:, 0, :], stats[:, 0, 0:parts].rearrange("p c k -> p (c k)")).then_inc(s["bn_var"], 1)
                nc.vector.bn_aggr(mv[0:C1, 1, :], stats[0:C1, 1, 0:parts].rearrange("p c k -> p (c k)")).then_inc(s["bn_var"], 1)
                scale, shift, part = bn_s[:, 0, :], bn_s[:, 1, :], bn_s[:, 2, :]
                dve.wait_ge(s["bn_root"], roots)
                ch.link(nc.vector.reciprocal(part, part))
                ch.link(tt(scale, part, bn_g[:, n, :], ALU.mult))
                ch.link(tt(part, mv[:, :, 0], scale, ALU.mult))
                ch.link(tt(shift, bn_b[:, n, :], part, ALU.subtract))
                for c in range(NCH):
                    for k, (x, rows_k) in enumerate(((hT0, 128), (hT1, C1))):
                        v = x[0:rows_k, CH * c:CH * c + CH]
                        ts_(v, v, bn_s[0:rows_k, 0, k:k + 1], bn_s[0:rows_k, 1, k:k + 1], ALU.mult, ALU.add)\
                            .then_inc(s[done], 1)

            def layer_norm(x0, x1, y0, y1, n, first_chunk=None):
                for c in range(NCH):
                    cs = slice(CH * c, CH * c + CH)
                    dve.wait_ge(s["lnm_ps"], n * NCH + c + 1)
                    tt(y0[:, cs], x0[:, cs], PS[:, c, :], ALU.subtract).then_inc(s["ln_cent"], 1)
                    tt(y1[0:C1, cs], x1[0:C1, cs], PS[0:C1, c, :], ALU.subtract).then_inc(s["ln_cent"], 1)
                def invert(c):
                    dve.wait_ge(s["ln_root"], n * NCH + c + 1)
                    nc.vector.reciprocal(rstd[:, c, :], rstd[:, c, :]).then_inc(s["ln_inv"], 1)

                invert(0)
                for c in range(NCH):
                    cs = slice(CH * c, CH * c + CH)
                    if c + 1 < NCH:
                        invert(c + 1)
                    dve.wait_ge(s["ln_all"], n * NCH + c + 1)
                    tt(y0[:, cs], y0[:, cs], PS[:, 4 + c, :], ALU.mult).then_inc(s["ln_norm"], 1)
                    tt(y1[0:C1, cs], y1[0:C1, cs], PS[0:C1, 4 + c, :], ALU.mult).then_inc(s["ln_norm"], 1)
                    if first_chunk and c == NCH - 2:
                        first_chunk()

            dve.wait_ge(s["tok_in"], TOK_IN)
            dve.wait_ge(s["pool_set"], MEMSETS)
            with dve.Fori(0, LAYERS) as l:
                mark = ch.enter(l, LAYER_LINKS)
                copy_first(hT0, hT1, "h_ready", l * (2 * NCH) + 2)
                attention(l * STEPS, True)
                dve.wait_ge(s["o_done"], l * STEPS + STEPS)
                part_stats(B - 1, slice(S * (B - 1), T))
                batch_norm(0, B, "bn1_done", l * 2 + 1)
                for c in range(NCH):
                    cs = slice(CH * c, CH * c + CH)
                    dve.wait_ge(s["ffn_ps"], l * (2 * NCH) + (2 * c + 2))
                    for k, (x, n) in enumerate(((hT0, 128), (hT1, C1))):
                        ch.put(tt(x[0:n, cs], x[0:n, cs], PS[0:n, 2 * c + k, :], ALU.add))
                    ch.wait()
                    part_stats(c, cs)
                batch_norm(1, NCH, "h_ready", l * 2 + 2)
                ch.leave(mark, LAYERS)

            dve.wait_ge(s["h_ready"], (LAYERS + 1) * 2 * NCH)
            layer_norm(hT0, hT1, nT0, nT1, 0)
            dd = [PS[:, 3 * (1 - k):3 * (1 - k) + 3, :].rearrange("p b (h m) -> p (b h) m", m=M) for k in range(2)]
            flat = [fmax[:, k].rearrange("p t h -> p (t h)") for k in range(2)]
            sub = [fsub[:, k].rearrange("p t h -> p (t h)") for k in range(2)]

            def wide(v):
                return v[:, :, None].broadcast_to([128, QT_ * H, M])

            def rf_squares(b):
                dve.wait_ge(s["rf_dgT"], b + 1)
                nc.vector.tensor_copy(fsub[:].rearrange("p k t (g j) -> p (k t) g j", j=J),
                                      PS[:, 4, 0:384].rearrange("p (n g r) -> p n g r", g=G, r=32)[:, :, :, 0:J])\
                    .then_inc(s["rf_diagev"], 1)

            def rf_key_maxima(b):
                dve.wait_ge(s["rf_dd"], b * 2 + 1)
                nc.vector.tensor_reduce(flat[1], dd[1], AX, ALU.max).then_inc(s["rf_fmax"], 1)

            def rf_turn(b, more):
                dve.wait_ge(s["rf_stT"], b + 1)
                ch.link(nc.vector.tensor_reduce(stab[:], PS[0:H, 6, 0:S], AX, ALU.max))
                ts_(stab_d[:], ident[0:H, 0:H], stab[:, 0:1], None, ALU.mult).then_inc(s["rf_std"], 1)
                dve.wait_ge(s["rf_stb"], b + 1)
                tt(fsub[:, 1], fsub[:, 1], PS[:, 6, 256:256 + H][:, None, :].broadcast_to([128, QT_, H]), ALU.add)\
                    .then_inc(s["rf_stbev"], 1)
                dve.wait_ge(s["rf_stbev"], b + 1)

                def subtract(k, X):
                    tt(X.rearrange("p t h m -> p (t h) m"), dd[k], wide(sub[k]), ALU.subtract).then_inc(s["rf_sub"], 1)

                subtract(1, KP)
                dve.wait_ge(s["rf_dd"], b * 2 + 2)
                ch.link(nc.vector.tensor_reduce(flat[0], dd[0], AX, ALU.max))
                ch.link(tt(sub[0], flat[0], sub[0], ALU.add))
                dve.wait_ge(s["rf_exp"], b * 2 + 1)
                v = KP.rearrange("p t h m -> p (t h m)")
                ts_(v, v, RF_EPS, None, ALU.add).then_inc(s["rf_eps"], 1)
                subtract(0, QP)
                if more:
                    rf_squares(b + 1)
                dve.wait_ge(s["rf_out"], b + 1)
                parts = ((obT0, 128, slice(0, S)), (obT1, C1, slice(S, 2 * S)))
                for o, n, cs in parts:
                    nc.vector.reciprocal(rden[0:n, cs], PS[0:n, 6, cs]).then_inc(s["rf_den"], 1)
                dve.wait_ge(s["rf_den"], b * 2 + 2)
                for o, n, cs in parts:
                    tt(o, PS[0:n, 7, cs], rden[0:n, cs], ALU.mult).then_inc(s["rf_o"], 1)
                if more:
                    rf_key_maxima(b + 1)

            rf_squares(0)
            rf_key_maxima(0)
            with dve.Fori(0, B - 1) as b:
                mark = ch.enter(b, 3)
                rf_turn(b, True)
                ch.leave(mark, B - 1)
            rf_turn(B - 1, False)

            layer_norm(hT0, hT1, xT0, xT1, 1)
            dve.wait_ge(s["ln_norm"], 2 * 2 * NCH)
            layer_norm(xT0, xT1, nT0, nT1, 2, lambda: copy_first(nT0, nT1, "ln_aff", 2))
            attention(LAYERS * STEPS, False)
            for c in range(NCH):
                cs = slice(CH * c, CH * c + CH)
                dve.wait_ge(s["xp_ps"], 2 * c + 2)
                for k, (x, n) in enumerate(((xT0, 128), (xT1, C1))):
                    tt(x[0:n, cs], x[0:n, cs], PS[0:n, 2 * c + k, :], ALU.add).then_inc(s["x2_done"], 1)
            dve.wait_ge(s["x2_done"], 2 * NCH)
            layer_norm(xT0, xT1, nT0, nT1, 3)
            tt(hT0[:], hT0[:], xT0[:], ALU.add).then_inc(s["res_done"], 1)
            tt(hT1[0:C1, :], hT1[0:C1, :], xT1[:], ALU.add).then_inc(s["res_done"], 1)

            def by_token(v):
                return v[:, :, None].broadcast_to([128, NT, E])

            numbers = expert_no[:, None, :].broadcast_to([128, NT, E])
            dve.wait_ge(s["lgT_ps"], 1)
            ch.link(nc.vector.tensor_copy(lg.rearrange("p t e -> p (t e)"), PS[:, 4, 0:NT * E]))
            logits = lg
            for n in range(2):
                top, first, pick = gs[:, n, :], gs[:, 3, :], gt[:, 3 + n]
                ch.link(nc.vector.tensor_reduce(top, logits, AX, ALU.max))
                ch.link(tt(gt[:, 0], logits, by_token(top), ALU.is_equal))
                ch.link(stt(gt[:, 1], gt[:, 0], -float(2 * E), numbers, ALU.mult, ALU.add))
                ch.link(nc.vector.tensor_reduce(first, gt[:, 1], AX, ALU.min))
                ch.link(tt(pick, gt[:, 1], by_token(first), ALU.is_equal))
                if n == 0:
                    ch.link(stt(gt[:, 2], pick, -3e38, lg, ALU.mult, ALU.add))
                    logits = gt[:, 2]
            tt(gt[:, 2], gt[:, 3], gt[:, 4], ALU.add).then_inc(s["picks_done"], 1)
            tt(gs[:, 2, :], gs[:, 1, :], gs[:, 0, :], ALU.subtract).then_inc(s["gate_arg"], 1)
            for r in run:
                ch.put(nc.vector.memset(r, 0.0))
            ch.put(nc.vector.memset(erun[:], 0.0))
            dve.wait_ge(s["gate_exp"], 1)
            ch.link(ts_(gs[:, 4, :], gs[:, 2, :], 1.0, None, ALU.add))
            ch.link(nc.vector.reciprocal(gs[:, 4, :], gs[:, 4, :]))
            ch.link(tt(gs[:, 5, :], gs[:, 2, :], gs[:, 4, :], ALU.mult))

            dve.wait_ge(s["count_ps"], 1)
            inside, total = (PS[:, 7, k * NT * E:(k + 1) * NT * E].rearrange("p (t e) -> p t e", e=E) for k in range(2))
            ch.link(nc.vector.tensor_copy(run[0][:, 9:8 + NT, :], total[:, 0:NT - 1, :]))
            for k in range(4):
                x, y = run[k % 2], run[(k + 1) % 2]
                ch.link(tt(y[:, 8:8 + NT, :], x[:, 8:8 + NT, :], x[:, 8 - 2 ** k:8 + NT - 2 ** k, :], ALU.add))
            before = run[0][:, 8:8 + NT, :]
            ch.link(tt(count[:], before[:, NT - 1, :], total[:, NT - 1, :], ALU.add))
            ch.link(ts_(count[:], count[:], 1.0 / 128, None, ALU.mult))
            ch.link(tt(more, count[:, :, None].broadcast_to([128, E, NT]),
                       count_up[:, None, 0:NT].broadcast_to([128, E, NT]), ALU.is_gt))
            ch.link(nc.vector.tensor_reduce(erun[:, 0, 9:9 + E], more, AX, ALU.add))
            for k in range(3):
                x, y = erun[:, k % 2, :], erun[:, (k + 1) % 2, :]
                ch.link(tt(y[:, 8:9 + E], x[:, 8:9 + E], x[:, 8 - 2 ** k:9 + E - 2 ** k], ALU.add))
            first, end = erun[:, 1, 8:8 + E], erun[:, 1, 9:9 + E]
            ch.link(stt(gt[:, 2], first[:, None, :].broadcast_to([128, NT, E]), 128.0, before, ALU.mult, ALU.add))
            ch.link(tt(gt[:, 2], gt[:, 2], inside, ALU.add))
            ch.link(tt(gt[:, 0:2], gt[:, 3:5], gt[:, 2:3].broadcast_to([128, TK, NT, E]), ALU.mult))
            ch.link(nc.vector.tensor_reduce(gs[:, 0:2, :], gt[:, 0:2], AX, ALU.add))
            ch.link(nc.vector.tensor_copy(slot[:, 2], gs[:, 0:2, :]))
            ch.link(ts_(slot[:, 0], slot[:, 2], 127, None, ALU.bitwise_and))
            ch.link(ts_(slot[:, 1], slot[:, 2], 7, None, ALU.logical_shift_right))
            ch.link(nc.vector.tensor_copy(place, slot[:, 0:2]))
            ch.link(tt(told, end[0:1, None, :].broadcast_to([1, TILES, E]),
                       count_up[0:1, 0:TILES, None].broadcast_to([1, TILES, E]), ALU.is_le))
            ch.link(nc.vector.tensor_reduce(tile_f, told, AX, ALU.add))
            ts_(tile_e[:], tile_f, float(E - 1), None, ALU.min).then_inc(s["tile_e_done"], 1)

            dve.wait_ge(s["tile_e_done"], 1)
            for g in range(TK * NT // 4):
                k, t = 4 * g // NT, 4 * g % NT
                if t == 0:
                    v = in_tile[k]
                    if k == 1:
                        dve.wait_ge(s["xr_ps"], NT)
                    ch.link(tt(v[:, :, 1], count_up[:, None, 0:TILES].broadcast_to([128, NT, TILES]),
                               place[:, 1, k, :, None].broadcast_to([128, NT, TILES]), ALU.is_equal))
                    ch.link(tt(v[:, :, 0], v[:, :, 1], token_no[:, 0:NT, None].broadcast_to([128, NT, TILES]), ALU.mult))
                    ch.link(tt(v[:, :, 1], v[:, :, 1], gs[:, 4 + k, :, None].broadcast_to([128, NT, TILES]), ALU.mult))
                if g >= 2:
                    dve.wait_ge(s["in_row_used"], g - 1)
                tt(in_row[:, g % 2], count_up[:, None, :].broadcast_to([128, 4, 128]),
                   place[:, 0, k, t:t + 4, None].broadcast_to([128, 4, 128]), ALU.is_equal).then_inc(s["in_row_set"], 1)

            dve.wait_ge(s["in_row_used"], TK * NT // 4)
            numbers, gates = PS[:, 4, 0:TILES], PS[:, 4, TILES:2 * TILES]
            ch.link(ts_(none, numbers, 0.0, token_no[:, NT:NT + 1], ALU.is_equal, ALU.mult))
            stt(ids[:], numbers, -1.0, none, ALU.add, ALU.add).then_inc(s["ids_done"], 1)
            nc.vector.tensor_copy(id_gates[:], gates).then_inc(s["ids_done"], 1)

            def stage(n, c):
                e = dve.value_load(tile_e[0:1, bass.ds(n, 1)], min_val=0, max_val=E - 1)
                if not isinstance(n, int) or n >= 2:
                    dve.wait_ge(s["l1_ps"], n * 2 - 2)
                w = W1S[c % 2]
                nc.vector.tensor_copy(w[:, 0], w1_0[:, bass.ds(e, 1), :].rearrange("p a n -> p (a n)")).then_inc(s["w1_in"], 1)
                nc.vector.tensor_copy(w[0:C1, 1], w1_1[:, bass.ds(e, 1), :].rearrange("p a n -> p (a n)")).then_inc(s["w1_in"], 1)
                if not isinstance(n, int) or n >= 2:
                    dve.wait_ge(s["hid_ready"], n * HT + HT)
                nc.vector.tensor_copy(B1S[:, c % 2], b1_s[:, bass.ds(e, 1), :].rearrange("p a n -> p (a n)")).then_inc(s["w1_in"], 1)
                nc.vector.tensor_copy(B2S[c % 3], b2_all[:, bass.ds(e, 1), :].rearrange("p a n -> p (a n)")).then_inc(s["w1_in"], 1)

            def scale(n, c):
                dve.wait_ge(s["y_ps"], n + 3)
                dve.wait_ge(s["y_free"], n + 1)
                dve.wait_ge(s["w1_in"], n * 4 + 4)
                tt(YS[:, c % 2], PS[:, 6 + c % 2, 0:D], B2S[c % 3], ALU.add).then_inc(s["y_biased"], 1)
                dve.wait_ge(s["y_biased"], n + 1)
                ts_(YS[:, c % 2], YS[:, c % 2], gate_c[:, c % UN:c % UN + 1], None, ALU.mult).then_inc(s["y_scaled"], 1)

            dve.wait_ge(s["moe_in"], 16 * (len(moe) + len(late)))
            dve.wait_ge(s["ids_done"], 2)
            dve.wait_ge(s["b2_in"], 16)
            stage(0, 0)
            stage(1, 1)
            with dve.Fori(0, TURNS) as i:
                for c in range(UN):
                    stage(i * UN + (c + 2), c + 2)
                    scale(i * UN + c, c)
            for n in range(UN * TURNS, TILES):
                if n + 2 < TILES:
                    stage(n + 2, n + 2)
                scale(n, n)


def constants():
    c = {"c_ident": np.eye(128, dtype=np.float32)}
    quarter = np.zeros((128, 4, 128), np.float32)
    for q in range(4):
        quarter[32 * q, q, :] = 1
    c["c_quarter"] = quarter
    regroup = np.zeros((J, 32, 128), np.float32)
    for k in range(2):
        for d in range(HD):
            for j in range(J):
                regroup[j, HD * k + d, 64 * k + HD * j + d] = 1
    c["c_regroup"] = regroup.reshape(128, 128)
    ho = np.zeros((128, 32), np.float32)
    kones = np.zeros((128, G), np.float32)
    for j in range(J):
        ho[32 * j:32 * j + HD, j] = 0.5
        kones[32 * j + HD, :] = 1
    c["c_head_half"], c["c_kones"] = ho, kones
    p, i = np.meshgrid(np.arange(S), np.arange(D // 2))
    pe = np.zeros((S, D), dtype=np.float32)
    pe[:, ::2] = np.sin(p / 2500 ** (2 * i / D)).T
    pe[:, 1::2] = np.cos(p / 2500 ** (2 * i / D)).T
    c["c_pos"] = pe
    c["c_upper"] = np.triu(np.ones((128, 128), np.float32), 1)
    c["c_ones"] = np.ones((128, 128), np.float32)
    numbers = np.arange(T + 128).reshape(NT + 1, 128).T + 1
    c["c_token_no"] = numbers.astype(np.float32)
    c["c_count_up"] = np.tile(np.arange(128, dtype=np.float32), (128, 1))
    c["c_zeros"] = np.zeros((128, D), np.float32)
    c["c_expert_no"] = np.tile(np.arange(E, dtype=np.float32), (128, 1))
    return c


def kernel(**inputs):
    import concourse.bacc as bacc
    from concourse.bass_utils import run_bass_kernel_spmd

    nc = bacc.Bacc("TRN2", target_bir_lowering=False, num_devices=1)
    arrays, aps = {}, {}
    given = {n: np.ascontiguousarray(v) for n, v in inputs.items()}
    given["c_projT"] = np.ascontiguousarray(given["L0_attn_proj"].T)
    given.update(constants())
    for name, v in given.items():
        if name == "L0_attn_proj":
            continue
        arrays[f"in_{name}"] = v
        aps[name] = nc.dram_tensor(f"in_{name}", v.shape, mybir.dt.from_np(v.dtype), kind="ExternalInput").ap()
    out = nc.dram_tensor("out_0", (B, S, D), F32, kind="ExternalOutput").ap()
    build(nc, aps, out)
    r = run_bass_kernel_spmd(nc, [arrays], core_ids=[0])
    return r.results[0]["out_0"]
```
